# Optimizing a Trainium2 kernel written in Bass

```python
import numpy as np
import jax
import jax.numpy as jnp

def _softmax(x, axis=-1):
    return jax.nn.softmax(x, axis=axis)

def _gelu(x):
    return jax.nn.gelu(x, approximate=True)

def _silu(x):
    return jax.nn.silu(x)

def _sigmoid(x):
    return jax.nn.sigmoid(x)

def _layernorm(x, axis=-1, eps=1e-05):
    m = jnp.mean(x, axis=axis, keepdims=True)
    v = jnp.var(x, axis=axis, keepdims=True)
    return (x - m) / jnp.sqrt(v + eps)

def _scatter_add(tgt, idx, src, axis=0):
    return tgt.at[idx].add(src)

def _segment_sum(src, seg, n):
    return jax.ops.segment_sum(src, seg, n)
kernel_name = 'mk_gnn_preln_d4_gnn_r8_5c631a'

def setup_inputs(seed: int=0):
    np.random.seed(seed)
    _w = jnp.asarray

    def _rec_inputs():
        import jax
        import jax.numpy as jnp
        _gk = jax.random.key(seed)
        x = -0.000202 + 1 * jax.random.normal(jax.random.fold_in(_gk, 1), (12500, 64), jnp.float32)
        src = jax.random.randint(jax.random.fold_in(_gk, 2), (200000,), 0, 12500, jnp.int32)
        dst = jax.random.randint(jax.random.fold_in(_gk, 3), (200000,), 0, 12500, jnp.int32)
        _o = jnp.argsort(dst, stable=True)
        src = src[_o]
        dst = dst[_o]
        edge_attr_64 = -8.16379e-05 + 0.999858 * jax.random.normal(jax.random.fold_in(_gk, 12), (200000, 64), jnp.float32)
        edge_weight = jax.random.uniform(jax.random.fold_in(_gk, 14), (200000,), jnp.float32, 0.0, 0.999999)
        edge_weight_n2 = jax.random.uniform(jax.random.fold_in(_gk, 15), (200000,), jnp.float32, 0.0, 0.999999)
        return (x, src, dst, edge_attr_64, edge_weight, edge_weight_n2)
    x, src, dst, edge_attr_64, edge_weight, edge_weight_n2 = _rec_inputs()

    def _L0_gnn_setup():
        import jax, jax.numpy as jnp
        import numpy as np
        N_NODES = 12500
        N_EDGES = 200000
        D = 64

        def _mlp(x, W1, b1, W2, b2):
            return jnp.dot(jax.nn.relu(jnp.dot(x, W1) + b1), W2) + b2
        key = jax.random.key(seed)
        ks = jax.random.split(key, 12)
        s = lambda fan_in: 1.0 / np.sqrt(fan_in)
        return {'node_x': jax.random.normal(ks[0], (N_NODES, D), jnp.float32), 'edge_x': jax.random.normal(ks[1], (N_EDGES, D), jnp.float32), 'sources': jax.random.randint(ks[2], (N_EDGES,), 0, N_NODES), 'targets': jax.random.randint(ks[3], (N_EDGES,), 0, N_NODES), 'msg_W1': jax.random.normal(ks[4], (3 * D, D), jnp.float32) * s(3 * D), 'msg_b1': jnp.zeros((D,), jnp.float32), 'msg_W2': jax.random.normal(ks[5], (D, D), jnp.float32) * s(D), 'msg_b2': jnp.zeros((D,), jnp.float32), 'upd_W1': jax.random.normal(ks[6], (2 * D, D), jnp.float32) * s(2 * D), 'upd_b1': jnp.zeros((D,), jnp.float32), 'upd_W2': jax.random.normal(ks[7], (D, D), jnp.float32) * s(D), 'upd_b2': jnp.zeros((D,), jnp.float32)}
    _L0_gnn_all = _L0_gnn_setup()
    _L0_gnn_in = {k: v for k, v in _L0_gnn_all.items() if k in ('msg_W1', 'msg_b1', 'msg_W2', 'msg_b2', 'upd_W1', 'upd_b1', 'upd_W2', 'upd_b2')}
    del _L0_gnn_all

    def _L1_gnn_setup():
        import jax, jax.numpy as jnp
        import numpy as np
        N, E, D_IN, D_OUT = (8192, 131072, 64, 64)
        EPS = 1e-08
        key = jax.random.key(seed)
        ks = jax.random.split(key, 8)
        h = jax.random.normal(ks[0], (N, D_IN), dtype=jnp.float32)
        edge_index = jax.random.randint(ks[1], (2, E), 0, N, dtype=jnp.int64 if jax.config.jax_enable_x64 else jnp.int32)
        adj_v = jax.random.uniform(ks[2], (E,), dtype=jnp.float32)
        deg_v = jax.random.uniform(ks[3], (E,), dtype=jnp.float32)
        W = jax.random.normal(ks[4], (D_IN, D_OUT), dtype=jnp.float32) / np.sqrt(D_IN)
        b = jax.random.normal(ks[5], (D_OUT,), dtype=jnp.float32) * 0.01
        deg_coeff = jnp.array([0.5, 0.0], dtype=jnp.float32)
        coeff_param = jnp.zeros((3,), dtype=jnp.float32)
        scale_param = 2.0 * jnp.ones((1,), dtype=jnp.float32)
        return {'h': h, 'edge_index': edge_index, 'adj_v': adj_v, 'deg_v': deg_v, 'W': W, 'b': b, 'deg_coeff': deg_coeff, 'coeff_param': coeff_param, 'scale_param': scale_param}
    _L1_gnn_all = _L1_gnn_setup()
    _L1_gnn_in = {k: v for k, v in _L1_gnn_all.items() if k in ('W', 'b', 'deg_coeff', 'coeff_param', 'scale_param')}
    del _L1_gnn_all

    def _L2_gnn_setup():
        import jax, jax.numpy as jnp
        import numpy as np
        N_NODES = 12500
        N_EDGES = 200000
        IN_DIM = 64
        HID_DIM = 64

        def _sage_conv(h, src, dst, W_l, b_l, W_r, num_nodes):
            msgs = h[src]
            agg = jax.ops.segment_sum(msgs, dst, num_segments=num_nodes)
            deg = jax.ops.segment_sum(jnp.ones((src.shape[0],), h.dtype), dst, num_segments=num_nodes)
            mean = agg / jnp.maximum(deg, 1.0)[:, None]
            return mean @ W_l + b_l + h @ W_r
        key = jax.random.key(seed)
        ks = jax.random.split(key, 8)
        s = 1.0 / np.sqrt(IN_DIM)
        return {'x': jax.random.normal(ks[0], (N_NODES, IN_DIM), dtype=jnp.float32), 'edge_index': jax.random.randint(ks[1], (2, N_EDGES), 0, N_NODES, dtype=jnp.int64), 'W1_l': jax.random.normal(ks[2], (IN_DIM, HID_DIM), dtype=jnp.float32) * s, 'b1_l': jnp.zeros((HID_DIM,), dtype=jnp.float32), 'W1_r': jax.random.normal(ks[3], (IN_DIM, HID_DIM), dtype=jnp.float32) * s, 'W2_l': jax.random.normal(ks[4], (HID_DIM, HID_DIM), dtype=jnp.float32) * s, 'b2_l': jnp.zeros((HID_DIM,), dtype=jnp.float32), 'W2_r': jax.random.normal(ks[5], (HID_DIM, HID_DIM), dtype=jnp.float32) * s}
    _L2_gnn_all = _L2_gnn_setup()
    _L2_gnn_in = {k: v for k, v in _L2_gnn_all.items() if k in ('W1_l', 'b1_l', 'W1_r', 'W2_l', 'b2_l', 'W2_r')}
    del _L2_gnn_all

    def _L3_gnn_setup():
        import jax, jax.numpy as jnp
        import numpy as np
        N_NODES = 6250
        N_EDGES = 150000
        IN_FEATS = 64
        OUT_FEATS = 64
        NEG_SLOPE = 0.01
        key = jax.random.key(seed)
        k1, k2, k3, k4, k5, k6 = jax.random.split(key, 6)
        feature = jax.random.normal(k1, (N_NODES, IN_FEATS), dtype=jnp.float32)
        attn_w = jax.random.normal(k2, (2 * IN_FEATS, 1), dtype=jnp.float32) * 0.1
        lin_w = jax.random.normal(k3, (OUT_FEATS, 2 * IN_FEATS), dtype=jnp.float32) * 0.1
        lin_b = jax.random.normal(k4, (OUT_FEATS,), dtype=jnp.float32) * 0.1
        src = jax.random.randint(k5, (N_EDGES,), 0, N_NODES, dtype=jnp.int32)
        dst = jax.random.randint(k6, (N_EDGES,), 0, N_NODES, dtype=jnp.int32)
        return {'feature': feature, 'attn_w': attn_w, 'lin_w': lin_w, 'lin_b': lin_b, 'src': src, 'dst': dst}
    _L3_gnn_all = _L3_gnn_setup()
    _L3_gnn_in = {k: v for k, v in _L3_gnn_all.items() if k in ('attn_w', 'lin_w', 'lin_b')}
    del _L3_gnn_all
    return {'x': x, 'src': src, 'dst': dst, 'edge_attr_64': edge_attr_64, 'edge_weight': edge_weight, 'edge_weight_n2': edge_weight_n2, 'L0_gnn_msg_W1': _L0_gnn_in['msg_W1'], 'L0_gnn_msg_b1': _L0_gnn_in['msg_b1'], 'L0_gnn_msg_W2': _L0_gnn_in['msg_W2'], 'L0_gnn_msg_b2': _L0_gnn_in['msg_b2'], 'L0_gnn_upd_W1': _L0_gnn_in['upd_W1'], 'L0_gnn_upd_b1': _L0_gnn_in['upd_b1'], 'L0_gnn_upd_W2': _L0_gnn_in['upd_W2'], 'L0_gnn_upd_b2': _L0_gnn_in['upd_b2'], 'L1_gnn_W': _L1_gnn_in['W'], 'L1_gnn_b': _L1_gnn_in['b'], 'L1_gnn_deg_coeff': _L1_gnn_in['deg_coeff'], 'L1_gnn_coeff_param': _L1_gnn_in['coeff_param'], 'L1_gnn_scale_param': _L1_gnn_in['scale_param'], 'L2_gnn_W1_l': _L2_gnn_in['W1_l'], 'L2_gnn_b1_l': _L2_gnn_in['b1_l'], 'L2_gnn_W1_r': _L2_gnn_in['W1_r'], 'L2_gnn_W2_l': _L2_gnn_in['W2_l'], 'L2_gnn_b2_l': _L2_gnn_in['b2_l'], 'L2_gnn_W2_r': _L2_gnn_in['W2_r'], 'L3_gnn_attn_w': _L3_gnn_in['attn_w'], 'L3_gnn_lin_w': _L3_gnn_in['lin_w'], 'L3_gnn_lin_b': _L3_gnn_in['lin_b']}

def reference(x, src, dst, edge_attr_64, edge_weight, edge_weight_n2, L0_gnn_msg_W1, L0_gnn_msg_b1, L0_gnn_msg_W2, L0_gnn_msg_b2, L0_gnn_upd_W1, L0_gnn_upd_b1, L0_gnn_upd_W2, L0_gnn_upd_b2, L1_gnn_W, L1_gnn_b, L1_gnn_deg_coeff, L1_gnn_coeff_param, L1_gnn_scale_param, L2_gnn_W1_l, L2_gnn_b1_l, L2_gnn_W1_r, L2_gnn_W2_l, L2_gnn_b2_l, L2_gnn_W2_r, L3_gnn_attn_w, L3_gnn_lin_w, L3_gnn_lin_b):
    import jax
    import jax.numpy as jnp

    def _L0_gnn_ref(node_x, edge_x, sources, targets, msg_W1, msg_b1, msg_W2, msg_b2, upd_W1, upd_b1, upd_W2, upd_b2):
        import jax, jax.numpy as jnp
        import numpy as np
        N_NODES = 12500
        N_EDGES = 200000
        D = 64

        def _mlp(x, W1, b1, W2, b2):
            return jnp.dot(jax.nn.relu(jnp.dot(x, W1) + b1), W2) + b2
        num_nodes = node_x.shape[0]
        source_x = jnp.take(node_x, sources, axis=0)
        target_x = jnp.take(node_x, targets, axis=0)
        message_in = jnp.concatenate((source_x, target_x, edge_x), axis=1)
        message_x = _mlp(message_in, msg_W1, msg_b1, msg_W2, msg_b2)
        agg = jax.ops.segment_sum(message_x, targets, num_segments=num_nodes)
        update_in = jnp.concatenate((agg, node_x), axis=1)
        return _mlp(update_in, upd_W1, upd_b1, upd_W2, upd_b2)

    def _L1_gnn_ref(h, edge_index, adj_v, deg_v, W, b, deg_coeff, coeff_param, scale_param):
        import jax, jax.numpy as jnp
        import numpy as np
        N, E, D_IN, D_OUT = (8192, 131072, 64, 64)
        EPS = 1e-08
        n_nodes = h.shape[0]
        Wh = h @ W + b
        row, col = (edge_index[0], edge_index[1])
        sc = jax.nn.softplus(deg_coeff[0] * deg_v + deg_coeff[1])
        Wr = Wh[row]
        Wc = Wh[col]
        dot = jnp.sum(Wr * Wc, axis=-1)
        nr = jnp.sqrt(jnp.sum(Wr * Wr, axis=-1))
        nc = jnp.sqrt(jnp.sum(Wc * Wc, axis=-1))
        sim = dot / jnp.maximum(nr * nc, EPS)
        sim_pos = jax.nn.relu(sim)
        sim_neg = -jax.nn.relu(-sim)
        no_diag = (row != col).astype(Wh.dtype)
        base = adj_v * sc * no_diag
        prop_pos = jax.ops.segment_sum((base * sim_pos)[:, None] * Wc, row, num_segments=n_nodes)
        prop_neg = jax.ops.segment_sum((base * sim_neg)[:, None] * Wc, row, num_segments=n_nodes)
        coeff = jax.nn.softmax(coeff_param)
        scale = jax.nn.softplus(scale_param)
        return scale * (coeff[0] * prop_pos + coeff[1] * prop_neg + coeff[2] * Wh)

    def _L2_gnn_ref(x, edge_index, W1_l, b1_l, W1_r, W2_l, b2_l, W2_r):
        import jax, jax.numpy as jnp
        import numpy as np
        N_NODES = 12500
        N_EDGES = 200000
        IN_DIM = 64
        HID_DIM = 64

        def _sage_conv(h, src, dst, W_l, b_l, W_r, num_nodes):
            msgs = h[src]
            agg = jax.ops.segment_sum(msgs, dst, num_segments=num_nodes)
            deg = jax.ops.segment_sum(jnp.ones((src.shape[0],), h.dtype), dst, num_segments=num_nodes)
            mean = agg / jnp.maximum(deg, 1.0)[:, None]
            return mean @ W_l + b_l + h @ W_r
        src, dst = (edge_index[0], edge_index[1])
        n = x.shape[0]
        h = jax.nn.relu(_sage_conv(x, src, dst, W1_l, b1_l, W1_r, n))
        out = jax.nn.relu(_sage_conv(h, src, dst, W2_l, b2_l, W2_r, n))
        return out

    def _L3_gnn_ref(feature, attn_w, lin_w, lin_b, src, dst):
        import jax, jax.numpy as jnp
        import numpy as np
        N_NODES = 6250
        N_EDGES = 150000
        IN_FEATS = 64
        OUT_FEATS = 64
        NEG_SLOPE = 0.01
        N = feature.shape[0]
        a_src, a_dst = (attn_w[:IN_FEATS, 0], attn_w[IN_FEATS:, 0])
        e = jax.nn.leaky_relu(feature[src] @ a_src + feature[dst] @ a_dst, negative_slope=NEG_SLOPE)
        emax = jax.ops.segment_max(e, dst, num_segments=N)
        emax = jnp.where(jnp.isfinite(emax), emax, 0.0)
        ex = jnp.exp(e - emax[dst])
        denom = jax.ops.segment_sum(ex, dst, num_segments=N)
        num = jax.ops.segment_sum(ex[:, None] * feature[src], dst, num_segments=N)
        hm = jnp.where(denom[:, None] > 0, num / denom[:, None], 0.0)
        h = jnp.concatenate([feature, hm], axis=1) @ lin_w.T + lin_b
        return jax.nn.relu(h)
    edge_index = jnp.stack([src, dst])
    h = jnp.maximum(_layernorm(x, axis=-1), 0.0)
    x = x + _L0_gnn_ref(h, edge_attr_64, src, dst, L0_gnn_msg_W1, L0_gnn_msg_b1, L0_gnn_msg_W2, L0_gnn_msg_b2, L0_gnn_upd_W1, L0_gnn_upd_b1, L0_gnn_upd_W2, L0_gnn_upd_b2)
    h = jnp.maximum(_layernorm(x, axis=-1), 0.0)
    x = x + _L1_gnn_ref(h, edge_index, edge_weight, edge_weight_n2, L1_gnn_W, L1_gnn_b, L1_gnn_deg_coeff, L1_gnn_coeff_param, L1_gnn_scale_param)
    h = jnp.maximum(_layernorm(x, axis=-1), 0.0)
    x = x + _L2_gnn_ref(h, edge_index, L2_gnn_W1_l, L2_gnn_b1_l, L2_gnn_W1_r, L2_gnn_W2_l, L2_gnn_b2_l, L2_gnn_W2_r)
    h = jnp.maximum(_layernorm(x, axis=-1), 0.0)
    x = x + _L3_gnn_ref(h, L3_gnn_attn_w, L3_gnn_lin_w, L3_gnn_lin_b, src, dst)
    return x

_drawn_inputs = setup_inputs


def setup_inputs(seed=0):
    import zlib

    import numpy as np

    out = dict(_drawn_inputs(seed))
    spreads = {'L0_gnn_msg_b1': (0.0, 0.1),
     'L0_gnn_msg_b2': (0.0, 0.1),
     'L0_gnn_upd_b1': (0.0, 0.336),
     'L0_gnn_upd_b2': (0.0, 0.326),
     'L1_gnn_coeff_param': (0.0, 0.1),
     'L2_gnn_b1_l': (0.0, 0.753),
     'L2_gnn_b2_l': (0.0, 0.539)}
    factors = {'edge_weight_n2': 3.747, 'L1_gnn_b': 5.423, 'L3_gnn_attn_w': 8.0, 'L3_gnn_lin_b': 3.223}
    for name, (base, spread) in spreads.items():
        noise = np.random.default_rng([zlib.crc32(name.encode()), seed]).standard_normal(out[name].shape)
        drawn = base * np.exp(spread * noise) if base else spread * noise
        out[name] = jnp.asarray(drawn.astype(out[name].dtype))
    for name, factor in factors.items():
        out[name] = (out[name] * factor).astype(out[name].dtype)
    return out
```

```python
from contextlib import ExitStack

import concourse.bass as bass
from concourse import mybir

P = 128
D = 64
TPC = 8
CE = P * TPC
U = 4
GT = 20
NPROP = 4
NEG = -1.0e30
BIG = 1.0e30

F32 = mybir.dt.float32
I32 = mybir.dt.int32
ALU = mybir.AluOpType
ACT = mybir.ActivationFunctionType
AX = mybir.AxisListType.X


class Progress:

    def __init__(self, sem):
        self.sem, self.before, self.steps = sem, 0, []

    def begin(self, steps):
        self.steps = steps.split()

    def at(self, name, g):
        return self.before + g * len(self.steps) + (self.steps.index(name) + 1)

    def end(self, groups):
        self.before += groups * len(self.steps)


def gnn_kernel(nc, a, out):
    N, E = a["x"].shape[0], a["src"].shape[0]
    C = -(-E // CE)
    NG = -(-(N + P) // (P * GT))
    NT = NG * GT
    NPAD = NT * P
    FULL, TAIL = N // P, N % P
    HALF = C // 2
    TWICE = C * CE - E
    assert C % U == 0 and HALF <= P and TWICE % TPC == 0 and TAIL and E >= CE and (C - 1) * CE < E
    DUP = TWICE // TPC

    with ExitStack() as ctx:
        def sb(name, shape, dt=F32):
            return ctx.enter_context(nc.sbuf_tensor(name, shape, dt))

        def sem(name):
            return ctx.enter_context(nc.semaphore(name))

        def dram(name, shape):
            return nc.dram_tensor(name, shape, F32, kind="Internal").ap()

        msg_src = dram("msg_src", (NPAD, D))
        msg_dst = dram("msg_dst", (NPAD, D))
        att = dram("att", (NPAD, D + 1))
        sage1 = dram("sage1", (NPAD, D))
        sage2 = dram("sage2", (NPAD, D))
        soft = dram("soft", (NPAD, D + 2))
        soft_dst = dram("soft_dst", (NPAD, 1))
        props = [dram(f"prop{k}", (NPAD, D)) for k in range(NPROP)]

        X = sb("X", [P, NT, D])
        acc = sb("acc", [P, NPAD])
        keep = sb("keep", [P, NPAD])
        dstf = sb("dstf", [P, C, TPC])
        srcf = sb("srcf", [P, C, TPC])
        srci = sb("srci", [P, C, TPC], I32)
        ewt = sb("ewt", [P, C, TPC])
        base_bc = sb("base_bc", [P, C])
        base0 = sb("base0", [P, C])
        base_i = sb("base_i", [1, C], I32)
        rounds_i = sb("rounds_i", [1, 1], I32)
        ident = sb("ident", [P, P])
        iota_f = sb("iota_f", [P, P])
        lower = sb("lower", [P, P])
        trash = sb("trash", [P, 1])
        small = sb("small", [P, 32])

        w_in = sb("w_in", [D + 1, 3 * D])
        w_edge = sb("w_edge", [D, D])
        w_upd1 = sb("w_upd1", [D, D])
        w_msg2 = sb("w_msg2", [D + 1, D])
        w_msg2T = sb("w_msg2T", [D, D + 1])
        w_fold = sb("w_fold", [D + 1, D])
        w_upd2 = sb("w_upd2", [D + 1, D])
        w_att = sb("w_att", [D + 1, D])
        w_r1 = sb("w_r1", [D + 1, D])
        w_l1 = sb("w_l1", [D, D])
        w_r2 = sb("w_r2", [D + 1, D])
        w_l2 = sb("w_l2", [D, D])
        w_lin = sb("w_lin", [D, 2 * D])
        w_own = sb("w_own", [D + 1, D + 2])
        w_hm = sb("w_hm", [D + 1, D + 1])
        e_deg = sb("e_deg", [D + 1, 1])
        coef = sb("coef", [P, 16])

        rdeg = sb("rdeg", [P, NT])

        ps = ctx.enter_context(nc.psum_tensor("ps", [P, 8, 512], F32))

        s_held = sem("held")

        def hold(eng):
            eng.sem_inc(s_held, 1)

        def bc(v, shape):
            return v.broadcast_to(shape)

        ld = sem("loads")
        loads = []

        def col(v):
            return v.rearrange("(a b) -> a b", b=1)

        def row(v):
            return v.rearrange("(a b) -> a b", a=1)

        def by_edge(v, lo, n):
            return v[lo:lo + n * CE].rearrange("(c p j) -> p c j", p=P, j=TPC)

        s_z = sem("zeroed")
        with nc.Block() as block:
            W1, U1 = a["L0_gnn_msg_W1"], a["L0_gnn_upd_W1"]
            loads += [
                (X[:, 0:FULL, :], a["x"][0:FULL * P].rearrange("(t p) d -> p t d", p=P)),
                (X[0:TAIL, FULL, :], a["x"][FULL * P:N]),
                (w_in[0:D, 0:D], W1[0:D]), (w_in[0:D, D:2 * D], W1[D:2 * D]), (w_edge[:], W1[2 * D:3 * D]),
                (w_in[0:D, 2 * D:3 * D], U1[D:2 * D]), (w_upd1[:], U1[0:D]),
                (w_in[D:D + 1, D:2 * D], row(a["L0_gnn_msg_b1"])), (w_in[D:D + 1, 2 * D:3 * D], row(a["L0_gnn_upd_b1"])),
                (w_msg2[0:D], a["L0_gnn_msg_W2"]), (w_msg2[D:D + 1], row(a["L0_gnn_msg_b2"])),
                (w_upd2[0:D], a["L0_gnn_upd_W2"]), (w_upd2[D:D + 1], row(a["L0_gnn_upd_b2"])),
                (w_att[0:D], a["L1_gnn_W"]), (w_att[D:D + 1], row(a["L1_gnn_b"])),
                (w_r1[0:D], a["L2_gnn_W1_r"]), (w_r1[D:D + 1], row(a["L2_gnn_b1_l"])), (w_l1[:], a["L2_gnn_W1_l"]),
                (w_r2[0:D], a["L2_gnn_W2_r"]), (w_r2[D:D + 1], row(a["L2_gnn_b2_l"])), (w_l2[:], a["L2_gnn_W2_l"]),
                (w_lin[:], a["L3_gnn_lin_w"]), (w_own[D:D + 1, 0:D], row(a["L3_gnn_lin_b"])),
                (w_own[0:D, D:D + 1], a["L3_gnn_attn_w"][0:D]), (w_own[0:D, D + 1:D + 2], a["L3_gnn_attn_w"][D:2 * D]),
                (coef[:, 0:2], bc(row(a["L1_gnn_deg_coeff"]), [P, 2])),
                (coef[:, 2:5], bc(row(a["L1_gnn_coeff_param"]), [P, 3])),
                (coef[:, 5:6], bc(row(a["L1_gnn_scale_param"]), [P, 1])),
            ]
            ints = acc[:, 0:2 * C * TPC].bitcast(I32).rearrange("p (k c j) -> p k c j", k=2, j=TPC)
            dsti = ints[:, 0]
            ew2 = acc[:, 2 * C * TPC:3 * C * TPC].rearrange("p (c j) -> p c j", j=TPC)
            for t, v in ((srci, a["src"]), (dsti, a["dst"]), (ewt, a["edge_weight"]), (ew2, a["edge_weight_n2"])):
                loads.append((t[:, 0:C - 1, :], by_edge(v, 0, C - 1)))
                loads.append((t[:, C - 1:C, :], by_edge(v, E - CE, 1)))

            @block.sync
            def _(sp):
                sp.wait_ge(s_z, 3)
                with nc.allow_non_contiguous_dma("columns of small weights"):
                    for dst, src in loads:
                        sp.dma_start(dst, src).then_inc(ld, 16)
                sp.wait_ge(ld, 16 * len(loads))

            s_i = sem("iotas")

            @block.gpsimd
            def _(pool):
                pool.memset(ident[:], 0.0).then_inc(s_i, 1)
                pool.memset(lower[:], 1.0).then_inc(s_i, 1)
                pool.iota(iota_f[:], [[1, P]], base=0, channel_multiplier=0, allow_small_or_imprecise_dtypes=True).then_inc(s_i, 1)
                pool.iota(trash[:], [[1, 1]], base=N, channel_multiplier=1, allow_small_or_imprecise_dtypes=True).then_inc(s_i, 1)
                pool.wait_ge(s_i, 4)
                pool.affine_select(out=ident[:], in_=ident[:], compare_op=ALU.not_equal, fill=1.0, base=0,
                                   pattern=[[-1, P]], channel_multiplier=1).then_inc(s_i, 1)
                pool.affine_select(out=lower[:], in_=lower[:], compare_op=ALU.is_gt, fill=0.0, base=0,
                                   pattern=[[-1, P]], channel_multiplier=1).then_inc(s_i, 1)
                pool.wait_ge(s_i, 6)

            @block.vector
            def _(dve):
                dve.memset(X[:, FULL:NT, :], 0.0).then_inc(s_z, 1)
                dve.memset(w_in[D:D + 1, 0:D], 0.0).then_inc(s_z, 1)
                dve.memset(w_own[D:D + 1, D:D + 2], 0.0).then_inc(s_z, 1)
                dve.memset(w_hm[:], 0.0).then_inc(s_z, 1)
                dve.memset(e_deg[:], 0.0).then_inc(s_z, 1)
                dve.wait_ge(s_z, 5)
                dve.memset(w_hm[D:D + 1, D:D + 1], 1.0).then_inc(s_z, 1)
                dve.memset(e_deg[D:D + 1, :], 1.0).then_inc(s_z, 1)
                dve.memset(small[:, 0:1], 1.0e-5).then_inc(s_z, 1)
                dve.memset(small[:, 1:2], 1.0).then_inc(s_z, 1)
                dve.memset(small[:, 8:9], -BIG).then_inc(s_z, 1)
                dve.wait_ge(s_z, 10)

        lo_hi = keep[:, 0:2 * C].rearrange("p (k c) -> p k c", k=2)
        loT = keep[:, 2 * C:2 * C + 2 * P].rearrange("p (k q) -> p k q", k=2)
        hi_bc = keep[:, 2 * C + 2 * P:3 * C + 2 * P]
        lim = keep[:, 1024:1024 + NT]
        sp_t = keep[:, 2048:2048 + C * TPC].rearrange("p (c j) -> p c j", j=TPC)
        c_v, c_a, c_p = sem("setup_dve"), sem("setup_act"), sem("setup_pe")
        with nc.Block() as block:
            @block.vector
            def _(dve):
                dve.tensor_copy(dstf[:], dsti).then_inc(c_v, 1)
                dve.tensor_copy(srcf[:], srci[:]).then_inc(c_v, 1)
                dve.wait_ge(c_v, 2)
                dve.tensor_reduce(lo_hi[:, 0, :], dstf[:], AX, ALU.min).then_inc(c_v, 1)
                dve.tensor_reduce(lo_hi[:, 1, :], dstf[:], AX, ALU.max).then_inc(c_v, 1)
                dve.tensor_scalar(ew2, ew2, coef[:, 0:1], coef[:, 1:2], ALU.mult, ALU.add).then_inc(c_v, 1)
                dve.wait_ge(c_v, 5)
                dve.scalar_tensor_tensor(sp_t, ew2, -1.0, ew2, ALU.mult, ALU.min).then_inc(c_v, 1)
                dve.tensor_copy(coef[:, 6:7], coef[:, 5:6]).then_inc(c_v, 1)
                dve.wait_ge(c_v, 7)
                dve.scalar_tensor_tensor(coef[:, 7:8], coef[:, 6:7], -1.0, coef[:, 6:7], ALU.mult, ALU.min).then_inc(c_v, 1)
                dve.tensor_reduce(coef[:, 8:9], coef[:, 2:5], AX, ALU.max).then_inc(c_v, 1)
                dve.wait_ge(c_v, 9)
                dve.tensor_scalar(coef[:, 2:5], coef[:, 2:5], coef[:, 8:9], None, ALU.subtract).then_inc(c_v, 1)
                dve.wait_ge(c_a, 4)
                dve.scalar_tensor_tensor(ew2, ew2, 0.0, sp_t, ALU.max, ALU.add).then_inc(c_v, 1)
                dve.scalar_tensor_tensor(coef[:, 6:7], coef[:, 6:7], 0.0, coef[:, 7:8], ALU.max, ALU.add).then_inc(c_v, 1)
                dve.tensor_reduce(coef[:, 8:9], coef[:, 10:13], AX, ALU.add).then_inc(c_v, 1)
                dve.wait_ge(c_v, 13)
                dve.reciprocal(coef[:, 9:10], coef[:, 8:9]).then_inc(c_v, 1)
                dve.tensor_tensor(ewt[:], ewt[:], ew2, ALU.mult).then_inc(c_v, 1)
                dve.tensor_tensor(sp_t, srcf[:], dstf[:], ALU.not_equal).then_inc(c_v, 1)
                dve.wait_ge(c_v, 16)
                dve.tensor_tensor(ewt[:], ewt[:], sp_t, ALU.mult).then_inc(c_v, 1)
                dve.tensor_scalar(coef[:, 10:13], coef[:, 10:13], coef[:, 9:10], coef[:, 6:7], ALU.mult, ALU.mult).then_inc(c_v, 1)
                dve.wait_ge(c_v, 18)
                dve.memset(ewt[0:DUP, C - 1, :], 0.0).then_inc(c_v, 1)
                dve.memset(dstf[0:DUP, C - 1, :], -4.0 * P).then_inc(c_v, 1)
                dve.wait_ge(c_p, 1)
                for k in range(4):
                    dve.tensor_reduce(small[0:HALF, 2 + k:3 + k], ps[0:HALF, k, 0:P], AX,
                                      (ALU.min, ALU.max)[k // 2]).then_inc(c_v, 1)
                dve.tensor_copy(w_msg2T[:], ps[0:D, 4, 0:D + 1]).then_inc(c_v, 1)
                dve.tensor_copy(w_own[0:D, 0:D], ps[0:D, 5, 0:D]).then_inc(c_v, 1)
                dve.tensor_copy(w_hm[0:D, 0:D], ps[0:D, 6, 0:D]).then_inc(c_v, 1)
                dve.wait_ge(c_p, 2)
                for k in range(4):
                    dst = (base_bc[:], hi_bc)[k // 2]
                    dve.tensor_copy(dst[:, (k % 2) * HALF:(k % 2 + 1) * HALF], ps[:, k, 0:HALF]).then_inc(c_v, 1)
                dve.tensor_copy(w_fold[:], ps[0:D + 1, 7, 0:D]).then_inc(c_v, 1)
                dve.wait_ge(c_v, 32)
                dve.tensor_tensor(hi_bc, hi_bc, base_bc[:], ALU.subtract).then_inc(c_v, 1)
                dve.tensor_copy(base0[:], base_bc[:])
                dve.tensor_copy(base_i[:], base_bc[0:1, :]).then_inc(c_v, 1)
                dve.wait_ge(c_v, 34)
                dve.tensor_reduce(small[:, 6:7], hi_bc, AX, ALU.max).then_inc(c_v, 1)
                dve.tensor_scalar(lim, iota_f[:, 0:NT], float(P), None, ALU.mult).then_inc(c_v, 1)
                dve.wait_ge(c_v, 36)
                dve.tensor_scalar(lim, lim, small[:, 6:7], None, ALU.is_le).then_inc(c_v, 1)
                dve.wait_ge(c_v, 37)
                dve.tensor_reduce(small[:, 7:8], lim, AX, ALU.add).then_inc(c_v, 1)
                dve.wait_ge(c_v, 38)
                dve.tensor_copy(rounds_i[:], small[0:1, 7:8]).then_inc(c_v, 1)
                dve.wait_ge(c_v, 39)

            @block.scalar
            def _(act):
                act.wait_ge(c_v, 10)
                act.activation(coef[:, 10:13], coef[:, 2:5], ACT.Exp).then_inc(c_a, 1)
                act.activation(sp_t, sp_t, ACT.Exp).then_inc(c_a, 1)
                act.activation(coef[:, 7:8], coef[:, 7:8], ACT.Exp).then_inc(c_a, 1)
                act.wait_ge(c_a, 3)
                act.activation(sp_t, sp_t, ACT.Ln, bias=small[:, 1:2])
                act.activation(coef[:, 7:8], coef[:, 7:8], ACT.Ln, bias=small[:, 1:2]).then_inc(c_a, 1)

            @block.tensor
            def _(pe):
                pe.wait_ge(c_v, 4)
                for k in range(4):
                    pe.transpose(ps[0:HALF, k, 0:P], lo_hi[:, k // 2, (k % 2) * HALF:(k % 2 + 1) * HALF], ident[:])
                pe.transpose(ps[0:D, 4, 0:D + 1], w_msg2[:], ident[0:D + 1, 0:D + 1])
                pe.transpose(ps[0:D, 5, 0:D], w_lin[:, 0:D], ident[0:D, 0:D])
                pe.transpose(ps[0:D, 6, 0:D], w_lin[:, D:2 * D], ident[0:D, 0:D]).then_inc(c_p, 1)
                pe.wait_ge(c_v, 27)
                for k in range(4):
                    pe.matmul(ps[:, k, 0:HALF], bc(small[0:HALF, 2 + k:3 + k], [HALF, P]), ident[0:HALF, 0:HALF],
                              start=True, stop=True)
                pe.matmul(ps[0:D + 1, 7, 0:D], w_msg2T[:], w_upd1[:], start=True, stop=True).then_inc(c_p, 1)

        V, A, T = Progress(sem("node_dve")), Progress(sem("node_act")), Progress(sem("node_pe"))
        s_ones = sem("ones_row")
        n_ones = [0]
        in_sem = [sem(f"prop_in{k}") for k in range(NPROP)]
        out_sem = [sem(f"rows_out{k}") for k in range(2)]
        outs = [0, 0]

        keepN = keep[:, 0:NT * D].rearrange("p (t d) -> p t d", d=D)
        NB = GT * P // 512
        psT = ps[0:D, 0:NB, :].rearrange("p b q -> p (b q)")
        SPAN = 66
        PB = 7
        parts = [(NB + b, PB * b, min(PB, GT - PB * b)) for b in range(-(-GT // PB))]

        def tiles_of(b, n, lo, hi):
            return ps[:, b, 0:n * SPAN].rearrange("p (t m) -> p t m", m=SPAN)[:, :, lo:hi]

        def each(v, n=GT):
            return v.rearrange("p (t o) -> p t o", o=1).broadcast_to([P, n, D])

        def one(v):
            return v.rearrange("p (t o) -> p t o", o=1)

        def node_rows(table, g):
            return table[bass.ds(g * (GT * P), GT * P), :].rearrange("(t p) d -> p t d", p=P)

        def products(pe, lhsT, k, w):
            m = w.shape[1]
            for b, t0, n in parts:
                for t in range(n):
                    lo = (t0 + t) * P
                    ins = pe.matmul(ps[:, b, t * SPAN:t * SPAN + m], lhsT[0:k, lo:lo + P], w, start=True, stop=True)
            return ins

        def phase(name, take, dve_steps, act_steps, pe_steps, rows):
            V.begin(dve_steps), A.begin(act_steps), T.begin(pe_steps)
            with ExitStack() as scratch:
                def tmp(n, shape):
                    return scratch.enter_context(nc.sbuf_tensor(f"{name}_{n}", shape, F32))

                xc, hN = tmp("xc", [P, GT, D]), tmp("hN", [P, GT, D + 2])
                hT, accS = tmp("hT", [D + 1, GT * P]), tmp("accS", [D + 1, GT * P])
                st = tmp("st", [P, 6, GT])
                late = [tmp("late0", [P, GT, D]), tmp("late1", [P, GT, D])] if take == "prop" else []
                src_of = {"hN": hN, "xc": xc}
                block = scratch.enter_context(nc.Block())
                n_ones[0] += 1

                def done(ins, who, step):
                    assert step in who.steps
                    ins.then_inc(who.sem, 1)

                def after(eng, who, step, g):
                    eng.wait_ge(who.sem, who.at(step, g))

                @block.sync
                def _(sp):
                    with sp.Fori(0, NG) as g:
                        if take == "prop":
                            after(sp, V, "own", g - 1)
                            hold(sp)
                            for k, t in enumerate([xc[:], hN[:, :, 0:D], late[0][:], late[1][:]]):
                                sp.dma_start(t, node_rows(props[k], g)).then_inc(in_sem[k], 16)
                        for k, (table, buf, cols, who, step) in enumerate(rows):
                            after(sp, who, step, g)
                            hold(sp)
                            with nc.allow_non_contiguous_dma("a column of scores"):
                                sp.dma_start(node_rows(table, g), src_of[buf][:, :, 0:cols]).then_inc(out_sem[k], 16)
                        for k in range(len(rows)):
                            sp.wait_ge(out_sem[k], outs[k] + g * 16 + 16)
                            hold(sp)

                @block.vector
                def _(dve):
                    dve.memset(hT[D:D + 1, :], 1.0).then_inc(s_ones, 1)
                    with dve.Fori(0, NG) as g:
                        xg = X[:, bass.ds(g * GT, GT), :]
                        kg = keepN[:, bass.ds(g * GT, GT), :]
                        dg = rdeg[:, bass.ds(g * GT, GT)]

                        def own_part(dst, t0, n):
                            return dst[:, bass.ds(g * GT + t0, n), :]

                        if take == "msg":
                            after(dve, T, "fold", g)
                            done(dve.tensor_tensor(hT[0:D, :], psT, keep[0:D, bass.ds(g * (GT * P), GT * P)], ALU.add), V, "z")
                            done(dve.tensor_scalar(dg, ps[:, NB, 0:GT], 1.0, None, ALU.max), V, "deg")
                            after(dve, V, "deg", g)
                            hold(dve)
                            done(dve.reciprocal(dg, dg), V, "rdeg")
                            after(dve, T, "upd", g)
                            for b, t0, n in parts:
                                ins = dve.tensor_tensor(own_part(X, t0, n), own_part(X, t0, n), tiles_of(b, n, 0, D), ALU.add)
                            done(ins, V, "x")
                        if take == "prop":
                            for k, t in enumerate([xc[:], hN[:, :, 0:D], late[0][:], late[1][:]]):
                                dve.wait_ge(in_sem[k], g * 16 + 16)
                                if k:
                                    after(dve, V, f"p{k - 1}", g)
                                done(dve.tensor_tensor(xg, xg, t, ALU.add), V, f"p{k}" if k < 3 else "x")
                        if take in ("sage1", "sage2"):
                            after(dve, T, "mean", g)
                            for b, t0, n in parts:
                                ins = dve.tensor_tensor(xc[:, t0:t0 + n, :], tiles_of(b, n, 0, D),
                                                        each(rdeg[:, bass.ds(g * GT + t0, n)], n), ALU.mult)
                            done(ins, V, "scaled")
                            after(dve, V, "scaled", g)
                            done(dve.tensor_tensor(xc[:], xc[:], kg, ALU.add), V, "pre")
                            after(dve, V, "pre", g)
                            if take == "sage1":
                                done(dve.tensor_scalar(hN[:, :, 0:D], xc[:], 0.0, None, ALU.max), V, "h")
                            else:
                                done(dve.scalar_tensor_tensor(xg, xc[:], 0.0, xg, ALU.max, ALU.add), V, "x")
                        if take == "soft":
                            after(dve, T, "mean", g)
                            for b, t0, n in parts:
                                ins = dve.tensor_scalar(one(st[:, 0, t0:t0 + n]), tiles_of(b, n, D, D + 1), 1.0e-30, None, ALU.max)
                            done(ins, V, "den")
                            after(dve, V, "den", g)
                            done(dve.reciprocal(st[:, 1, :], st[:, 0, :]), V, "rden")
                            after(dve, V, "rden", g)
                            for b, t0, n in parts:
                                ins = dve.tensor_tensor(xc[:, t0:t0 + n, :], tiles_of(b, n, 0, D), each(st[:, 1, t0:t0 + n], n), ALU.mult)
                            done(ins, V, "scaled")
                            after(dve, V, "scaled", g)
                            done(dve.tensor_tensor(xc[:], xc[:], kg, ALU.add), V, "pre")
                            after(dve, V, "pre", g)
                            done(dve.scalar_tensor_tensor(xg, xc[:], 0.0, xg, ALU.max, ALU.add), V, "x")
                        if "rstd" in V.steps:
                            if take:
                                after(dve, V, "x", g)
                                hold(dve)
                            done(dve.tensor_reduce(st[:, 0, :], xg, AX, ALU.add), V, "sum")
                            after(dve, V, "sum", g)
                            done(dve.tensor_scalar(st[:, 1, :], st[:, 0, :], 1.0 / D, None, ALU.mult), V, "avg")
                            after(dve, V, "avg", g)
                            done(dve.tensor_tensor(xc[:], xg, each(st[:, 1, :]), ALU.subtract), V, "xc")
                            after(dve, A, "square", g)
                            done(dve.tensor_reduce(st[:, 2, :], hN[:, :, 0:D], AX, ALU.add), V, "var")
                            after(dve, A, "std", g)
                            done(dve.reciprocal(st[:, 4, :], st[:, 3, :]), V, "rstd")
                            after(dve, V, "rstd", g)
                            done(dve.scalar_tensor_tensor(hN[:, :, 0:D], xc[:], 0.0, each(st[:, 4, :]), ALU.max, ALU.mult), V, "h")
                        if take is None:
                            after(dve, T, "src", g)
                            hold(dve)
                            done(dve.tensor_copy(keep[0:D, bass.ds(g * (GT * P), GT * P)], psT), V, "own")
                            after(dve, T, "dst", g)
                            for b, t0, n in parts:
                                ins = dve.tensor_copy(xc[:, t0:t0 + n, :], tiles_of(b, n, 0, D))
                            done(ins, V, "dst_row")
                        if take == "msg":
                            after(dve, T, "wh", g)
                            for b, t0, n in parts:
                                ins = dve.tensor_copy(xc[:, t0:t0 + n, :], tiles_of(b, n, 0, D))
                            done(ins, V, "wh")
                            after(dve, V, "wh", g)
                            done(dve.scalar_tensor_tensor(xg, xc[:], coef[:, 12:13], xg, ALU.mult, ALU.add), V, "x_wh")
                            after(dve, A, "wh_square", g)
                            done(dve.tensor_reduce(st[:, 2, :], hN[:, :, 0:D], AX, ALU.add), V, "norm2")
                            after(dve, A, "norm", g)
                            done(dve.tensor_copy(hN[:, :, D:D + 1], one(st[:, 3, :])), V, "norm_col")
                            done(dve.tensor_copy(hN[:, :, 0:D], xc[:]), V, "row")
                        if take in ("prop", "sage1", "sage2"):
                            after(dve, T, "own", g)
                            hold(dve)
                            for b, t0, n in parts:
                                ins = dve.tensor_copy(own_part(keepN, t0, n), tiles_of(b, n, 0, D))
                            done(ins, V, "own")
                        if take == "sage2":
                            for b, t0, n in parts:
                                ins = dve.tensor_copy(hN[:, t0:t0 + n, D + 1:D + 2], tiles_of(b, n, D, D + 1))
                            done(ins, V, "score")
                            for b, t0, n in parts:
                                ins = dve.tensor_copy(xc[:, t0:t0 + n, 0:1], tiles_of(b, n, D + 1, D + 2))
                            done(ins, V, "dst_score")
                            done(dve.memset(hN[:, :, D:D + 1], 1.0), V, "row")
                        for k in range(len(rows)):
                            dve.wait_ge(out_sem[k], outs[k] + g * 16 + 16)

                @block.scalar
                def _(act):
                    with act.Fori(0, NG) as g:
                        if "sums" in A.steps:
                            done(act.activation(accS[:], acc[0:D + 1, bass.ds(g * (GT * P), GT * P)], ACT.Copy), A, "sums")
                        if take == "msg":
                            after(act, V, "z", g)
                            act.wait_ge(s_ones, n_ones[0])
                            done(act.activation(hT[0:D, :], hT[0:D, :], ACT.Relu), A, "z")
                        if "std" in A.steps:
                            after(act, V, "xc", g)
                            done(act.activation(hN[:, :, 0:D], xc[:], ACT.Square), A, "square")
                            after(act, V, "var", g)
                            done(act.activation(st[:, 3, :], st[:, 2, :], ACT.Sqrt, bias=small[:, 0:1], scale=1.0 / D), A, "std")
                        if "hT" in A.steps:
                            after(act, T, "turned", g)
                            done(act.activation(hT[0:D, :], psT, ACT.Copy), A, "hT")
                        if take is None:
                            after(act, T, "src", g)
                            for b, t0, n in parts:
                                ins = act.activation(hN[:, t0:t0 + n, 0:D], tiles_of(b, n, 0, D), ACT.Copy)
                            done(ins, A, "src_row")
                            after(act, T, "dst", g)
                        if take == "msg":
                            after(act, V, "wh", g)
                            done(act.activation(hN[:, :, 0:D], xc[:], ACT.Square), A, "wh_square")
                            after(act, V, "norm2", g)
                            done(act.activation(st[:, 3, :], st[:, 2, :], ACT.Sqrt), A, "norm")
                        if "own" in T.steps:
                            after(act, T, "own", g)
                        if take == "soft":
                            after(act, T, "mean", g)

                @block.tensor
                def _(pe):
                    with pe.Fori(0, NG) as g:
                        if take == "msg":
                            after(pe, A, "sums", g)
                            for t in range(GT):
                                pe.matmul(ps[:, NB, t:t + 1], accS[:, t * P:(t + 1) * P], e_deg[:], start=True, stop=True)
                            for b in range(NB):
                                ins = pe.matmul(ps[0:D, b, :], w_fold[:], accS[:, b * 512:(b + 1) * 512], start=True, stop=True)
                            done(ins, T, "fold")
                            after(pe, V, "deg", g)
                            after(pe, A, "z", g)
                            done(products(pe, hT, D + 1, w_upd2[:]), T, "upd")
                        if take in ("sage1", "sage2", "soft"):
                            after(pe, A, "sums", g)
                            w = {"sage1": w_l1, "sage2": w_l2, "soft": w_hm}[take]
                            done(products(pe, accS, w.shape[0], w[:]), T, "mean")
                        if "turned" in T.steps:
                            after(pe, V, "h", g)
                            hold(pe)
                            for t in range(GT):
                                ins = pe.transpose(psT[:, t * P:(t + 1) * P], hN[:, t, 0:D], ident[:])
                            done(ins, T, "turned")
                            after(pe, A, "hT", g)
                            pe.wait_ge(s_ones, n_ones[0])
                        if take is None:
                            for b in range(NB):
                                pe.matmul(ps[0:D, b, :], w_in[:, 2 * D:3 * D], hT[:, b * 512:(b + 1) * 512], start=True, stop=True)
                            done(products(pe, hT, D + 1, w_in[:, 0:D]), T, "src")
                            after(pe, A, "src_row", g)
                            done(products(pe, hT, D + 1, w_in[:, D:2 * D]), T, "dst")
                            after(pe, V, "dst_row", g)
                        if take == "msg":
                            done(products(pe, hT, D + 1, w_att[:]), T, "wh")
                            after(pe, V, "wh", g)
                        if take in ("prop", "sage1", "sage2"):
                            w = {"prop": w_r1, "sage1": w_r2, "sage2": w_own}[take]
                            done(products(pe, hT, D + 1, w[:]), T, "own")
                            after(pe, V, "dst_score" if take == "sage2" else "own", g)
                        if take == "soft":
                            after(pe, V, "scaled", g)
            for k in range(len(rows)):
                outs[k] += 16 * NG
            for who in (V, A, T):
                who.end(NG)

        LN = " sum avg xc var rstd h"

        s_acc0 = sem("acc_zeroed")
        n_acc0 = [0]
        s_next = sem("next_bases")
        n_next = [0]

        def zero_sums(start_max=False, fill_props=None):
            n_acc0[0] += 1
            with nc.Block() as block:
                @block.vector
                def _(dve):
                    dve.memset(acc[:, 0:NPAD // 2], 0.0)
                    dve.memset(acc[:, NPAD // 2:], 0.0).then_inc(s_acc0, 1)
                    if start_max:
                        dve.wait_ge(s_acc0, n_acc0[0])
                        dve.memset(acc[96:97, :], NEG)

                if fill_props is not None:
                    @block.gpsimd
                    def _(sp):
                        sp.wait_ge(s_acc0, n_acc0[0])
                        for k in range(NPROP):
                            sp.dma_start(props[k].rearrange("(p t) d -> p (t d)", p=P), acc[:, 0:NT * D]).then_inc(fill_props[k], FILL)
                        for k in range(NPROP):
                            sp.wait_ge(fill_props[k], FILL)

        def move_bases(dve, to_start):
            if to_start:
                dve.tensor_copy(base_bc[:], base0[:]).then_inc(s_next, 1)
            else:
                dve.tensor_scalar(base_bc[:], base_bc[:], float(P), float(N), ALU.add, ALU.min).then_inc(s_next, 1)
            dve.drain()
            dve.tensor_copy(base_i[:], base_bc[0:1, :]).then_inc(s_next, 1)
            dve.drain()

        def edge_pass(name, stages, src_table, cols, bufs, programs, rows_user, oh_user="sums", win_user="pre",
                      last_stage="acc", win_table=None, wcols=0, edges=False, pool=None, views={}):
            with ExitStack() as scope:
                S = {n: sem(f"{name}_{n}") for n in stages.split()}
                gathered = [sem(f"{name}_gathered{k}") for k in range(U)]
                loaded = [sem(f"{name}_loaded{k}") for k in range(2)]
                s_const = sem(f"{name}_constants")

                def buf(n, shape, dt=F32, k=2):
                    return [scope.enter_context(nc.sbuf_tensor(f"{name}_{n}{i}", shape, dt)) for i in range(k)]

                B = {"G": buf("G", [P, TPC, cols], k=U), "idx": buf("idx", [P, TPC], I32, k=U),
                     "OH": buf("OH", [P, TPC, P]), "drel": buf("drel", [P, TPC])}
                if win_table is not None:
                    B["win"], B["OHT"] = buf("win", [P, wcols]), buf("OHT", [P, TPC, P])
                if edges:
                    B["edge"] = buf("edge", [P, TPC, D])
                for n, shape, dt, k in bufs:
                    B[n] = buf(n, shape, dt, k)
                B.update(views)
                load_inc = 16 * ((win_table is not None) + edges)
                with nc.Block() as block:
                    @block.vector
                    def _(dve):
                        for s in S.values():
                            dve.sem_inc(s, U)
                        k = 0
                        if "msg" in B:
                            for m in B["msg"]:
                                dve.memset(m[:, :, D:D + 1], 1.0).then_inc(s_const, 1)
                                k += 1
                        if k:
                            dve.wait_ge(s_const, k)
                rounds = nc.values_load(rounds_i[0:1, 0:1], min_val=1, max_val=NT)
                with nc.Fori(0, rounds) as r:

                    def at(c, back=0):
                        return r * C + (c + 1 + U - back)

                    def chunks(eng, body, lead=None):
                        if lead:
                            lead()
                        with eng.Fori(0, C // U - 1) as i:
                            for h in range(U):
                                body(i * U + h, h, r * (C // U) + (i + 1), False)
                        for h in range(U):
                            body(C - U + h, h, r * (C // U) + C // U, h == U - 1)

                    def wait_gather(eng, h, turn):
                        eng.wait_ge(gathered[h], turn * (16 * TPC))

                    def wait_loads(eng, h, turn):
                        eng.wait_ge(loaded[h % 2], turn * (U // 2 * load_inc) + (h // 2 + 1 - U // 2) * load_inc)

                    K = dict(S=S, B=B, at=at, rows_user=rows_user, oh_user=oh_user, wait_gather=wait_gather, wait_loads=wait_loads, chunks=chunks, r=r)

                    def run(eng, key):
                        prep, main = programs[key]

                        def body(c, h, turn, last):
                            if prep and not last:
                                prep(K, eng, c + 1, (h + 1) % U, turn + (h + 1) // U)
                            main(K, eng, c, h, turn)

                        chunks(eng, body, (lambda: prep(K, eng, 0, 0, r * (C // U) + 1)) if prep else None)

                    def gather(eng, c, h, turn):
                        eng.wait_ge(S[rows_user], at(c, U))
                        eng.wait_ge(S["idx"], at(c))
                        hold(eng)
                        for j in range(TPC):
                            eng.indirect_dma_start(B["G"][h][:, j, :], None, src_table, bass.IndirectOffsetOnAxis(
                                ap=B["idx"][h][:, j:j + 1], axis=0)).then_inc(gathered[h], 16)

                    with nc.Block() as block:
                        if load_inc:
                            @block.sync
                            def _(sp):
                                def body(c, h, turn, last):
                                    b = h % 2
                                    if win_table is not None:
                                        first = sp.value_load(base_i[0:1, bass.ds(c, 1)], min_val=0, max_val=N)
                                        sp.wait_ge(S[win_user], at(c, 2))
                                        hold(sp)
                                        with nc.allow_non_contiguous_dma("a window's column"):
                                            sp.dma_start(B["win"][b][:], win_table[bass.ds(first, P), 0:wcols]).then_inc(loaded[b], 16)
                                    if edges:
                                        sp.wait_ge(S["edge_turned"], at(c, 2))
                                        hold(sp)
                                        lo = E - CE if last else c * CE
                                        rows = a["edge_attr_64"][bass.ds(lo, CE), :].rearrange("(p j) d -> p j d", j=TPC)
                                        sp.dma_start(B["edge"][b][:], rows).then_inc(loaded[b], 16)
                                chunks(sp, body)

                        @block.gpsimd
                        def _(eng):
                            if pool is None:
                                chunks(eng, lambda c, h, turn, last: gather(eng, c, h, turn))
                            else:
                                pool(K, eng, gather)

                        @block.vector
                        def _(dve):
                            run(dve, "dve")
                            dve.wait_ge(S[last_stage], at(C - 1))
                            move_bases(dve, False)

                        @block.scalar
                        def _(act):
                            run(act, "act")

                        @block.tensor
                        def _(pe):
                            run(pe, "pe")
                with nc.Block() as block:
                    @block.vector
                    def _(dve):
                        move_bases(dve, True)

        def cols_of(t, c):
            return t[:, bass.ds(c, 1), :].rearrange("p o j -> p (o j)")

        def wide(v, m):
            return v.rearrange("p (j o) -> p j o", o=1).broadcast_to([P, TPC, m])

        iota_all = iota_f[:].rearrange("p (o n) -> p o n", o=1).broadcast_to([P, TPC, P])
        banks = lambda b: ps[:, b:b + 2, :].rearrange("p b q -> p (b q)").rearrange("p (j n) -> p j n", n=P)

        def one_hot(K, dve, c, h, turn):
            S, B, at, b = K["S"], K["B"], K["at"], h % 2
            dve.tensor_scalar(B["drel"][b][:], cols_of(dstf, c), base_bc[:, bass.ds(c, 1)], None, ALU.subtract).then_inc(S["drel"], 1)
            dve.wait_ge(S[K["oh_user"]], at(c, 2))
            dve.wait_ge(S["drel"], at(c))
            dve.tensor_tensor(B["OH"][b][:], iota_all, wide(B["drel"][b][:], P), ALU.is_equal).then_inc(S["oh"], 1)

        def copy_indices(K, act, c, h, turn):
            S, B, at = K["S"], K["B"], K["at"]
            act.wait_ge(S[K["rows_user"]], at(c, U))
            act.activation(B["idx"][h][:], cols_of(srci, c), ACT.Copy).then_inc(S["idx"], 1)

        def turn_one_hot(K, pe, c, h, turn):
            S, B, at, b = K["S"], K["B"], K["at"], h % 2
            pe.wait_ge(S["oh"], at(c))
            pe.wait_ge(S["oht"], at(c, 1))
            for j in range(TPC):
                ins = pe.transpose(banks(0)[:, j, :], B["OH"][b][:, j, :], ident[:])
            ins.then_inc(S["oh_turned"], 1)

        def take_one_hot(K, act, c, h, turn, user):
            S, B, at, b = K["S"], K["B"], K["at"], h % 2
            act.wait_ge(S["oh_turned"], at(c))
            act.wait_ge(S[user], at(c, 2))
            act.activation(B["OHT"][b][:], banks(0), ACT.Copy).then_inc(S["oht"], 1)

        def sum_by_node(K, pe, rows, m, c, h):
            S, B, at = K["S"], K["B"], K["at"]
            pe.wait_ge(S["acc"], at(c, 2))
            for j in range(TPC):
                ins = pe.matmul(ps[0:m, 6 + h % 2, 0:P], rows(j), B["OH"][h % 2][:, j, :], start=(j == 0), stop=(j == TPC - 1))
            ins.then_inc(S["sums"], 1)

        def add_sums(K, dve, m, c, h):
            S, at = K["S"], K["at"]
            first = dve.value_load(base_i[0:1, bass.ds(c, 1)], min_val=0, max_val=N)
            dve.wait_ge(S["sums"], at(c))
            dve.wait_ge(S["acc"], at(c, 1))
            w = acc[0:m, bass.ds(first, P)]
            dve.tensor_tensor(w, w, ps[0:m, 6 + h % 2, 0:P], ALU.add).then_inc(S["acc"], 1)

        def msg_dve_prep(K, dve, c, h, turn):
            one_hot(K, dve, c, h, turn)

        def msg_dve(K, dve, c, h, turn):
            S, B, at, b = K["S"], K["B"], K["at"], h % 2
            dve.wait_ge(S["pre"], at(c))
            dve.wait_ge(S["sums"], at(c, 2))
            K["wait_gather"](dve, h, turn)
            dve.tensor_tensor(B["msg"][b][:, :, 0:D], ps[:, 4 + b, :].rearrange("p (j d) -> p j d", d=D), B["G"][h][:], ALU.add).then_inc(S["summed"], 1)
            add_sums(K, dve, D + 1, c, h)

        def msg_act_prep(K, act, c, h, turn):
            copy_indices(K, act, c, h, turn)
            take_one_hot(K, act, c, h, turn, "pre")
            S, B, at, b = K["S"], K["B"], K["at"], h % 2
            act.wait_ge(S["edge_turned"], at(c))
            act.activation(B["edgeT"][b][:], banks(2)[0:D], ACT.Copy).then_inc(S["edgeT"], 1)

        def msg_act(K, act, c, h, turn):
            S, B, at, b = K["S"], K["B"], K["at"], h % 2
            act.wait_ge(S["summed"], at(c))
            act.activation(B["msg"][b][:, :, 0:D], B["msg"][b][:, :, 0:D], ACT.Relu).then_inc(S["msg"], 1)

        def msg_pe_prep(K, pe, c, h, turn):
            S, B, at, b = K["S"], K["B"], K["at"], h % 2
            turn_one_hot(K, pe, c, h, turn)
            K["wait_loads"](pe, h, turn)
            pe.wait_ge(S["edgeT"], at(c, 1))
            hold(pe)
            for j in range(TPC):
                ins = pe.transpose(banks(2)[0:D, j, :], B["edge"][b][:, j, :], ident[:])
            ins.then_inc(S["edge_turned"], 1)

        def msg_pe(K, pe, c, h, turn):
            S, B, at, b = K["S"], K["B"], K["at"], h % 2
            pe.wait_ge(S["edgeT"], at(c))
            pe.wait_ge(S["oht"], at(c))
            pe.wait_ge(S["summed"], at(c, 2))
            for j in range(TPC):
                o = ps[:, 4 + b, j * D:(j + 1) * D]
                pe.matmul(o, B["edgeT"][b][:, j, :], w_edge[:], start=True, stop=False)
                ins = pe.matmul(o, B["OHT"][b][:, j, :], B["win"][b][:], start=False, stop=True)
            ins.then_inc(S["pre"], 1)
            pe.wait_ge(S["msg"], at(c))
            sum_by_node(K, pe, lambda j: B["msg"][b][:, j, :], D + 1, c, h)

        def sage_act(K, act, c, h, turn):
            copy_indices(K, act, c, h, turn)

        def sage_pe(K, pe, c, h, turn):
            K["wait_gather"](pe, h, turn)
            pe.wait_ge(K["S"]["oh"], K["at"](c))
            sum_by_node(K, pe, lambda j: K["B"]["G"][h][:, j, :], D, c, h)

        def sage_dve(K, dve, c, h, turn):
            add_sums(K, dve, D, c, h)

        FILL = 64
        s_prop = [sem(f"prop{k}") for k in range(NPROP)]

        def scatters_before(K, c, more=0):
            return (K["r"] * C + c) * (16 * TPC // NPROP) + (FILL + more)

        def wait_scatters(K, eng, c):
            for s in s_prop:
                eng.wait_ge(s, scatters_before(K, c, -16 * TPC // NPROP))

        def att_pool(K, eng, gather):
            S, B, at, r = K["S"], K["B"], K["at"], K["r"]

            def scatter(c, h):
                eng.wait_ge(S["sidx"], at(c))
                eng.wait_ge(S["out"], at(c))
                for j in range(TPC):
                    k = j % NPROP
                    eng.wait_ge(s_prop[k], scatters_before(K, c, 16 * (j // NPROP)))
                    hold(eng)
                    eng.indirect_dma_start(props[k], bass.IndirectOffsetOnAxis(ap=B["sidx"][h % 2][:, j:j + 1], axis=0),
                                           B["out"][h % 2][:, j, :], None, compute_op=ALU.add).then_inc(s_prop[k], 16)

            def body(c, h, turn, last, end=False):
                if not (end and h >= U - 2):
                    gather(eng, c + 2, (h + 2) % U, turn + (h + 2) // U)
                scatter(c, h)

            for h in range(2):
                gather(eng, h, h, r * (C // U) + 1)
            with eng.Fori(0, C // U - 1) as i:
                for h in range(U):
                    body(i * U + h, h, None or (r * (C // U) + (i + 1)), False)
            for h in range(U):
                body(C - U + h, h, r * (C // U) + C // U, h == U - 1, end=True)
            for s in s_prop:
                eng.wait_ge(s, scatters_before(K, C))

        def att_dve_prep(K, dve, c, h, turn):
            S, B, at, b = K["S"], K["B"], K["at"], h % 2
            one_hot(K, dve, c, h, turn)
            dve.wait_ge(S["src_turned"], at(c))
            dve.wait_ge(S["merged"], at(c, 2))
            dve.tensor_tensor(B["SM"][b][:], banks(2), wide(B["srcs"][b][:], P), ALU.is_equal).then_inc(S["sm"], 1)
            dve.wait_ge(S["sm"], at(c))
            dve.tensor_tensor(B["before"][0][:], B["SM"][b][:], lower[:].rearrange("p (o n) -> p o n", o=1).broadcast_to([P, TPC, P]), ALU.mult).then_inc(S["before"], 1)
            dve.tensor_scalar(B["t"][b][:, 0], B["srcs"][b][:], -1.0, trash[:], ALU.mult, ALU.add).then_inc(S["away"], 1)
            dve.wait_ge(S["before"], at(c))
            dve.tensor_reduce(B["t"][b][:, 1], B["before"][0][:], AX, ALU.add).then_inc(S["count"], 1)
            dve.wait_ge(S["count"], at(c))
            dve.wait_ge(S["away"], at(c))
            dve.scalar_tensor_tensor(B["t"][b][:, 2], B["t"][b][:, 1], 0.5, B["t"][b][:, 0], ALU.is_gt, ALU.mult).then_inc(S["shift"], 1)
            dve.wait_ge(S["shift"], at(c))
            wait_scatters(K, dve, c)
            dve.tensor_tensor(B["sidx"][b][:], B["t"][b][:, 2], B["srcs"][b][:], ALU.add).then_inc(S["sidx"], 1)

        def att_dve(K, dve, c, h, turn):
            S, B, at, b = K["S"], K["B"], K["at"], h % 2
            t = B["m"][b]
            G = B["G"][h]
            wc = lambda q, lo, hi: ps[:, 4 + q, 0:4 * (D + 1)].rearrange("p (j d) -> p j d", d=D + 1)[:, :, lo:hi]
            K["wait_gather"](dve, h, turn)
            dve.wait_ge(S["wc"], at(c))
            for q in range(2):
                j = slice(4 * q, 4 * q + 4)
                dve.tensor_tensor(B["prod"][0][:, j, :], G[:, j, 0:D], wc(q, 0, D), ALU.mult)
                ins = dve.tensor_tensor(t[:, 0, j].rearrange("p (j o) -> p j o", o=1), G[:, j, D:D + 1], wc(q, D, D + 1), ALU.mult)
            ins.then_inc(S["dot"], 1)
            dve.wait_ge(S["dot"], at(c))
            dve.tensor_reduce(t[:, 1], B["prod"][0][:], AX, ALU.add)
            dve.tensor_scalar(t[:, 2], t[:, 0], 1.0e-8, None, ALU.max).then_inc(S["a1"], 1)
            dve.wait_ge(S["a1"], at(c))
            dve.reciprocal(t[:, 3], t[:, 2]).then_inc(S["a2"], 1)
            dve.wait_ge(S["a2"], at(c))
            dve.tensor_tensor(t[:, 4], t[:, 1], t[:, 3], ALU.mult).then_inc(S["sim"], 1)
            dve.wait_ge(S["sim"], at(c))
            dve.tensor_scalar(t[:, 5], t[:, 4], 0.0, coef[:, 10:11], ALU.max, ALU.mult)
            dve.tensor_scalar(t[:, 6], t[:, 4], 0.0, coef[:, 11:12], ALU.min, ALU.mult).then_inc(S["a3"], 1)
            dve.wait_ge(S["a3"], at(c))
            dve.tensor_tensor(t[:, 7], t[:, 5], t[:, 6], ALU.add).then_inc(S["a4"], 1)
            dve.wait_ge(S["a4"], at(c))
            dve.tensor_tensor(t[:, 8], t[:, 7], cols_of(ewt, c), ALU.mult).then_inc(S["weight"], 1)
            dve.wait_ge(S["weight"], at(c))
            dve.wait_ge(S["merged"], at(c, 2))
            for q in range(2):
                j = slice(4 * q, 4 * q + 4)
                w = t[:, 8, j].rearrange("p (j o) -> p j o", o=1).broadcast_to([P, 4, D])
                ins = dve.tensor_tensor(B["V"][b][:, j, :], wc(q, 0, D), w, ALU.mult)
            ins.then_inc(S["v"], 1)

        def att_act_prep(K, act, c, h, turn):
            S, B, at, b = K["S"], K["B"], K["at"], h % 2
            copy_indices(K, act, c, h, turn)
            act.wait_ge(S["sidx"], at(c, 2))
            act.activation(B["srcs"][b][:], cols_of(srcf, c), ACT.Copy).then_inc(S["srcs"], 1)
            take_one_hot(K, act, c, h, turn, "wc")

        def att_act(K, act, c, h, turn):
            S, B, at, b = K["S"], K["B"], K["at"], h % 2
            act.wait_ge(S["merged"], at(c))
            wait_scatters(K, act, c)
            act.activation(B["out"][b][:], ps[:, 6 + b, :].rearrange("p (j d) -> p j d", d=D), ACT.Copy).then_inc(S["out"], 1)

        def att_pe_prep(K, pe, c, h, turn):
            S, B, at, b = K["S"], K["B"], K["at"], h % 2
            turn_one_hot(K, pe, c, h, turn)
            pe.wait_ge(S["srcs"], at(c))
            pe.wait_ge(S["sm"], at(c, 1))
            for j in range(TPC):
                ins = pe.transpose(banks(2)[:, j, :], B["srcs"][b][:, j:j + 1].broadcast_to([P, P]), ident[:])
            ins.then_inc(S["src_turned"], 1)

        def att_pe(K, pe, c, h, turn):
            S, B, at, b = K["S"], K["B"], K["at"], h % 2
            pe.wait_ge(S["oht"], at(c))
            K["wait_loads"](pe, h, turn)
            pe.wait_ge(S["v"], at(c, 1))
            for j in range(TPC):
                ins = pe.matmul(ps[:, 4 + j // 4, (j % 4) * (D + 1):(j % 4 + 1) * (D + 1)], B["OHT"][b][:, j, :], B["win"][b][:], start=True, stop=True)
            ins.then_inc(S["wc"], 1)
            pe.wait_ge(S["v"], at(c))
            pe.wait_ge(S["sm"], at(c))
            pe.wait_ge(S["out"], at(c, 2))
            for j in range(TPC):
                ins = pe.matmul(ps[:, 6 + b, j * D:(j + 1) * D], B["SM"][b][:, j, :], B["V"][b][:, j, :], start=True, stop=True)
            ins.then_inc(S["merged"], 1)

        TOP = 96

        def soft_act_prep(K, act, c, h, turn):
            S, B, at, b = K["S"], K["B"], K["at"], h % 2
            copy_indices(K, act, c, h, turn)
            act.wait_ge(S["oh_turned"], at(c))
            act.wait_ge(S["top"], at(c, 2))
            act.activation(B["pen"][b], banks(0), ACT.Identity, bias=small[:, 8:9], scale=BIG)
            act.wait_ge(S["spread"], at(c, 2))
            act.activation(B["OHT"][b][:], banks(0), ACT.Copy).then_inc(S["oht"], 1)

        def soft_act(K, act, c, h, turn):
            S, B, at, b = K["S"], K["B"], K["at"], h % 2
            act.wait_ge(S["em"], at(c))
            act.wait_ge(S["rows"], at(c, 2))
            act.activation(B["Q"][b][:, 0:TOP], B["q"][b][:, 7:8].broadcast_to([P, TOP]), ACT.Exp).then_inc(S["ratio"], 1)
            act.wait_ge(S["e4"], at(c))
            act.activation(B["e"][b][:, 4], B["e"][b][:, 3], ACT.Exp).then_inc(S["ex"], 1)

        def soft_pe_prep(K, pe, c, h, turn):
            turn_one_hot(K, pe, c, h, turn)

        def soft_pe(K, pe, c, h, turn):
            S, B, at, b = K["S"], K["B"], K["at"], h % 2
            K["wait_gather"](pe, h, turn)
            pe.wait_ge(S["top"], at(c, 1))
            for j in range(TPC):
                pe.transpose(banks(2)[:, j, :], B["G"][h][:, j, D + 1:D + 2].broadcast_to([P, P]), ident[:])
            pe.wait_ge(S["mrow"], at(c))
            pe.wait_ge(S["e3"], at(c, 1))
            pe.matmul(ps[:, 4, 0:1], B["mrow"][b][:], small[0:1, 1:2], start=True, stop=True).then_inc(S["old"], 1)
            pe.wait_ge(S["em"], at(c))
            pe.wait_ge(S["oht"], at(c))
            for j in range(TPC):
                ins = pe.matmul(ps[:, 4, 16 + 2 * j:18 + 2 * j], B["OHT"][b][:, j, :], B["em"][b][:], start=True, stop=True)
            ins.then_inc(S["spread"], 1)
            pe.wait_ge(S["ratio"], at(c))
            pe.wait_ge(S["top_row"], at(c, 1))
            pe.matmul(ps[0:TOP + 1, 5, 0:P], B["Q"][b][:], ident[:], start=True, stop=True).then_inc(S["rows"], 1)
            pe.wait_ge(S["msg"], at(c))
            sum_by_node(K, pe, lambda j: B["msg"][b][:, j, :], D + 1, c, h)

        def soft_dve(K, dve, c, h, turn):
            S, B, at, b = K["S"], K["B"], K["at"], h % 2
            q, e, em, G, t_dst = B["q"][b], B["e"][b], B["em"][b], B["G"][h], B["win"][b]
            first = dve.value_load(base_i[0:1, bass.ds(c, 1)], min_val=0, max_val=N)
            dve.wait_ge(S["top_row"], at(c, 1))
            dve.wait_ge(S["old"], at(c, 2))
            hold(dve)
            dve.tensor_copy(B["mrow"][b][:], acc[TOP:TOP + 1, bass.ds(first, P)]).then_inc(S["mrow"], 1)
            dve.wait_ge(S["old"], at(c))
            dve.wait_ge(S["oht"], at(c))
            hold(dve)
            dve.tensor_tensor_reduce(B["junk"][0], two_banks(2), B["pen"][b].rearrange("p j n -> p (j n)"), 1.0, NEG, ALU.add, ALU.max,
                                     q[:, 2:3]).then_inc(S["top"], 1)
            dve.tensor_copy(q[:, 0:1], ps[:, 4, 0:1])
            dve.wait_ge(S["top"], at(c))
            dve.tensor_tensor(q[:, 1:2], ps[:, 4, 0:1], q[:, 2:3], ALU.max).then_inc(S["new"], 1)
            K["wait_loads"](dve, h, turn)
            dve.wait_ge(S["new"], at(c))
            dve.wait_ge(S["rows"], at(c, 2))
            dve.tensor_copy(B["Q"][b][:, TOP:TOP + 1], q[:, 1:2])
            dve.tensor_scalar(q[:, 3:5], q[:, 0:2], t_dst[:, 0:1], None, ALU.add).then_inc(S["u"], 1)
            dve.wait_ge(S["u"], at(c))
            dve.scalar_tensor_tensor(q[:, 5:7], q[:, 3:5], 0.01, q[:, 3:5], ALU.mult, ALU.max).then_inc(S["l"], 1)
            dve.wait_ge(S["l"], at(c))
            dve.tensor_tensor(q[:, 7:8], q[:, 5:6], q[:, 6:7], ALU.subtract)
            dve.tensor_copy(em[:, 0:1], t_dst[:, 0:1])
            dve.tensor_copy(em[:, 1:2], q[:, 6:7]).then_inc(S["em"], 1)
            sp2 = ps[:, 4, 16:16 + 2 * TPC].rearrange("p (j k) -> p k j", k=2)
            dve.wait_ge(S["spread"], at(c))
            dve.tensor_tensor(e[:, 0], G[:, :, D + 1], sp2[:, 0], ALU.add).then_inc(S["e1"], 1)
            dve.wait_ge(S["e1"], at(c))
            dve.scalar_tensor_tensor(e[:, 1], e[:, 0], 0.01, e[:, 0], ALU.mult, ALU.max).then_inc(S["e2"], 1)
            dve.wait_ge(S["e2"], at(c))
            dve.tensor_tensor(e[:, 2], e[:, 1], sp2[:, 1], ALU.subtract).then_inc(S["e3"], 1)
            dve.wait_ge(S["e3"], at(c))
            dve.tensor_scalar(e[:, 3], e[:, 2], 0.0, None, ALU.min).then_inc(S["e4"], 1)
            dve.wait_ge(S["ex"], at(c))
            dve.wait_ge(S["sums"], at(c, 2))
            K["wait_gather"](dve, h, turn)
            dve.tensor_tensor(B["msg"][b][:], G[:, :, 0:D + 1], wide(e[:, 4], D + 1), ALU.mult).then_inc(S["msg"], 1)
            w = acc[0:D + 1, bass.ds(first, P)]
            dve.wait_ge(S["rows"], at(c))
            dve.wait_ge(S["acc"], at(c, 1))
            dve.tensor_tensor(w, w, ps[0:D + 1, 5, 0:P], ALU.mult).then_inc(S["scaled"], 1)
            dve.tensor_copy(acc[TOP:TOP + 1, bass.ds(first, P)], ps[TOP:TOP + 1, 5, 0:P]).then_inc(S["top_row"], 1)
            dve.wait_ge(S["sums"], at(c))
            dve.wait_ge(S["scaled"], at(c))
            dve.tensor_tensor(w, w, ps[0:D + 1, 6 + b, 0:P], ALU.add).then_inc(S["acc"], 1)

        two_banks = lambda b: ps[:, b:b + 2, :].rearrange("p b q -> p (b q)")
        zero_sums(fill_props=s_prop)
        phase("enter", None, "sum avg xc var rstd h own dst_row", "square std hT src_row", "turned src dst",
              [(msg_src, "hN", D, A, "src_row"), (msg_dst, "xc", D, V, "dst_row")])
        edge_pass("msg", "drel oh idx oh_turned oht edge_turned edgeT pre summed msg sums acc", msg_src, D,
                  [("edgeT", [D, TPC, P], F32, 2), ("msg", [P, TPC, D + 1], F32, 2)],
                  {"dve": (msg_dve_prep, msg_dve), "act": (msg_act_prep, msg_act), "pe": (msg_pe_prep, msg_pe)},
                  rows_user="summed", win_table=msg_dst, wcols=D, edges=True)
        phase("after_msg", "msg", "z deg rdeg x" + LN + " wh x_wh norm2 norm_col row", "sums z square std hT wh_square norm",
              "fold upd turned wh", [(att, "hN", D + 1, V, "row")])
        edge_pass("att", "drel oh idx oh_turned oht srcs src_turned sm before away count shift sidx wc dot a1 a2 sim a3 a4 weight v merged out",
                  att, D + 1,
                  [("V", [P, TPC, D], F32, 2), ("out", [P, TPC, D], F32, 2), ("sidx", [P, TPC], I32, 2), ("srcs", [P, TPC], F32, 2),
                   ("t", [P, 3, TPC], F32, 2), ("m", [P, 9, TPC], F32, 2)],
                  {"dve": (att_dve_prep, att_dve), "act": (att_act_prep, att_act), "pe": (att_pe_prep, att_pe)},
                  rows_user="dot", oh_user="oh_turned", win_user="wc", last_stage="v", win_table=att, wcols=D + 1, pool=att_pool,
                  views={"SM": [acc[:, k * CE:(k + 1) * CE].rearrange("p (j n) -> p j n", n=P) for k in range(2)],
                         "before": [acc[:, 2 * CE:3 * CE].rearrange("p (j n) -> p j n", n=P)],
                         "prod": [acc[:, 3 * CE:3 * CE + TPC * D].rearrange("p (j d) -> p j d", d=D)]})
        phase("after_att", "prop", "p0 p1 p2 x" + LN + " own", "square std hT", "turned own", [(sage1, "hN", D, V, "h")])
        sage = {"dve": (one_hot, sage_dve), "act": (None, sage_act), "pe": (None, sage_pe)}
        zero_sums()
        edge_pass("sage1", "drel oh idx sums acc", sage1, D, [], sage, rows_user="sums")
        phase("after_sage1", "sage1", "scaled pre h own", "sums hT", "mean turned own", [(sage2, "hN", D, V, "h")])
        zero_sums()
        edge_pass("sage2", "drel oh idx sums acc", sage2, D, [], sage, rows_user="sums")
        phase("after_sage2", "sage2", "scaled pre x" + LN + " own score dst_score row", "sums square std hT",
              "mean turned own", [(soft, "hN", D + 2, V, "row"), (soft_dst, "xc", 1, V, "dst_score")])
        zero_sums(start_max=True)
        free = keep[:, NT * D:]
        edge_pass("soft", "drel oh idx oh_turned oht mrow old top new u l em ratio spread rows e1 e2 e3 e4 ex msg scaled top_row sums acc",
                  soft, D + 2,
                  [("msg", [P, TPC, D + 1], F32, 2), ("q", [P, 8], F32, 2), ("e", [P, 5, TPC], F32, 2), ("em", [P, 2], F32, 2),
                   ("mrow", [1, P], F32, 2), ("Q", [P, TOP + 1], F32, 2)],
                  {"dve": (one_hot, soft_dve), "act": (soft_act_prep, soft_act), "pe": (soft_pe_prep, soft_pe)},
                  rows_user="msg", win_user="em", win_table=soft_dst, wcols=1,
                  views={"pen": [free[:, k * CE:(k + 1) * CE].rearrange("p (j n) -> p j n", n=P) for k in range(2)],
                         "junk": [free[:, 2 * CE:3 * CE]]})
        phase("leave", "soft", "den rden scaled pre x", "sums", "mean", [])

        s_out = sem("out")
        with nc.Block() as block:
            @block.sync
            def _(sp):
                sp.dma_start(out[0:FULL * P].rearrange("(t p) d -> p t d", p=P), X[:, 0:FULL, :]).then_inc(s_out, 16)
                sp.dma_start(out[FULL * P:N], X[0:TAIL, FULL, :]).then_inc(s_out, 16)
                sp.wait_ge(s_out, 32)


def kernel(**inputs):
    import numpy as _np
    import concourse.bacc as _bacc
    from concourse import mybir as _mybir
    from concourse.bass_utils import run_bass_kernel_spmd as _run

    nc = _bacc.Bacc("TRN2", target_bir_lowering=False, num_devices=1)
    arrays, aps = {}, {}
    for name, v in inputs.items():
        v = _np.ascontiguousarray(v)
        arrays[name] = v
        aps[name] = nc.dram_tensor(name, v.shape, _mybir.dt.from_np(v.dtype), kind="ExternalInput").ap()
    out = nc.dram_tensor("result", inputs["x"].shape, F32, kind="ExternalOutput").ap()
    gnn_kernel(nc, aps, out)
    r = _run(nc, [arrays], core_ids=[0])
    return r.results[0]["result"]
```

```python
from contextlib import ExitStack

import concourse.bass as bass
from concourse import mybir

P = 128
D = 64
TPC = 8
CE = P * TPC
U = 4
GT = 20
NPROP = 4
NEG = -1.0e30
BIG = 1.0e30

F32 = mybir.dt.float32
I32 = mybir.dt.int32
ALU = mybir.AluOpType
ACT = mybir.ActivationFunctionType
AX = mybir.AxisListType.X


class Progress:

    def __init__(self, sem):
        self.sem, self.before, self.steps = sem, 0, []

    def begin(self, steps):
        self.steps = steps.split()

    def at(self, name, g):
        return self.before + g * len(self.steps) + (self.steps.index(name) + 1)

    def end(self, groups):
        self.before += groups * len(self.steps)


def gnn_kernel(nc, a, out):
    N, E = a["x"].shape[0], a["src"].shape[0]
    C = -(-E // CE)
    NG = -(-(N + P) // (P * GT))
    NT = NG * GT
    NPAD = NT * P
    FULL, TAIL = N // P, N % P
    HALF = C // 2
    TWICE = C * CE - E
    assert C % U == 0 and HALF <= P and TWICE % TPC == 0 and TAIL and E >= CE and (C - 1) * CE < E
    DUP = TWICE // TPC

    with ExitStack() as ctx:
        def sb(name, shape, dt=F32):
            return ctx.enter_context(nc.sbuf_tensor(name, shape, dt))

        def sem(name):
            return ctx.enter_context(nc.semaphore(name))

        def dram(name, shape):
            return nc.dram_tensor(name, shape, F32, kind="Internal").ap()

        msg_src = dram("msg_src", (NPAD, D))
        msg_dst = dram("msg_dst", (NPAD, D))
        att = dram("att", (NPAD, D + 1))
        sage1 = dram("sage1", (NPAD, D))
        sage2 = dram("sage2", (NPAD, D))
        soft = dram("soft", (NPAD, D + 2))
        soft_dst = dram("soft_dst", (NPAD, 1))
        props = [dram(f"prop{k}", (NPAD, D)) for k in range(NPROP)]

        X = sb("X", [P, NT, D])
        acc = sb("acc", [P, NPAD])
        keep = sb("keep", [P, NT * D])
        dstf = sb("dstf", [P, C, TPC])
        srci = sb("srci", [P, C, TPC], I32)
        ewt = sb("ewt", [P, C, TPC])
        base_bc = sb("base_bc", [P, C])
        base0 = sb("base0", [P, C])
        base_i = sb("base_i", [1, C], I32)
        rounds_i = sb("rounds_i", [1, 1], I32)
        ident = sb("ident", [P, P])
        iota_f = sb("iota_f", [P, P])
        lower = sb("lower", [P, P])
        trash = sb("trash", [P, 1])
        small = sb("small", [P, 32])

        w_in = sb("w_in", [D + 1, 3 * D])
        w_edge = sb("w_edge", [D, D])
        w_upd1 = sb("w_upd1", [D, D])
        w_msg2 = sb("w_msg2", [D + 1, D])
        w_msg2T = sb("w_msg2T", [D, D + 1])
        w_fold = sb("w_fold", [D + 1, D + 1])
        w_upd2 = sb("w_upd2", [D + 1, D])
        w_att = sb("w_att", [D + 1, D])
        w_r1 = sb("w_r1", [D + 1, D])
        w_l1 = sb("w_l1", [D, D])
        w_r2 = sb("w_r2", [D + 1, D])
        w_l2 = sb("w_l2", [D, D])
        w_lin = sb("w_lin", [D, 2 * D])
        w_own = sb("w_own", [D + 1, D + 2])
        w_hm = sb("w_hm", [D + 1, D + 1])
        coef = sb("coef", [P, 16])

        rdeg = sb("rdeg", [P, NT])

        ps = ctx.enter_context(nc.psum_tensor("ps", [P, 8, 512], F32))

        s_held = sem("held")

        def hold(eng):
            eng.sem_inc(s_held, 1)

        def bc(v, shape):
            return v.broadcast_to(shape)

        ld = sem("loads")
        loads = []

        def col(v):
            return v.rearrange("(a b) -> a b", b=1)

        def row(v):
            return v.rearrange("(a b) -> a b", a=1)

        def by_edge(v, lo, n):
            return v[lo:lo + n * CE].rearrange("(c p j) -> p c j", p=P, j=TPC)

        s_z = sem("zeroed")
        with nc.Block() as block:
            W1, U1 = a["L0_gnn_msg_W1"], a["L0_gnn_upd_W1"]
            loads += [
                (X[:, 0:FULL, :], a["x"][0:FULL * P].rearrange("(t p) d -> p t d", p=P)),
                (X[0:TAIL, FULL, :], a["x"][FULL * P:N]),
                (w_in[0:D, 0:D], W1[0:D]), (w_in[0:D, D:2 * D], W1[D:2 * D]), (w_edge[:], W1[2 * D:3 * D]),
                (w_in[0:D, 2 * D:3 * D], U1[D:2 * D]), (w_upd1[:], U1[0:D]),
                (w_in[D:D + 1, D:2 * D], row(a["L0_gnn_msg_b1"])), (w_in[D:D + 1, 2 * D:3 * D], row(a["L0_gnn_upd_b1"])),
                (w_msg2[0:D], a["L0_gnn_msg_W2"]), (w_msg2[D:D + 1], row(a["L0_gnn_msg_b2"])),
                (w_upd2[0:D], a["L0_gnn_upd_W2"]), (w_upd2[D:D + 1], row(a["L0_gnn_upd_b2"])),
                (w_att[0:D], a["L1_gnn_W"]), (w_att[D:D + 1], row(a["L1_gnn_b"])),
                (w_r1[0:D], a["L2_gnn_W1_r"]), (w_r1[D:D + 1], row(a["L2_gnn_b1_l"])), (w_l1[:], a["L2_gnn_W1_l"]),
                (w_r2[0:D], a["L2_gnn_W2_r"]), (w_r2[D:D + 1], row(a["L2_gnn_b2_l"])), (w_l2[:], a["L2_gnn_W2_l"]),
                (w_lin[:], a["L3_gnn_lin_w"]), (w_own[D:D + 1, 0:D], row(a["L3_gnn_lin_b"])),
                (w_own[0:D, D:D + 1], a["L3_gnn_attn_w"][0:D]), (w_own[0:D, D + 1:D + 2], a["L3_gnn_attn_w"][D:2 * D]),
                (coef[:, 0:2], bc(row(a["L1_gnn_deg_coeff"]), [P, 2])),
                (coef[:, 2:5], bc(row(a["L1_gnn_coeff_param"]), [P, 3])),
                (coef[:, 5:6], bc(row(a["L1_gnn_scale_param"]), [P, 1])),
            ]
            ints = acc[:, 0:2 * C * TPC].bitcast(I32).rearrange("p (k c j) -> p k c j", k=2, j=TPC)
            dsti = ints[:, 0]
            ew2 = acc[:, 2 * C * TPC:3 * C * TPC].rearrange("p (c j) -> p c j", j=TPC)
            for t, v in ((srci, a["src"]), (dsti, a["dst"]), (ewt, a["edge_weight"]), (ew2, a["edge_weight_n2"])):
                loads.append((t[:, 0:C - 1, :], by_edge(v, 0, C - 1)))
                loads.append((t[:, C - 1:C, :], by_edge(v, E - CE, 1)))

            @block.sync
            def _(sp):
                sp.wait_ge(s_z, 3)
                with nc.allow_non_contiguous_dma("columns of small weights"):
                    for dst, src in loads:
                        sp.dma_start(dst, src).then_inc(ld, 16)
                sp.wait_ge(ld, 16 * len(loads))

            s_i = sem("iotas")

            @block.gpsimd
            def _(pool):
                pool.memset(ident[:], 0.0).then_inc(s_i, 1)
                pool.memset(lower[:], 1.0).then_inc(s_i, 1)
                pool.iota(iota_f[:], [[1, P]], base=0, channel_multiplier=0, allow_small_or_imprecise_dtypes=True).then_inc(s_i, 1)
                pool.iota(trash[:], [[1, 1]], base=N, channel_multiplier=1, allow_small_or_imprecise_dtypes=True).then_inc(s_i, 1)
                pool.wait_ge(s_i, 4)
                pool.affine_select(out=ident[:], in_=ident[:], compare_op=ALU.not_equal, fill=1.0, base=0,
                                   pattern=[[-1, P]], channel_multiplier=1).then_inc(s_i, 1)
                pool.affine_select(out=lower[:], in_=lower[:], compare_op=ALU.is_gt, fill=0.0, base=0,
                                   pattern=[[-1, P]], channel_multiplier=1).then_inc(s_i, 1)
                pool.wait_ge(s_i, 6)

            @block.vector
            def _(dve):
                dve.memset(X[:, FULL:NT, :], 0.0).then_inc(s_z, 1)
                dve.memset(w_in[D:D + 1, 0:D], 0.0).then_inc(s_z, 1)
                dve.memset(w_own[D:D + 1, D:D + 2], 0.0).then_inc(s_z, 1)
                dve.memset(w_hm[:], 0.0).then_inc(s_z, 1)
                dve.memset(w_fold[:, D:D + 1], 0.0).then_inc(s_z, 1)
                dve.wait_ge(s_z, 5)
                dve.memset(w_hm[D:D + 1, D:D + 1], 1.0).then_inc(s_z, 1)
                dve.memset(w_fold[D:D + 1, D:D + 1], 1.0).then_inc(s_z, 1)
                dve.memset(small[:, 0:1], 1.0e-5).then_inc(s_z, 1)
                dve.memset(small[:, 1:2], 1.0).then_inc(s_z, 1)
                dve.memset(small[:, 8:9], -BIG).then_inc(s_z, 1)
                dve.wait_ge(s_z, 10)

        lo_hi = keep[:, 0:2 * C].rearrange("p (k c) -> p k c", k=2)
        loT = keep[:, 2 * C:2 * C + 2 * P].rearrange("p (k q) -> p k q", k=2)
        hi_bc = keep[:, 2 * C + 2 * P:3 * C + 2 * P]
        lim = keep[:, 1024:1024 + NT]
        srcf = acc[:, 3 * C * TPC:4 * C * TPC].rearrange("p (c j) -> p c j", j=TPC)
        sp_t = keep[:, 2048:2048 + C * TPC].rearrange("p (c j) -> p c j", j=TPC)
        c_v, c_a, c_p = sem("setup_dve"), sem("setup_act"), sem("setup_pe")
        with nc.Block() as block:
            @block.vector
            def _(dve):
                dve.tensor_copy(dstf[:], dsti).then_inc(c_v, 1)
                dve.tensor_copy(srcf[:], srci[:]).then_inc(c_v, 1)
                dve.wait_ge(c_v, 2)
                dve.tensor_reduce(lo_hi[:, 0, :], dstf[:], AX, ALU.min).then_inc(c_v, 1)
                dve.tensor_reduce(lo_hi[:, 1, :], dstf[:], AX, ALU.max).then_inc(c_v, 1)
                dve.tensor_scalar(ew2, ew2, coef[:, 0:1], coef[:, 1:2], ALU.mult, ALU.add).then_inc(c_v, 1)
                dve.wait_ge(c_v, 5)
                dve.scalar_tensor_tensor(sp_t, ew2, -1.0, ew2, ALU.mult, ALU.min).then_inc(c_v, 1)
                dve.tensor_copy(coef[:, 6:7], coef[:, 5:6]).then_inc(c_v, 1)
                dve.wait_ge(c_v, 7)
                dve.scalar_tensor_tensor(coef[:, 7:8], coef[:, 6:7], -1.0, coef[:, 6:7], ALU.mult, ALU.min).then_inc(c_v, 1)
                dve.tensor_reduce(coef[:, 8:9], coef[:, 2:5], AX, ALU.max).then_inc(c_v, 1)
                dve.wait_ge(c_v, 9)
                dve.tensor_scalar(coef[:, 2:5], coef[:, 2:5], coef[:, 8:9], None, ALU.subtract).then_inc(c_v, 1)
                dve.wait_ge(c_a, 4)
                dve.scalar_tensor_tensor(ew2, ew2, 0.0, sp_t, ALU.max, ALU.add).then_inc(c_v, 1)
                dve.scalar_tensor_tensor(coef[:, 6:7], coef[:, 6:7], 0.0, coef[:, 7:8], ALU.max, ALU.add).then_inc(c_v, 1)
                dve.tensor_reduce(coef[:, 8:9], coef[:, 10:13], AX, ALU.add).then_inc(c_v, 1)
                dve.wait_ge(c_v, 13)
                dve.reciprocal(coef[:, 9:10], coef[:, 8:9]).then_inc(c_v, 1)
                dve.tensor_tensor(ewt[:], ewt[:], ew2, ALU.mult).then_inc(c_v, 1)
                dve.tensor_tensor(sp_t, srcf[:], dstf[:], ALU.not_equal).then_inc(c_v, 1)
                dve.wait_ge(c_v, 16)
                dve.tensor_tensor(ewt[:], ewt[:], sp_t, ALU.mult).then_inc(c_v, 1)
                dve.tensor_scalar(coef[:, 10:13], coef[:, 10:13], coef[:, 9:10], coef[:, 6:7], ALU.mult, ALU.mult).then_inc(c_v, 1)
                dve.wait_ge(c_v, 18)
                dve.memset(ewt[0:DUP, C - 1, :], 0.0).then_inc(c_v, 1)
                dve.memset(dstf[0:DUP, C - 1, :], -4.0 * P).then_inc(c_v, 1)
                dve.wait_ge(c_p, 1)
                for k in range(4):
                    dve.tensor_reduce(small[0:HALF, 2 + k:3 + k], ps[0:HALF, k, 0:P], AX,
                                      (ALU.min, ALU.max)[k // 2]).then_inc(c_v, 1)
                dve.tensor_copy(w_msg2T[:], ps[0:D, 4, 0:D + 1]).then_inc(c_v, 1)
                dve.tensor_copy(w_own[0:D, 0:D], ps[0:D, 5, 0:D]).then_inc(c_v, 1)
                dve.tensor_copy(w_hm[0:D, 0:D], ps[0:D, 6, 0:D]).then_inc(c_v, 1)
                dve.wait_ge(c_p, 2)
                for k in range(4):
                    dst = (base_bc[:], hi_bc)[k // 2]
                    dve.tensor_copy(dst[:, (k % 2) * HALF:(k % 2 + 1) * HALF], ps[:, k, 0:HALF]).then_inc(c_v, 1)
                dve.tensor_copy(w_fold[:, 0:D], ps[0:D + 1, 7, 0:D]).then_inc(c_v, 1)
                dve.wait_ge(c_v, 32)
                dve.tensor_tensor(hi_bc, hi_bc, base_bc[:], ALU.subtract).then_inc(c_v, 1)
                dve.tensor_copy(base0[:], base_bc[:])
                dve.tensor_copy(base_i[:], base_bc[0:1, :]).then_inc(c_v, 1)
                dve.wait_ge(c_v, 34)
                dve.tensor_reduce(small[:, 6:7], hi_bc, AX, ALU.max).then_inc(c_v, 1)
                dve.tensor_scalar(lim, iota_f[:, 0:NT], float(P), None, ALU.mult).then_inc(c_v, 1)
                dve.wait_ge(c_v, 36)
                dve.tensor_scalar(lim, lim, small[:, 6:7], None, ALU.is_le).then_inc(c_v, 1)
                dve.wait_ge(c_v, 37)
                dve.tensor_reduce(small[:, 7:8], lim, AX, ALU.add).then_inc(c_v, 1)
                dve.wait_ge(c_v, 38)
                dve.tensor_copy(rounds_i[:], small[0:1, 7:8]).then_inc(c_v, 1)
                dve.wait_ge(c_v, 39)

            @block.scalar
            def _(act):
                act.wait_ge(c_v, 10)
                act.activation(coef[:, 10:13], coef[:, 2:5], ACT.Exp).then_inc(c_a, 1)
                act.activation(sp_t, sp_t, ACT.Exp).then_inc(c_a, 1)
                act.activation(coef[:, 7:8], coef[:, 7:8], ACT.Exp).then_inc(c_a, 1)
                act.wait_ge(c_a, 3)
                act.activation(sp_t, sp_t, ACT.Ln, bias=small[:, 1:2])
                act.activation(coef[:, 7:8], coef[:, 7:8], ACT.Ln, bias=small[:, 1:2]).then_inc(c_a, 1)

            @block.tensor
            def _(pe):
                pe.wait_ge(c_v, 4)
                for k in range(4):
                    pe.transpose(ps[0:HALF, k, 0:P], lo_hi[:, k // 2, (k % 2) * HALF:(k % 2 + 1) * HALF], ident[:])
                pe.transpose(ps[0:D, 4, 0:D + 1], w_msg2[:], ident[0:D + 1, 0:D + 1])
                pe.transpose(ps[0:D, 5, 0:D], w_lin[:, 0:D], ident[0:D, 0:D])
                pe.transpose(ps[0:D, 6, 0:D], w_lin[:, D:2 * D], ident[0:D, 0:D]).then_inc(c_p, 1)
                pe.wait_ge(c_v, 27)
                for k in range(4):
                    pe.matmul(ps[:, k, 0:HALF], bc(small[0:HALF, 2 + k:3 + k], [HALF, P]), ident[0:HALF, 0:HALF],
                              start=True, stop=True)
                pe.matmul(ps[0:D + 1, 7, 0:D], w_msg2T[:], w_upd1[:], start=True, stop=True).then_inc(c_p, 1)

        V, A, T = Progress(sem("node_dve")), Progress(sem("node_act")), Progress(sem("node_pe"))
        s_ones = sem("ones_row")
        n_ones = [0]
        in_sem = [sem(f"prop_in{k}") for k in range(NPROP)]
        out_sem = [sem(f"rows_out{k}") for k in range(2)]
        outs = [0, 0]

        keepN = keep[:].rearrange("p (t d) -> p t d", d=D)
        NB = GT * P // 512
        psT = ps[0:D, 0:NB, :].rearrange("p b q -> p (b q)")
        SPAN = 66
        PB = 7
        parts = [(NB + b, PB * b, min(PB, GT - PB * b)) for b in range(-(-GT // PB))]

        def tiles_of(b, n, lo, hi):
            return ps[:, b, 0:n * SPAN].rearrange("p (t m) -> p t m", m=SPAN)[:, :, lo:hi]

        def each(v, n=GT):
            return v.rearrange("p (t o) -> p t o", o=1).broadcast_to([P, n, D])

        def one(v):
            return v.rearrange("p (t o) -> p t o", o=1)

        def node_rows(table, g):
            return table[bass.ds(g * (GT * P), GT * P), :].rearrange("(t p) d -> p t d", p=P)

        def products(pe, lhsT, k, w):
            m = w.shape[1]
            for b, t0, n in parts:
                for t in range(n):
                    lo = (t0 + t) * P
                    ins = pe.matmul(ps[:, b, t * SPAN:t * SPAN + m], lhsT[0:k, lo:lo + P], w, start=True, stop=True)
            return ins

        def phase(name, take, dve_steps, act_steps, pe_steps, rows):
            V.begin(dve_steps), A.begin(act_steps), T.begin(pe_steps)
            with ExitStack() as scratch:
                def tmp(n, shape):
                    return scratch.enter_context(nc.sbuf_tensor(f"{name}_{n}", shape, F32))

                xc, hN = tmp("xc", [P, GT, D]), tmp("hN", [P, GT, D + 2])
                hT, accS = tmp("hT", [D + 1, GT * P]), tmp("accS", [D + 1, GT * P])
                st = tmp("st", [P, 6, GT])
                late = [tmp("late0", [P, GT, D]), tmp("late1", [P, GT, D])] if take == "prop" else []
                src_of = {"hN": hN, "xc": xc}
                block = scratch.enter_context(nc.Block())
                n_ones[0] += 1

                def done(ins, who, step):
                    assert step in who.steps
                    ins.then_inc(who.sem, 1)

                def after(eng, who, step, g):
                    eng.wait_ge(who.sem, who.at(step, g))

                @block.sync
                def _(sp):
                    with sp.Fori(0, NG) as g:
                        if take == "prop":
                            after(sp, V, "own", g - 1)
                            hold(sp)
                            for k, t in enumerate([xc[:], hN[:, :, 0:D], late[0][:], late[1][:]]):
                                sp.dma_start(t, node_rows(props[k], g)).then_inc(in_sem[k], 16)
                        for k, (table, buf, cols, who, step) in enumerate(rows):
                            after(sp, who, step, g)
                            hold(sp)
                            with nc.allow_non_contiguous_dma("a column of scores"):
                                sp.dma_start(node_rows(table, g), src_of[buf][:, :, 0:cols]).then_inc(out_sem[k], 16)
                        for k in range(len(rows)):
                            sp.wait_ge(out_sem[k], outs[k] + g * 16 + 16)
                            hold(sp)

                @block.vector
                def _(dve):
                    dve.memset(hT[D:D + 1, :], 1.0).then_inc(s_ones, 1)
                    with dve.Fori(0, NG) as g:
                        xg = X[:, bass.ds(g * GT, GT), :]
                        kg = keepN[:, bass.ds(g * GT, GT), :]
                        dg = rdeg[:, bass.ds(g * GT, GT)]

                        def own_part(dst, t0, n):
                            return dst[:, bass.ds(g * GT + t0, n), :]

                        if take == "msg":
                            after(dve, T, "fold", g)
                            for b, t0, n in parts:
                                dve.tensor_scalar(one(rdeg[:, bass.ds(g * GT + t0, n)]), tiles_of(b, n, D, D + 1), 1.0, None, ALU.max)
                                ins = dve.tensor_tensor(xc[:, t0:t0 + n, :], tiles_of(b, n, 0, D), own_part(keepN, t0, n), ALU.add)
                            done(ins, V, "deg")
                            after(dve, V, "deg", g)
                            done(dve.tensor_scalar(hN[:, :, 0:D], xc[:], 0.0, None, ALU.max), V, "z")
                            done(dve.reciprocal(dg, dg), V, "rdeg")
                            after(dve, T, "upd", g)
                            for b, t0, n in parts:
                                ins = dve.tensor_tensor(own_part(X, t0, n), own_part(X, t0, n), tiles_of(b, n, 0, D), ALU.add)
                            done(ins, V, "x")
                        if take == "prop":
                            for k, t in enumerate([xc[:], hN[:, :, 0:D], late[0][:], late[1][:]]):
                                dve.wait_ge(in_sem[k], g * 16 + 16)
                                if k:
                                    after(dve, V, f"p{k - 1}", g)
                                done(dve.tensor_tensor(xg, xg, t, ALU.add), V, f"p{k}" if k < 3 else "x")
                        if take in ("sage1", "sage2"):
                            after(dve, T, "mean", g)
                            for b, t0, n in parts:
                                ins = dve.tensor_tensor(xc[:, t0:t0 + n, :], tiles_of(b, n, 0, D),
                                                        each(rdeg[:, bass.ds(g * GT + t0, n)], n), ALU.mult)
                            done(ins, V, "scaled")
                            after(dve, V, "scaled", g)
                            done(dve.tensor_tensor(xc[:], xc[:], kg, ALU.add), V, "pre")
                            after(dve, V, "pre", g)
                            if take == "sage1":
                                done(dve.tensor_scalar(hN[:, :, 0:D], xc[:], 0.0, None, ALU.max), V, "h")
                            else:
                                done(dve.scalar_tensor_tensor(xg, xc[:], 0.0, xg, ALU.max, ALU.add), V, "x")
                        if take == "soft":
                            after(dve, T, "mean", g)
                            for b, t0, n in parts:
                                ins = dve.tensor_scalar(one(st[:, 0, t0:t0 + n]), tiles_of(b, n, D, D + 1), 1.0e-30, None, ALU.max)
                            done(ins, V, "den")
                            after(dve, V, "den", g)
                            done(dve.reciprocal(st[:, 1, :], st[:, 0, :]), V, "rden")
                            after(dve, V, "rden", g)
                            for b, t0, n in parts:
                                ins = dve.tensor_tensor(xc[:, t0:t0 + n, :], tiles_of(b, n, 0, D), each(st[:, 1, t0:t0 + n], n), ALU.mult)
                            done(ins, V, "scaled")
                            after(dve, V, "scaled", g)
                            done(dve.tensor_tensor(xc[:], xc[:], kg, ALU.add), V, "pre")
                            after(dve, V, "pre", g)
                            done(dve.scalar_tensor_tensor(xg, xc[:], 0.0, xg, ALU.max, ALU.add), V, "x")
                        if "rstd" in V.steps:
                            if take:
                                after(dve, V, "x", g)
                                hold(dve)
                            done(dve.tensor_reduce(st[:, 0, :], xg, AX, ALU.add), V, "sum")
                            after(dve, V, "sum", g)
                            done(dve.tensor_scalar(st[:, 1, :], st[:, 0, :], 1.0 / D, None, ALU.mult), V, "avg")
                            after(dve, V, "avg", g)
                            done(dve.tensor_tensor(xc[:], xg, each(st[:, 1, :]), ALU.subtract), V, "xc")
                            after(dve, A, "square", g)
                            done(dve.tensor_reduce(st[:, 2, :], hN[:, :, 0:D], AX, ALU.add), V, "var")
                            after(dve, A, "std", g)
                            done(dve.reciprocal(st[:, 4, :], st[:, 3, :]), V, "rstd")
                            after(dve, V, "rstd", g)
                            done(dve.scalar_tensor_tensor(hN[:, :, 0:D], xc[:], 0.0, each(st[:, 4, :]), ALU.max, ALU.mult), V, "h")
                        if take is None:
                            after(dve, T, "own", g)
                            hold(dve)
                            for b, t0, n in parts:
                                ins = dve.tensor_copy(own_part(keepN, t0, n), tiles_of(b, n, 0, D))
                            done(ins, V, "own")
                            after(dve, T, "dst", g)
                            for b, t0, n in parts:
                                ins = dve.tensor_copy(xc[:, t0:t0 + n, :], tiles_of(b, n, 0, D))
                            done(ins, V, "dst_row")
                        if take == "msg":
                            after(dve, T, "wh", g)
                            for b, t0, n in parts:
                                ins = dve.tensor_copy(xc[:, t0:t0 + n, :], tiles_of(b, n, 0, D))
                            done(ins, V, "wh")
                            after(dve, V, "wh", g)
                            done(dve.scalar_tensor_tensor(xg, xc[:], coef[:, 12:13], xg, ALU.mult, ALU.add), V, "x_wh")
                            after(dve, A, "wh_square", g)
                            done(dve.tensor_reduce(st[:, 2, :], hN[:, :, 0:D], AX, ALU.add), V, "norm2")
                            after(dve, A, "norm", g)
                            done(dve.tensor_copy(hN[:, :, D:D + 1], one(st[:, 3, :])), V, "norm_col")
                            done(dve.tensor_copy(hN[:, :, 0:D], xc[:]), V, "row")
                        if take in ("prop", "sage1", "sage2"):
                            after(dve, T, "own", g)
                            hold(dve)
                            for b, t0, n in parts:
                                ins = dve.tensor_copy(own_part(keepN, t0, n), tiles_of(b, n, 0, D))
                            done(ins, V, "own")
                        if take == "sage2":
                            for b, t0, n in parts:
                                ins = dve.tensor_copy(hN[:, t0:t0 + n, D + 1:D + 2], tiles_of(b, n, D, D + 1))
                            done(ins, V, "score")
                            for b, t0, n in parts:
                                ins = dve.tensor_copy(xc[:, t0:t0 + n, 0:1], tiles_of(b, n, D + 1, D + 2))
                            done(ins, V, "dst_score")
                            done(dve.memset(hN[:, :, D:D + 1], 1.0), V, "row")
                        for k in range(len(rows)):
                            dve.wait_ge(out_sem[k], outs[k] + g * 16 + 16)

                @block.scalar
                def _(act):
                    with act.Fori(0, NG) as g:
                        if "sums" in A.steps:
                            done(act.activation(accS[:], acc[0:D + 1, bass.ds(g * (GT * P), GT * P)], ACT.Copy), A, "sums")
                        if take == "msg":
                            after(act, T, "z_turned", g)
                            act.wait_ge(s_ones, n_ones[0])
                            done(act.activation(hT[0:D, :], psT, ACT.Copy), A, "z")
                        if "std" in A.steps:
                            after(act, V, "xc", g)
                            done(act.activation(hN[:, :, 0:D], xc[:], ACT.Square), A, "square")
                            after(act, V, "var", g)
                            done(act.activation(st[:, 3, :], st[:, 2, :], ACT.Sqrt, bias=small[:, 0:1], scale=1.0 / D), A, "std")
                        if "hT" in A.steps:
                            after(act, T, "turned", g)
                            done(act.activation(hT[0:D, :], psT, ACT.Copy), A, "hT")
                        if take is None:
                            after(act, T, "src", g)
                            for b, t0, n in parts:
                                ins = act.activation(hN[:, t0:t0 + n, 0:D], tiles_of(b, n, 0, D), ACT.Copy)
                            done(ins, A, "src_row")
                            after(act, T, "dst", g)
                        if take == "msg":
                            after(act, V, "wh", g)
                            done(act.activation(hN[:, :, 0:D], xc[:], ACT.Square), A, "wh_square")
                            after(act, V, "norm2", g)
                            done(act.activation(st[:, 3, :], st[:, 2, :], ACT.Sqrt), A, "norm")
                        if take in ("prop", "sage1", "sage2"):
                            after(act, T, "own", g)
                        if take == "soft":
                            after(act, T, "mean", g)

                @block.tensor
                def _(pe):
                    with pe.Fori(0, NG) as g:
                        if take == "msg":
                            after(pe, A, "sums", g)
                            done(products(pe, accS, D + 1, w_fold[:]), T, "fold")
                            after(pe, V, "z", g)
                            hold(pe)
                            for t in range(GT):
                                ins = pe.transpose(psT[:, t * P:(t + 1) * P], hN[:, t, 0:D], ident[:])
                            done(ins, T, "z_turned")
                            after(pe, A, "z", g)
                            done(products(pe, hT, D + 1, w_upd2[:]), T, "upd")
                        if take in ("sage1", "sage2", "soft"):
                            after(pe, A, "sums", g)
                            w = {"sage1": w_l1, "sage2": w_l2, "soft": w_hm}[take]
                            done(products(pe, accS, w.shape[0], w[:]), T, "mean")
                        if "turned" in T.steps:
                            after(pe, V, "h", g)
                            hold(pe)
                            for t in range(GT):
                                ins = pe.transpose(psT[:, t * P:(t + 1) * P], hN[:, t, 0:D], ident[:])
                            done(ins, T, "turned")
                            after(pe, A, "hT", g)
                            pe.wait_ge(s_ones, n_ones[0])
                        if take is None:
                            done(products(pe, hT, D + 1, w_in[:, 2 * D:3 * D]), T, "own")
                            after(pe, V, "own", g)
                            done(products(pe, hT, D + 1, w_in[:, 0:D]), T, "src")
                            after(pe, A, "src_row", g)
                            done(products(pe, hT, D + 1, w_in[:, D:2 * D]), T, "dst")
                            after(pe, V, "dst_row", g)
                        if take == "msg":
                            done(products(pe, hT, D + 1, w_att[:]), T, "wh")
                            after(pe, V, "wh", g)
                        if take in ("prop", "sage1", "sage2"):
                            w = {"prop": w_r1, "sage1": w_r2, "sage2": w_own}[take]
                            done(products(pe, hT, D + 1, w[:]), T, "own")
                            after(pe, V, "dst_score" if take == "sage2" else "own", g)
                        if take == "soft":
                            after(pe, V, "scaled", g)
            for k in range(len(rows)):
                outs[k] += 16 * NG
            for who in (V, A, T):
                who.end(NG)

        LN = " sum avg xc var rstd h"

        s_acc0 = sem("acc_zeroed")
        n_acc0 = [0]
        s_next = sem("next_bases")
        n_next = [0]

        def zero_sums(start_max=False, fill_props=None):
            n_acc0[0] += 1
            with nc.Block() as block:
                @block.vector
                def _(dve):
                    dve.memset(acc[:, 0:NPAD // 2], 0.0)
                    dve.memset(acc[:, NPAD // 2:], 0.0).then_inc(s_acc0, 1)
                    if start_max:
                        dve.wait_ge(s_acc0, n_acc0[0])
                        dve.memset(acc[96:97, :], NEG)

                if fill_props is not None:
                    @block.gpsimd
                    def _(sp):
                        sp.wait_ge(s_acc0, n_acc0[0])
                        for k in range(NPROP):
                            sp.dma_start(props[k].rearrange("(p t) d -> p (t d)", p=P), acc[:, 0:NT * D]).then_inc(fill_props[k], FILL)
                        for k in range(NPROP):
                            sp.wait_ge(fill_props[k], FILL)

        def move_bases(dve, to_start):
            if to_start:
                dve.tensor_copy(base_bc[:], base0[:]).then_inc(s_next, 1)
            else:
                dve.tensor_scalar(base_bc[:], base_bc[:], float(P), float(N), ALU.add, ALU.min).then_inc(s_next, 1)
            dve.drain()
            dve.tensor_copy(base_i[:], base_bc[0:1, :]).then_inc(s_next, 1)
            dve.drain()

        def edge_pass(name, stages, src_table, cols, bufs, programs, rows_user, oh_user="sums", win_user="pre",
                      last_stage="acc", win_table=None, wcols=0, edges=False, pool=None, views={}):
            with ExitStack() as scope:
                S = {n: sem(f"{name}_{n}") for n in stages.split()}
                gathered = [sem(f"{name}_gathered{k}") for k in range(U)]
                loaded = [sem(f"{name}_loaded{k}") for k in range(2)]
                s_const = sem(f"{name}_constants")

                def buf(n, shape, dt=F32, k=2):
                    return [scope.enter_context(nc.sbuf_tensor(f"{name}_{n}{i}", shape, dt)) for i in range(k)]

                B = {"G": buf("G", [P, TPC, cols], k=U), "idx": buf("idx", [P, TPC], I32, k=U),
                     "OH": buf("OH", [P, TPC, P], k=U), "drel": buf("drel", [P, TPC])}
                if win_table is not None:
                    B["win"], B["OHT"] = buf("win", [P, wcols]), buf("OHT", [P, TPC, P])
                if edges:
                    B["edge"] = buf("edge", [P, TPC, D])
                for n, shape, dt, k in bufs:
                    B[n] = buf(n, shape, dt, k)
                B.update(views)
                load_inc = 16 * ((win_table is not None) + edges)
                with nc.Block() as block:
                    @block.vector
                    def _(dve):
                        for s in S.values():
                            dve.sem_inc(s, U)
                        k = 0
                        if "msg" in B:
                            for m in B["msg"]:
                                dve.memset(m[:, :, D:D + 1], 1.0).then_inc(s_const, 1)
                                k += 1
                        if k:
                            dve.wait_ge(s_const, k)
                rounds = nc.values_load(rounds_i[0:1, 0:1], min_val=1, max_val=NT)
                with nc.Fori(0, rounds) as r:

                    def at(c, back=0):
                        return r * C + (c + 1 + U - back)

                    def chunks(eng, *stages):
                        def iteration(i, k, lo, hi):
                            for lag, body in stages:
                                s = k - lag
                                if lo <= s < hi:
                                    body((i * U) + s, s % U, r * (C // U) + (i + (s // U + 1)), isinstance(i, int) and i * U + s == C - 1)

                        for k in range(U):
                            iteration(0, k, 0, C)
                        with eng.Fori(1, C // U - 1) as i:
                            for k in range(U):
                                iteration(i, k, -U, C)
                        for k in range(U + max(lag for lag, _ in stages)):
                            iteration(C // U - 1, k, -U, U)

                    def wait_gather(eng, h, turn):
                        eng.wait_ge(gathered[h], turn * (16 * TPC))

                    def wait_loads(eng, h, turn):
                        eng.wait_ge(loaded[h % 2], turn * (U // 2 * load_inc) + (h // 2 + 1 - U // 2) * load_inc)

                    K = dict(S=S, B=B, at=at, rows_user=rows_user, oh_user=oh_user, wait_gather=wait_gather, wait_loads=wait_loads, chunks=chunks, r=r)

                    def run(eng, key):
                        chunks(eng, *[(lag, lambda c, h, turn, last, f=f: f(K, eng, c, h, turn)) for lag, f in programs[key]])

                    def gather(eng, c, h, turn):
                        eng.wait_ge(S[rows_user], at(c, U))
                        eng.wait_ge(S["idx"], at(c))
                        hold(eng)
                        for j in range(TPC):
                            gather_tile(eng, h, j)

                    def gather_tile(eng, h, j):
                        eng.indirect_dma_start(B["G"][h][:, j, :], None, src_table, bass.IndirectOffsetOnAxis(
                            ap=B["idx"][h][:, j:j + 1], axis=0)).then_inc(gathered[h], 16)

                    with nc.Block() as block:
                        if load_inc:
                            @block.sync
                            def _(sp):
                                def body(c, h, turn, last):
                                    b = h % 2
                                    if win_table is not None:
                                        first = sp.value_load(base_i[0:1, bass.ds(c, 1)], min_val=0, max_val=N)
                                        sp.wait_ge(S[win_user], at(c, 2))
                                        hold(sp)
                                        with nc.allow_non_contiguous_dma("a window's column"):
                                            sp.dma_start(B["win"][b][:], win_table[bass.ds(first, P), 0:wcols]).then_inc(loaded[b], 16)
                                    if edges:
                                        sp.wait_ge(S["edge_turned"], at(c, 2))
                                        hold(sp)
                                        lo = E - CE if last else c * CE
                                        rows = a["edge_attr_64"][bass.ds(lo, CE), :].rearrange("(p j) d -> p j d", j=TPC)
                                        sp.dma_start(B["edge"][b][:], rows).then_inc(loaded[b], 16)
                                chunks(sp, (0, body))

                        @block.gpsimd
                        def _(eng):
                            if pool is None:
                                chunks(eng, (0, lambda c, h, turn, last: gather(eng, c, h, turn)))
                            else:
                                pool(K, eng, gather_tile)

                        @block.vector
                        def _(dve):
                            run(dve, "dve")
                            dve.wait_ge(S[last_stage], at(C - 1))
                            move_bases(dve, False)

                        @block.scalar
                        def _(act):
                            run(act, "act")

                        @block.tensor
                        def _(pe):
                            run(pe, "pe")
                with nc.Block() as block:
                    @block.vector
                    def _(dve):
                        move_bases(dve, True)

        def cols_of(t, c):
            return t[:, bass.ds(c, 1), :].rearrange("p o j -> p (o j)")

        def wide(v, m):
            return v.rearrange("p (j o) -> p j o", o=1).broadcast_to([P, TPC, m])

        iota_all = iota_f[:].rearrange("p (o n) -> p o n", o=1).broadcast_to([P, TPC, P])
        banks = lambda b: ps[:, b:b + 2, :].rearrange("p b q -> p (b q)").rearrange("p (j n) -> p j n", n=P)

        def one_hot(K, dve, c, h, turn):
            S, B, at, b = K["S"], K["B"], K["at"], h % 2
            dve.tensor_scalar(B["drel"][b][:], cols_of(dstf, c), base_bc[:, bass.ds(c, 1)], None, ALU.subtract).then_inc(S["drel"], 1)
            dve.wait_ge(S[K["oh_user"]], at(c, U))
            dve.wait_ge(S["drel"], at(c))
            dve.tensor_tensor(B["OH"][h][:], iota_all, wide(B["drel"][b][:], P), ALU.is_equal).then_inc(S["oh"], 1)

        def copy_indices(K, act, c, h, turn):
            S, B, at = K["S"], K["B"], K["at"]
            act.wait_ge(S[K["rows_user"]], at(c, U))
            hold(act)
            act.activation(B["idx"][h][:], cols_of(srci, c), ACT.Copy).then_inc(S["idx"], 1)

        def turn_one_hot(K, pe, c, h, turn):
            S, B, at, b = K["S"], K["B"], K["at"], h % 2
            pe.wait_ge(S["oh"], at(c))
            pe.wait_ge(S["oht"], at(c, 1))
            for j in range(TPC):
                ins = pe.transpose(banks(0)[:, j, :], B["OH"][h][:, j, :], ident[:])
            ins.then_inc(S["oh_turned"], 1)

        def take_one_hot(K, act, c, h, turn, user):
            S, B, at, b = K["S"], K["B"], K["at"], h % 2
            act.wait_ge(S["oh_turned"], at(c))
            act.wait_ge(S[user], at(c, 2))
            act.activation(B["OHT"][b][:], banks(0), ACT.Copy).then_inc(S["oht"], 1)

        def sum_by_node(K, pe, rows, m, c, h):
            S, B, at = K["S"], K["B"], K["at"]
            pe.wait_ge(S["acc"], at(c, 2))
            for j in range(TPC):
                ins = pe.matmul(ps[0:m, 6 + h % 2, 0:P], rows(j), B["OH"][h][:, j, :], start=(j == 0), stop=(j == TPC - 1))
            ins.then_inc(S["sums"], 1)

        def add_sums(K, dve, m, c, h):
            S, at = K["S"], K["at"]
            first = dve.value_load(base_i[0:1, bass.ds(c, 1)], min_val=0, max_val=N)
            dve.wait_ge(S["sums"], at(c))
            dve.wait_ge(S["acc"], at(c, 1))
            w = acc[0:m, bass.ds(first, P)]
            dve.tensor_tensor(w, w, ps[0:m, 6 + h % 2, 0:P], ALU.add).then_inc(S["acc"], 1)

        def msg_dve(K, dve, c, h, turn):
            S, B, at, b = K["S"], K["B"], K["at"], h % 2
            dve.wait_ge(S["pre"], at(c))
            dve.wait_ge(S["sums"], at(c, 2))
            K["wait_gather"](dve, h, turn)
            dve.tensor_tensor(B["msg"][b][:, :, 0:D], ps[:, 4 + b, :].rearrange("p (j d) -> p j d", d=D), B["G"][h][:], ALU.add).then_inc(S["summed"], 1)

        def msg_dve_add(K, dve, c, h, turn):
            add_sums(K, dve, D + 1, c, h)

        def msg_act_prep(K, act, c, h, turn):
            take_one_hot(K, act, c, h, turn, "pre")
            S, B, at, b = K["S"], K["B"], K["at"], h % 2
            act.wait_ge(S["edge_turned"], at(c))
            act.activation(B["edgeT"][b][:], banks(2)[0:D], ACT.Copy).then_inc(S["edgeT"], 1)

        def msg_act(K, act, c, h, turn):
            S, B, at, b = K["S"], K["B"], K["at"], h % 2
            act.wait_ge(S["summed"], at(c))
            act.activation(B["msg"][b][:, :, 0:D], B["msg"][b][:, :, 0:D], ACT.Relu).then_inc(S["msg"], 1)

        def msg_pe_prep(K, pe, c, h, turn):
            S, B, at, b = K["S"], K["B"], K["at"], h % 2
            turn_one_hot(K, pe, c, h, turn)
            K["wait_loads"](pe, h, turn)
            pe.wait_ge(S["edgeT"], at(c, 1))
            hold(pe)
            for j in range(TPC):
                ins = pe.transpose(banks(2)[0:D, j, :], B["edge"][b][:, j, :], ident[:])
            ins.then_inc(S["edge_turned"], 1)

        def msg_pe(K, pe, c, h, turn):
            S, B, at, b = K["S"], K["B"], K["at"], h % 2
            pe.wait_ge(S["edgeT"], at(c))
            pe.wait_ge(S["oht"], at(c))
            pe.wait_ge(S["summed"], at(c, 2))
            for j in range(TPC):
                o = ps[:, 4 + b, j * D:(j + 1) * D]
                pe.matmul(o, B["edgeT"][b][:, j, :], w_edge[:], start=True, stop=False)
                ins = pe.matmul(o, B["OHT"][b][:, j, :], B["win"][b][:], start=False, stop=True)
            ins.then_inc(S["pre"], 1)

        def msg_pe_sum(K, pe, c, h, turn):
            S, B, at, b = K["S"], K["B"], K["at"], h % 2
            pe.wait_ge(S["msg"], at(c))
            sum_by_node(K, pe, lambda j: B["msg"][b][:, j, :], D + 1, c, h)

        def sage_act(K, act, c, h, turn):
            copy_indices(K, act, c, h, turn)

        def sage_pe(K, pe, c, h, turn):
            K["wait_gather"](pe, h, turn)
            pe.wait_ge(K["S"]["oh"], K["at"](c))
            sum_by_node(K, pe, lambda j: K["B"]["G"][h][:, j, :], D, c, h)

        def sage_dve(K, dve, c, h, turn):
            add_sums(K, dve, D, c, h)

        FILL = 16 * TPC // NPROP * U
        s_prop = [sem(f"prop{k}") for k in range(NPROP)]

        def scatters_before(K, c, more=0):
            return (K["r"] * C + c) * (16 * TPC // NPROP) + (FILL + more)

        def wait_scatters(K, eng, c):
            for s in s_prop:
                eng.wait_ge(s, scatters_before(K, c, -16 * TPC // NPROP * (U - 1)))

        def att_pool(K, eng, gather_tile):
            S, B, at = K["S"], K["B"], K["at"]

            def tiles(c, h, gathers, scatters):
                if gathers:
                    c2, h2 = c + 2, (h + 2) % U
                    eng.wait_ge(S[K["rows_user"]], at(c2, U))
                    eng.wait_ge(S["idx"], at(c2))
                if scatters:
                    eng.wait_ge(S["sidx"], at(c))
                    eng.wait_ge(S["out"], at(c))
                hold(eng)
                for j in range(TPC):
                    if gathers:
                        gather_tile(eng, h2, j)
                    if scatters:
                        k = j % NPROP
                        eng.wait_ge(s_prop[k], scatters_before(K, c, 16 * (j // NPROP)))
                        hold(eng)
                        eng.indirect_dma_start(props[k], bass.IndirectOffsetOnAxis(ap=B["sidx"][h][:, j:j + 1], axis=0),
                                               B["out"][h][:, j, :], None, compute_op=ALU.add).then_inc(s_prop[k], 16)

            for h in (-2, -1):
                tiles(h, h, True, False)
            with eng.Fori(0, C // U - 1) as i:
                for h in range(U):
                    tiles(i * U + h, h, True, True)
            for h in range(U):
                tiles(C - U + h, h, h < U - 2, True)
            for s in s_prop:
                eng.wait_ge(s, scatters_before(K, C))

        def att_dve_prep(K, dve, c, h, turn):
            S, B, at, b = K["S"], K["B"], K["at"], h % 2
            dve.wait_ge(S["src_turned"], at(c))
            dve.wait_ge(S["merged"], at(c, 2))
            dve.tensor_tensor(B["SM"][b][:], banks(2), wide(B["srcs"][b][:], P), ALU.is_equal).then_inc(S["sm"], 1)
            dve.wait_ge(S["sm"], at(c))
            dve.tensor_tensor(B["before"][0][:], B["SM"][b][:], lower[:].rearrange("p (o n) -> p o n", o=1).broadcast_to([P, TPC, P]), ALU.mult).then_inc(S["before"], 1)
            dve.tensor_scalar(B["t"][b][:, 0], B["srcs"][b][:], -1.0, trash[:], ALU.mult, ALU.add).then_inc(S["away"], 1)
            dve.wait_ge(S["before"], at(c))
            dve.tensor_reduce(B["t"][b][:, 1], B["before"][0][:], AX, ALU.add).then_inc(S["count"], 1)
            dve.wait_ge(S["count"], at(c))
            dve.wait_ge(S["away"], at(c))
            dve.scalar_tensor_tensor(B["t"][b][:, 2], B["t"][b][:, 1], 0.5, B["t"][b][:, 0], ALU.is_gt, ALU.mult).then_inc(S["shift"], 1)
            dve.wait_ge(S["shift"], at(c))
            wait_scatters(K, dve, c)
            dve.tensor_tensor(B["sidx"][h][:], B["t"][b][:, 2], B["srcs"][b][:], ALU.add).then_inc(S["sidx"], 1)

        def att_dve(K, dve, c, h, turn):
            S, B, at, b = K["S"], K["B"], K["at"], h % 2
            t = B["m"][b]
            G = B["G"][h]
            wc = lambda q, lo, hi: ps[:, 4 + q, 0:4 * (D + 1)].rearrange("p (j d) -> p j d", d=D + 1)[:, :, lo:hi]
            K["wait_gather"](dve, h, turn)
            dve.wait_ge(S["wc"], at(c))
            for q in range(2):
                j = slice(4 * q, 4 * q + 4)
                dve.tensor_tensor(B["prod"][0][:, j, :], G[:, j, 0:D], wc(q, 0, D), ALU.mult)
                ins = dve.tensor_tensor(t[:, 0, j].rearrange("p (j o) -> p j o", o=1), G[:, j, D:D + 1], wc(q, D, D + 1), ALU.mult)
            ins.then_inc(S["dot"], 1)
            dve.wait_ge(S["dot"], at(c))
            dve.tensor_reduce(t[:, 1], B["prod"][0][:], AX, ALU.add)
            dve.tensor_scalar(t[:, 2], t[:, 0], 1.0e-8, None, ALU.max).then_inc(S["a1"], 1)
            dve.wait_ge(S["a1"], at(c))
            dve.reciprocal(t[:, 3], t[:, 2]).then_inc(S["a2"], 1)
            dve.wait_ge(S["a2"], at(c))
            dve.tensor_tensor(t[:, 4], t[:, 1], t[:, 3], ALU.mult).then_inc(S["sim"], 1)
            dve.wait_ge(S["sim"], at(c))
            dve.tensor_scalar(t[:, 5], t[:, 4], 0.0, coef[:, 10:11], ALU.max, ALU.mult)
            dve.tensor_scalar(t[:, 6], t[:, 4], 0.0, coef[:, 11:12], ALU.min, ALU.mult).then_inc(S["a3"], 1)
            dve.wait_ge(S["a3"], at(c))
            dve.tensor_tensor(t[:, 7], t[:, 5], t[:, 6], ALU.add).then_inc(S["a4"], 1)
            dve.wait_ge(S["a4"], at(c))
            dve.tensor_tensor(t[:, 8], t[:, 7], cols_of(ewt, c), ALU.mult).then_inc(S["weight"], 1)
            dve.wait_ge(S["weight"], at(c))
            dve.wait_ge(S["merged"], at(c, 2))
            for q in range(2):
                j = slice(4 * q, 4 * q + 4)
                w = t[:, 8, j].rearrange("p (j o) -> p j o", o=1).broadcast_to([P, 4, D])
                ins = dve.tensor_tensor(B["V"][b][:, j, :], wc(q, 0, D), w, ALU.mult)
            ins.then_inc(S["v"], 1)

        def att_act_prep(K, act, c, h, turn):
            S, B, at, b = K["S"], K["B"], K["at"], h % 2
            act.wait_ge(S["sidx"], at(c, 2))
            hold(act)
            act.activation(B["srcs"][b][:], cols_of(srci, c), ACT.Copy).then_inc(S["srcs"], 1)
            take_one_hot(K, act, c, h, turn, "wc")

        def att_act(K, act, c, h, turn):
            S, B, at, b = K["S"], K["B"], K["at"], h % 2
            act.wait_ge(S["merged"], at(c))
            wait_scatters(K, act, c)
            act.activation(B["out"][h][:], ps[:, 6 + b, :].rearrange("p (j d) -> p j d", d=D), ACT.Copy).then_inc(S["out"], 1)

        def att_pe_prep(K, pe, c, h, turn):
            S, B, at, b = K["S"], K["B"], K["at"], h % 2
            turn_one_hot(K, pe, c, h, turn)
            pe.wait_ge(S["srcs"], at(c))
            pe.wait_ge(S["sm"], at(c, 1))
            for j in range(TPC):
                ins = pe.transpose(banks(2)[:, j, :], B["srcs"][b][:, j:j + 1].broadcast_to([P, P]), ident[:])
            ins.then_inc(S["src_turned"], 1)

        def att_pe(K, pe, c, h, turn):
            S, B, at, b = K["S"], K["B"], K["at"], h % 2
            pe.wait_ge(S["oht"], at(c))
            K["wait_loads"](pe, h, turn)
            pe.wait_ge(S["v"], at(c, 1))
            for j in range(TPC):
                ins = pe.matmul(ps[:, 4 + j // 4, (j % 4) * (D + 1):(j % 4 + 1) * (D + 1)], B["OHT"][b][:, j, :], B["win"][b][:], start=True, stop=True)
            ins.then_inc(S["wc"], 1)

        def att_pe_merge(K, pe, c, h, turn):
            S, B, at, b = K["S"], K["B"], K["at"], h % 2
            pe.wait_ge(S["v"], at(c))
            pe.wait_ge(S["sm"], at(c))
            pe.wait_ge(S["out"], at(c, 2))
            for j in range(TPC):
                ins = pe.matmul(ps[:, 6 + b, j * D:(j + 1) * D], B["SM"][b][:, j, :], B["V"][b][:, j, :], start=True, stop=True)
            ins.then_inc(S["merged"], 1)

        TOP = 96

        def soft_act_prep(K, act, c, h, turn):
            S, B, at, b = K["S"], K["B"], K["at"], h % 2
            act.wait_ge(S["oh_turned"], at(c))
            act.wait_ge(S["top"], at(c, 2))
            act.activation(B["pen"][b][:], banks(0), ACT.Identity, bias=small[:, 8:9], scale=BIG)
            act.wait_ge(S["spread"], at(c, 2))
            act.activation(B["OHT"][b][:], banks(0), ACT.Copy).then_inc(S["oht"], 1)

        def soft_act_ratio(K, act, c, h, turn):
            S, B, at, b = K["S"], K["B"], K["at"], h % 2
            act.wait_ge(S["em"], at(c))
            act.activation(B["Q"][b][:, 0:TOP], B["q"][b][:, 7:8].broadcast_to([P, TOP]), ACT.Exp).then_inc(S["ratio"], 1)

        def soft_act_ex(K, act, c, h, turn):
            S, B, at, b = K["S"], K["B"], K["at"], h % 2
            act.wait_ge(S["e4"], at(c))
            act.activation(B["e"][b][:, 4], B["e"][b][:, 3], ACT.Exp).then_inc(S["ex"], 1)

        def soft_pe_spread(K, pe, c, h, turn):
            S, B, at, b = K["S"], K["B"], K["at"], h % 2
            pe.wait_ge(S["em"], at(c))
            pe.wait_ge(S["oht"], at(c))
            pe.wait_ge(S["e3"], at(c, 1))
            for j in range(TPC):
                ins = pe.matmul(ps[:, 4, 2 * j:2 * j + 2], B["OHT"][b][:, j, :], B["em"][b][:], start=True, stop=True)
            ins.then_inc(S["spread"], 1)

        def soft_pe_scores(K, pe, c, h, turn):
            S, B, at, b = K["S"], K["B"], K["at"], h % 2
            K["wait_gather"](pe, h, turn)
            pe.wait_ge(S["top"], at(c, 1))
            for j in range(TPC):
                pe.transpose(banks(2)[:, j, :], B["G"][h][:, j, D + 1:D + 2].broadcast_to([P, P]), ident[:])
            pe.wait_ge(S["mrow"], at(c))
            pe.wait_ge(S["top_row"], at(c, 1))
            pe.matmul(ps[:, 5, 2 * P:2 * P + 1], B["mrow"][b][:], small[0:1, 1:2], start=True, stop=True).then_inc(S["old"], 1)

        def soft_pe_rows(K, pe, c, h, turn):
            S, B, at, b = K["S"], K["B"], K["at"], h % 2
            pe.wait_ge(S["ratio"], at(c))
            pe.wait_ge(S["scaled"], at(c, 2))
            pe.matmul(ps[0:TOP + 1, 5, b * P:(b + 1) * P], B["Q"][b][:], ident[:], start=True, stop=True).then_inc(S["rows"], 1)

        def soft_pe_sum(K, pe, c, h, turn):
            pe.wait_ge(K["S"]["msg"], K["at"](c))
            sum_by_node(K, pe, lambda j: K["B"]["msg"][h % 2][:, j, :], D + 1, c, h)

        def soft_dve_old(K, dve, c, h, turn):
            S, B, at, b = K["S"], K["B"], K["at"], h % 2
            first = dve.value_load(base_i[0:1, bass.ds(c, 1)], min_val=0, max_val=N)
            dve.wait_ge(S["top_row"], at(c, 1))
            dve.wait_ge(S["old"], at(c, 2))
            hold(dve)
            dve.tensor_copy(B["mrow"][b][:], acc[TOP:TOP + 1, bass.ds(first, P)]).then_inc(S["mrow"], 1)

        def soft_dve_top(K, dve, c, h, turn):
            S, B, at, b = K["S"], K["B"], K["at"], h % 2
            q, em, t_dst = B["q"][b], B["em"][b], B["win"][b]
            dve.wait_ge(S["old"], at(c))
            dve.wait_ge(S["oht"], at(c))
            hold(dve)
            dve.tensor_tensor_reduce(B["junk"][0][:], two_banks(2), B["pen"][b].rearrange("p j n -> p (j n)"), 1.0, NEG, ALU.add, ALU.max,
                                     q[:, 2:3]).then_inc(S["top"], 1)
            dve.tensor_copy(q[:, 0:1], ps[:, 5, 2 * P:2 * P + 1])
            dve.wait_ge(S["top"], at(c))
            dve.tensor_tensor(q[:, 1:2], ps[:, 5, 2 * P:2 * P + 1], q[:, 2:3], ALU.max).then_inc(S["new"], 1)
            K["wait_loads"](dve, h, turn)
            dve.wait_ge(S["new"], at(c))
            dve.wait_ge(S["rows"], at(c, 2))
            dve.tensor_copy(B["Q"][b][:, TOP:TOP + 1], q[:, 1:2])
            dve.tensor_scalar(q[:, 3:5], q[:, 0:2], t_dst[:, 0:1], None, ALU.add).then_inc(S["u"], 1)
            dve.wait_ge(S["u"], at(c))
            dve.scalar_tensor_tensor(q[:, 5:7], q[:, 3:5], 0.01, q[:, 3:5], ALU.mult, ALU.max).then_inc(S["l"], 1)
            dve.wait_ge(S["l"], at(c))
            dve.wait_ge(S["spread"], at(c, 2))
            dve.tensor_tensor(q[:, 7:8], q[:, 5:6], q[:, 6:7], ALU.subtract)
            dve.tensor_copy(em[:, 0:1], t_dst[:, 0:1])
            dve.tensor_copy(em[:, 1:2], q[:, 6:7]).then_inc(S["em"], 1)

        def soft_dve_score(K, dve, c, h, turn):
            S, B, at, b = K["S"], K["B"], K["at"], h % 2
            e, G = B["e"][b], B["G"][h]
            sp2 = ps[:, 4, 0:2 * TPC].rearrange("p (j k) -> p k j", k=2)
            K["wait_gather"](dve, h, turn)
            dve.wait_ge(S["spread"], at(c))
            dve.tensor_tensor(e[:, 0], G[:, :, D + 1], sp2[:, 0], ALU.add).then_inc(S["e1"], 1)
            dve.wait_ge(S["e1"], at(c))
            dve.scalar_tensor_tensor(e[:, 1], e[:, 0], 0.01, e[:, 0], ALU.mult, ALU.max).then_inc(S["e2"], 1)
            dve.wait_ge(S["e2"], at(c))
            dve.tensor_tensor(e[:, 2], e[:, 1], sp2[:, 1], ALU.subtract).then_inc(S["e3"], 1)
            dve.wait_ge(S["e3"], at(c))
            dve.tensor_scalar(e[:, 3], e[:, 2], 0.0, None, ALU.min).then_inc(S["e4"], 1)

        def soft_dve_msg(K, dve, c, h, turn):
            S, B, at, b = K["S"], K["B"], K["at"], h % 2
            dve.wait_ge(S["ex"], at(c))
            dve.wait_ge(S["sums"], at(c, 2))
            dve.tensor_tensor(B["msg"][b][:], B["G"][h][:, :, 0:D + 1], wide(B["e"][b][:, 4], D + 1), ALU.mult).then_inc(S["msg"], 1)

        def soft_dve_add(K, dve, c, h, turn):
            S, B, at, b = K["S"], K["B"], K["at"], h % 2
            first = dve.value_load(base_i[0:1, bass.ds(c, 1)], min_val=0, max_val=N)
            w = acc[0:D + 1, bass.ds(first, P)]
            dve.wait_ge(S["rows"], at(c))
            dve.wait_ge(S["acc"], at(c, 1))
            dve.tensor_tensor(w, w, ps[0:D + 1, 5, b * P:(b + 1) * P], ALU.mult).then_inc(S["scaled"], 1)
            dve.wait_ge(S["sums"], at(c))
            dve.wait_ge(S["scaled"], at(c))
            dve.tensor_tensor(w, w, ps[0:D + 1, 6 + b, 0:P], ALU.add).then_inc(S["acc"], 1)

        def soft_dve_row(K, dve, c, h, turn):
            S, B, at, b = K["S"], K["B"], K["at"], h % 2
            first = dve.value_load(base_i[0:1, bass.ds(c, 1)], min_val=0, max_val=N)
            dve.wait_ge(S["rows"], at(c))
            hold(dve)
            dve.tensor_copy(acc[TOP:TOP + 1, bass.ds(first, P)], ps[TOP:TOP + 1, 5, b * P:(b + 1) * P]).then_inc(S["top_row"], 1)

        two_banks = lambda b: ps[:, b:b + 2, :].rearrange("p b q -> p (b q)")
        zero_sums(fill_props=s_prop)
        phase("enter", None, "sum avg xc var rstd h own dst_row", "square std hT src_row", "turned own src dst",
              [(msg_src, "hN", D, A, "src_row"), (msg_dst, "xc", D, V, "dst_row")])
        edge_pass("msg", "drel oh idx oh_turned oht edge_turned edgeT pre summed msg sums acc", msg_src, D,
                  [("edgeT", [D, TPC, P], F32, 2), ("msg", [P, TPC, D + 1], F32, 2)],
                  {"dve": [(0, one_hot), (2, msg_dve), (3, msg_dve_add)], "act": [(0, copy_indices), (1, msg_act_prep), (2, msg_act)],
                   "pe": [(1, msg_pe_prep), (2, msg_pe), (3, msg_pe_sum)]},
                  rows_user="summed", win_table=msg_dst, wcols=D, edges=True)
        phase("after_msg", "msg", "deg z rdeg x" + LN + " wh x_wh norm2 norm_col row", "sums z square std hT wh_square norm",
              "fold z_turned upd turned wh", [(att, "hN", D + 1, V, "row")])
        edge_pass("att", "drel oh idx oh_turned oht srcs src_turned sm before away count shift sidx wc dot a1 a2 sim a3 a4 weight v merged out",
                  att, D + 1,
                  [("V", [P, TPC, D], F32, 2), ("out", [P, TPC, D], F32, U), ("sidx", [P, TPC], I32, U), ("srcs", [P, TPC], F32, 2),
                   ("t", [P, 3, TPC], F32, 2), ("m", [P, 9, TPC], F32, 2)],
                  {"dve": [(0, one_hot), (2, att_dve), (1, att_dve_prep)], "act": [(0, copy_indices), (1, att_act_prep), (3, att_act)],
                   "pe": [(1, att_pe_prep), (2, att_pe), (3, att_pe_merge)]},
                  rows_user="dot", oh_user="oh_turned", win_user="wc", last_stage="v", win_table=att, wcols=D + 1, pool=att_pool,
                  views={"SM": [acc[:, k * CE:(k + 1) * CE].rearrange("p (j n) -> p j n", n=P) for k in range(2)],
                         "before": [acc[:, 2 * CE:3 * CE].rearrange("p (j n) -> p j n", n=P)],
                         "prod": [acc[:, 3 * CE:3 * CE + TPC * D].rearrange("p (j d) -> p j d", d=D)]})
        phase("after_att", "prop", "p0 p1 p2 x" + LN + " own", "square std hT", "turned own", [(sage1, "hN", D, V, "h")])
        sage = {"dve": [(0, one_hot), (1, sage_dve)], "act": [(0, sage_act)], "pe": [(0, sage_pe)]}
        zero_sums()
        edge_pass("sage1", "drel oh idx sums acc", sage1, D, [], sage, rows_user="sums")
        phase("after_sage1", "sage1", "scaled pre h own", "sums hT", "mean turned own", [(sage2, "hN", D, V, "h")])
        zero_sums()
        edge_pass("sage2", "drel oh idx sums acc", sage2, D, [], sage, rows_user="sums")
        phase("after_sage2", "sage2", "scaled pre x" + LN + " own score dst_score row", "sums square std hT",
              "mean turned own", [(soft, "hN", D + 2, V, "row"), (soft_dst, "xc", 1, V, "dst_score")])
        zero_sums(start_max=True)
        edge_pass("soft", "drel oh idx oh_turned oht mrow old top new u l em ratio spread rows e1 e2 e3 e4 ex msg scaled top_row sums acc",
                  soft, D + 2,
                  [("msg", [P, TPC, D + 1], F32, 2), ("q", [P, 8], F32, 2), ("e", [P, 5, TPC], F32, 2), ("em", [P, 2], F32, 2),
                   ("mrow", [1, P], F32, 2), ("Q", [P, TOP + 1], F32, 2), ("pen", [P, TPC, P], F32, 2), ("junk", [P, CE], F32, 1)],
                  {"dve": [(1, soft_dve_old), (0, one_hot), (2, soft_dve_score), (1, soft_dve_top), (2, soft_dve_msg),
                           (3, soft_dve_add), (1, soft_dve_row)],
                   "act": [(0, copy_indices), (2, soft_act_ex), (0, soft_act_prep), (1, soft_act_ratio)],
                   "pe": [(2, soft_pe_spread), (1, soft_pe_scores), (0, turn_one_hot), (3, soft_pe_sum), (1, soft_pe_rows)]},
                  rows_user="msg", win_user="em", win_table=soft_dst, wcols=1)
        phase("leave", "soft", "den rden scaled pre x", "sums", "mean", [])

        s_out = sem("out")
        with nc.Block() as block:
            @block.sync
            def _(sp):
                sp.dma_start(out[0:FULL * P].rearrange("(t p) d -> p t d", p=P), X[:, 0:FULL, :]).then_inc(s_out, 16)
                sp.dma_start(out[FULL * P:N], X[0:TAIL, FULL, :]).then_inc(s_out, 16)
                sp.wait_ge(s_out, 32)


def kernel(**inputs):
    import numpy as _np
    import concourse.bacc as _bacc
    from concourse import mybir as _mybir
    from concourse.bass_utils import run_bass_kernel_spmd as _run

    nc = _bacc.Bacc("TRN2", target_bir_lowering=False, num_devices=1)
    arrays, aps = {}, {}
    for name, v in inputs.items():
        v = _np.ascontiguousarray(v)
        arrays[name] = v
        aps[name] = nc.dram_tensor(name, v.shape, _mybir.dt.from_np(v.dtype), kind="ExternalInput").ap()
    out = nc.dram_tensor("result", inputs["x"].shape, F32, kind="ExternalOutput").ap()
    gnn_kernel(nc, aps, out)
    r = _run(nc, [arrays], core_ids=[0])
    return r.results[0]["result"]
```

```python
from contextlib import ExitStack

import concourse.bass as bass
from concourse import mybir

P = 128
D = 64
TPC = 8
CE = P * TPC
U = 4
GT = 10
NPROP = 4
NEG = -1.0e30
BIG = 1.0e30
TOP = 96

F32 = mybir.dt.float32
I32 = mybir.dt.int32
ALU = mybir.AluOpType
ACT = mybir.ActivationFunctionType
AX = mybir.AxisListType.X


class Step:

    def __init__(self, sem):
        self.sem, self.before = sem, 0

    def at(self, g):
        return self.before + g + 1


def gnn_kernel(nc, a, out):
    N, E = a["x"].shape[0], a["src"].shape[0]
    C = -(-E // CE)
    NG = -(-(N + P) // (2 * P * GT)) * 2
    NT = NG * GT
    NPAD = NT * P
    FULL, TAIL = N // P, N % P
    HALF = C // 2
    TWICE = C * CE - E
    assert C % U == 0 and HALF <= P and TWICE % TPC == 0 and TAIL and E >= CE and (C - 1) * CE < E
    DUP = TWICE // TPC

    with ExitStack() as ctx:
        def sb(name, shape, dt=F32):
            return ctx.enter_context(nc.sbuf_tensor(name, shape, dt))

        def sem(name):
            return ctx.enter_context(nc.semaphore(name))

        def dram(name, shape):
            return nc.dram_tensor(name, shape, F32, kind="Internal").ap()

        msg_src = dram("msg_src", (NPAD, D))
        msg_dst = dram("msg_dst", (NPAD, D))
        att = dram("att", (NPAD, D + 1))
        sage1 = dram("sage1", (NPAD, D))
        sage2 = dram("sage2", (NPAD, D))
        soft = dram("soft", (NPAD, D + 2))
        soft_dst = dram("soft_dst", (NPAD, 1))
        props = [dram(f"prop{k}", (NPAD, D)) for k in range(NPROP)]

        X = sb("X", [P, NT, D])
        acc = sb("acc", [P, NPAD])
        keep = sb("keep", [P, NT * D])
        dstf = sb("dstf", [P, C, TPC])
        srci = sb("srci", [P, C, TPC], I32)
        ewt = sb("ewt", [P, C, TPC])
        zero = sb("zero", [P, NT // 4 * D])
        base_bc = sb("base_bc", [P, C])
        base0 = sb("base0", [P, C])
        base_i = sb("base_i", [1, C], I32)
        rounds_i = sb("rounds_i", [1, 1], I32)
        ident = sb("ident", [P, P])
        iota_f = sb("iota_f", [P, P])
        lower = sb("lower", [P, P])
        trash = sb("trash", [P, 1])
        small = sb("small", [P, 32])

        w_in = sb("w_in", [D + 1, 3 * D])
        w_edge = sb("w_edge", [D, D])
        w_upd1 = sb("w_upd1", [D, D])
        w_msg2 = sb("w_msg2", [D + 1, D])
        w_msg2T = sb("w_msg2T", [D, D + 1])
        w_fold = sb("w_fold", [D + 1, D + 1])
        w_upd2 = sb("w_upd2", [D + 1, D])
        w_att = sb("w_att", [D + 1, D])
        w_r1 = sb("w_r1", [D + 1, D])
        w_l1 = sb("w_l1", [D, D])
        w_r2 = sb("w_r2", [D + 1, D])
        w_l2 = sb("w_l2", [D, D])
        w_lin = sb("w_lin", [D, 2 * D])
        w_own = sb("w_own", [D + 1, D + 2])
        w_hm = sb("w_hm", [D + 1, D + 1])
        coef = sb("coef", [P, 16])

        rdeg = sb("rdeg", [P, NT])

        ps = ctx.enter_context(nc.psum_tensor("ps", [P, 8, 512], F32))

        s_held = sem("held")

        def hold(eng):
            eng.sem_inc(s_held, 1)

        def bc(v, shape):
            return v.broadcast_to(shape)

        ld = sem("loads")
        loads, index_loads = [], []
        ld_index = sem("index_loads")

        def col(v):
            return v.rearrange("(a b) -> a b", b=1)

        def row(v):
            return v.rearrange("(a b) -> a b", a=1)

        def by_edge(v, lo, n):
            return v[lo:lo + n * CE].rearrange("(c p j) -> p c j", p=P, j=TPC)

        s_z = sem("zeroed")
        s_filler, s_fill = sem("filler"), sem("props_filled")
        with nc.Block() as block:
            W1, U1 = a["L0_gnn_msg_W1"], a["L0_gnn_upd_W1"]
            loads += [
                (X[:, 0:FULL, :], a["x"][0:FULL * P].rearrange("(t p) d -> p t d", p=P)),
                (X[0:TAIL, FULL, :], a["x"][FULL * P:N]),
                (w_in[0:D, 0:D], W1[0:D]), (w_in[0:D, D:2 * D], W1[D:2 * D]), (w_edge[:], W1[2 * D:3 * D]),
                (w_in[0:D, 2 * D:3 * D], U1[D:2 * D]), (w_upd1[:], U1[0:D]),
                (w_in[D:D + 1, D:2 * D], row(a["L0_gnn_msg_b1"])), (w_in[D:D + 1, 2 * D:3 * D], row(a["L0_gnn_upd_b1"])),
                (w_msg2[0:D], a["L0_gnn_msg_W2"]), (w_msg2[D:D + 1], row(a["L0_gnn_msg_b2"])),
                (w_upd2[0:D], a["L0_gnn_upd_W2"]), (w_upd2[D:D + 1], row(a["L0_gnn_upd_b2"])),
                (w_att[0:D], a["L1_gnn_W"]), (w_att[D:D + 1], row(a["L1_gnn_b"])),
                (w_r1[0:D], a["L2_gnn_W1_r"]), (w_r1[D:D + 1], row(a["L2_gnn_b1_l"])), (w_l1[:], a["L2_gnn_W1_l"]),
                (w_r2[0:D], a["L2_gnn_W2_r"]), (w_r2[D:D + 1], row(a["L2_gnn_b2_l"])), (w_l2[:], a["L2_gnn_W2_l"]),
                (w_lin[:], a["L3_gnn_lin_w"]), (w_own[D:D + 1, 0:D], row(a["L3_gnn_lin_b"])),
                (w_own[0:D, D:D + 1], a["L3_gnn_attn_w"][0:D]), (w_own[0:D, D + 1:D + 2], a["L3_gnn_attn_w"][D:2 * D]),
                (coef[:, 0:2], bc(row(a["L1_gnn_deg_coeff"]), [P, 2])),
                (coef[:, 2:5], bc(row(a["L1_gnn_coeff_param"]), [P, 3])),
                (coef[:, 5:6], bc(row(a["L1_gnn_scale_param"]), [P, 1])),
            ]
            ints = acc[:, 0:2 * C * TPC].bitcast(I32).rearrange("p (k c j) -> p k c j", k=2, j=TPC)
            dsti = ints[:, 0]
            ew2 = acc[:, 2 * C * TPC:3 * C * TPC].rearrange("p (c j) -> p c j", j=TPC)
            for t, v in ((srci, a["src"]), (dsti, a["dst"]), (ewt, a["edge_weight"]), (ew2, a["edge_weight_n2"])):
                index_loads.append((t[:, 0:C - 1, :], by_edge(v, 0, C - 1)))
                index_loads.append((t[:, C - 1:C, :], by_edge(v, E - CE, 1)))

            @block.sync
            def _(sp):
                sp.wait_ge(s_z, 3)
                with nc.allow_non_contiguous_dma("columns of small weights"):
                    for dst, src in loads:
                        sp.dma_start(dst, src).then_inc(ld, 16)
                    for dst, src in index_loads:
                        sp.dma_start(dst, src).then_inc(ld_index, 16)
                sp.wait_ge(ld, 16 * len(loads))

            s_i = sem("iotas")

            @block.gpsimd
            def _(pool):
                pool.memset(ident[:], 0.0).then_inc(s_i, 1)
                pool.memset(lower[:], 1.0).then_inc(s_i, 1)
                pool.iota(iota_f[:], [[1, P]], base=0, channel_multiplier=0, allow_small_or_imprecise_dtypes=True).then_inc(s_i, 1)
                pool.iota(trash[:], [[1, 1]], base=N, channel_multiplier=1, allow_small_or_imprecise_dtypes=True).then_inc(s_i, 1)
                pool.wait_ge(s_i, 4)
                pool.affine_select(out=ident[:], in_=ident[:], compare_op=ALU.not_equal, fill=1.0, base=0,
                                   pattern=[[-1, P]], channel_multiplier=1).then_inc(s_i, 1)
                pool.affine_select(out=lower[:], in_=lower[:], compare_op=ALU.is_gt, fill=0.0, base=0,
                                   pattern=[[-1, P]], channel_multiplier=1).then_inc(s_i, 1)
                pool.memset(zero[:], 0.0).then_inc(s_filler, 1)
                pool.wait_ge(s_i, 6)

            @block.vector
            def _(dve):
                dve.memset(X[:, FULL:NT, :], 0.0).then_inc(s_z, 1)
                dve.memset(w_in[D:D + 1, 0:D], 0.0).then_inc(s_z, 1)
                dve.memset(w_own[D:D + 1, D:D + 2], 0.0).then_inc(s_z, 1)
                dve.memset(w_hm[:], 0.0).then_inc(s_z, 1)
                dve.memset(w_fold[:, D:D + 1], 0.0).then_inc(s_z, 1)
                dve.wait_ge(s_z, 5)
                dve.memset(w_hm[D:D + 1, D:D + 1], 1.0).then_inc(s_z, 1)
                dve.memset(w_fold[D:D + 1, D:D + 1], 1.0).then_inc(s_z, 1)
                dve.memset(small[:, 0:1], 1.0e-5).then_inc(s_z, 1)
                dve.memset(small[:, 1:2], 1.0).then_inc(s_z, 1)
                dve.memset(small[:, 8:9], -BIG).then_inc(s_z, 1)
                dve.wait_ge(s_z, 10)

        steps = {}
        s_ones = sem("ones_row")
        in_sem = [[sem(f"prop_in{k}_{s}") for s in range(2)] for k in range(NPROP)]
        out_sem = [[sem(f"rows_out{k}_{s}") for s in range(2)] for k in range(2)]
        outs = [0, 0]

        keepN = keep[:].rearrange("p (t d) -> p t d", d=D)
        psT = ps[0:D, 0:3, :].rearrange("p b q -> p (b q)")
        SPAN, PB = 66, 7
        parts = [(b, PB * b, min(PB, GT - PB * b)) for b in range(-(-GT // PB))]
        FIRST, SECOND = 3, 5

        def tiles_of(b, n, lo, hi):
            return ps[:, b, 0:n * SPAN].rearrange("p (t m) -> p t m", m=SPAN)[:, :, lo:hi]

        def each(v, n=GT):
            return v.rearrange("p (t o) -> p t o", o=1).broadcast_to([P, n, D])

        def one(v):
            return v.rearrange("p (t o) -> p t o", o=1)

        def node_rows(table, g):
            return table[bass.ds(g * (GT * P), GT * P), :].rearrange("(t p) d -> p t d", p=P)

        def group_of(t, g, t0=0, n=GT):
            return t[:, bass.ds(g * GT + t0, n), :]

        def products(pe, lhsT, k, w, place):
            m = w.shape[1]
            for b, t0, n in parts:
                for t in range(n):
                    lo = (t0 + t) * P
                    ins = pe.matmul(ps[:, place + b, t * SPAN:t * SPAN + m], lhsT[0:k, lo:lo + P], w, start=True, stop=True)
            return ins

        def phase(name, take, plan, rows):
            with ExitStack() as scratch:
                used = []

                def pair(n, shape):
                    return [scratch.enter_context(nc.sbuf_tensor(f"{name}_{n}{k}", shape, F32)) for k in range(2)]

                xc, hN, hT = pair("xc", [P, GT, D]), pair("hN", [P, GT, D + 2]), pair("hT", [D + 1, GT * P])
                st = pair("st", [P, 6, GT])
                accS = pair("accS", [D + 1, GT * P]) if take not in (None, "prop") else None
                zN, zT, rN = (pair("zN", [P, GT, D]), pair("zT", [D + 1, GT * P]), pair("rN", [P, GT, D + 1])) if take == "msg" else (None,) * 3
                tN = pair("tN", [P, GT, D]) if take in (None, "sage1", "sage2", "soft") else None
                loaded = [pair(f"prop{k}", [P, GT, D]) for k in range(NPROP)] if take == "prop" else None
                tS = pair("tS", [P, GT, 1])
                src_of = {"hN": hN, "tN": tN, "rN": rN, "tS": tS}
                total_ones = [0]

                def done(ins, step):
                    if step not in steps:
                        steps[step] = Step(sem("node_" + step))
                    if step not in used:
                        used.append(step)
                    ins.then_inc(steps[step].sem, 1)

                def after(eng, step, g, back=0):
                    if step not in steps:
                        steps[step] = Step(sem("node_" + step))
                    if not (isinstance(g, int) and g < back):
                        eng.wait_ge(steps[step].sem, steps[step].at(g - back))

                def rows_left(eng, k, s, turn):
                    if not (isinstance(turn, int) and turn < 2):
                        eng.wait_ge(out_sem[k][s], outs[k] + (turn - 1) * 16)

                def load_props(sp, g, s, turn):
                    after(sp, "x", g, 2)
                    hold(sp)
                    for k in range(NPROP):
                        sp.dma_start(loaded[k][s][:], node_rows(props[k], g)).then_inc(in_sem[k][s], 16)

                def store(k):
                    table, buf, cols, step, _ = rows[k]

                    def f(sp, g, s, turn):
                        after(sp, step, g)
                        hold(sp)
                        with nc.allow_non_contiguous_dma("a column of scores"):
                            sp.dma_start(node_rows(table, g), src_of[buf][s][:, :, 0:cols]).then_inc(out_sem[k][s], 16)
                    return f

                def v_z(dve, g, s, turn):
                    after(dve, "mean", g)
                    for b, t0, n in parts:
                        dve.tensor_scalar(one(rdeg[:, bass.ds(g * GT + t0, n)]), tiles_of(FIRST + b, n, D, D + 1), 1.0, None, ALU.max)
                        ins = dve.tensor_tensor(zN[s][:, t0:t0 + n, :], tiles_of(FIRST + b, n, 0, D), group_of(keepN, g, t0, n), ALU.add)
                    done(ins, "pre")
                    after(dve, "pre", g)
                    done(dve.tensor_scalar(zN[s][:], zN[s][:], 0.0, None, ALU.max), "z")
                    dg = rdeg[:, bass.ds(g * GT, GT)]
                    dve.reciprocal(dg, dg)

                def v_x_msg(dve, g, s, turn):
                    after(dve, "upd", g)
                    for b, t0, n in parts:
                        ins = dve.tensor_tensor(group_of(X, g, t0, n), group_of(X, g, t0, n), tiles_of(SECOND + b, n, 0, D), ALU.add)
                    done(ins, "x")

                def v_x_prop(dve, g, s, turn):
                    for k in range(NPROP):
                        dve.wait_ge(in_sem[k][s], turn * 16)
                        if k:
                            after(dve, f"p{k - 1}", g)
                        done(dve.tensor_tensor(group_of(X, g), group_of(X, g), loaded[k][s][:], ALU.add), f"p{k}" if k < NPROP - 1 else "x")

                def v_mean(dve, g, s, turn):
                    after(dve, "mean", g)
                    for b, t0, n in parts:
                        ins = dve.tensor_tensor(tN[s][:, t0:t0 + n, :], tiles_of(FIRST + b, n, 0, D),
                                                each(rdeg[:, bass.ds(g * GT + t0, n)], n), ALU.mult)
                    done(ins, "scaled")
                    after(dve, "scaled", g)
                    done(dve.tensor_tensor(tN[s][:], tN[s][:], group_of(keepN, g), ALU.add), "pre")
                    after(dve, "pre", g)
                    if take == "sage1":
                        rows_left(dve, 0, s, turn)
                        hold(dve)
                        done(dve.tensor_scalar(hN[s][:, :, 0:D], tN[s][:], 0.0, None, ALU.max), "h")
                    else:
                        done(dve.scalar_tensor_tensor(group_of(X, g), tN[s][:], 0.0, group_of(X, g), ALU.max, ALU.add), "x")

                def v_soft(dve, g, s, turn):
                    after(dve, "mean", g)
                    for b, t0, n in parts:
                        ins = dve.tensor_scalar(one(st[s][:, 0, t0:t0 + n]), tiles_of(FIRST + b, n, D, D + 1), 1.0e-30, None, ALU.max)
                    done(ins, "den")
                    after(dve, "den", g)
                    done(dve.reciprocal(st[s][:, 1, :], st[s][:, 0, :]), "rden")
                    after(dve, "rden", g)
                    for b, t0, n in parts:
                        ins = dve.tensor_tensor(tN[s][:, t0:t0 + n, :], tiles_of(FIRST + b, n, 0, D), each(st[s][:, 1, t0:t0 + n], n), ALU.mult)
                    done(ins, "scaled")
                    after(dve, "scaled", g)
                    done(dve.tensor_tensor(tN[s][:], tN[s][:], group_of(keepN, g), ALU.add), "pre")
                    after(dve, "pre", g)
                    done(dve.scalar_tensor_tensor(group_of(X, g), tN[s][:], 0.0, group_of(X, g), ALU.max, ALU.add), "x")

                def v_xc(dve, g, s, turn):
                    if take:
                        after(dve, "x", g)
                        hold(dve)
                    done(dve.tensor_reduce(st[s][:, 0, :], group_of(X, g), AX, ALU.add), "sum")
                    after(dve, "sum", g)
                    done(dve.tensor_scalar(st[s][:, 1, :], st[s][:, 0, :], 1.0 / D, None, ALU.mult), "avg")
                    after(dve, "avg", g)
                    done(dve.tensor_tensor(xc[s][:], group_of(X, g), each(st[s][:, 1, :]), ALU.subtract), "xc")

                def v_var(dve, g, s, turn):
                    after(dve, "square", g)
                    done(dve.tensor_reduce(st[s][:, 2, :], hN[s][:, :, 0:D], AX, ALU.add), "var")

                def v_h(dve, g, s, turn):
                    after(dve, "std", g)
                    done(dve.reciprocal(st[s][:, 4, :], st[s][:, 3, :]), "rstd")
                    after(dve, "rstd", g)
                    done(dve.scalar_tensor_tensor(hN[s][:, :, 0:D], xc[s][:], 0.0, each(st[s][:, 4, :]), ALU.max, ALU.mult), "h")

                def v_own(dve, g, s, turn):
                    after(dve, "own", g)
                    hold(dve)
                    for b, t0, n in parts:
                        ins = dve.tensor_copy(group_of(keepN, g, t0, n), tiles_of(SECOND + b, n, 0, D))
                    done(ins, "kept")

                def v_dst_row(dve, g, s, turn):
                    after(dve, "dst", g)
                    rows_left(dve, 1, s, turn)
                    hold(dve)
                    for b, t0, n in parts:
                        ins = dve.tensor_copy(tN[s][:, t0:t0 + n, :], tiles_of(SECOND + b, n, 0, D))
                    done(ins, "dst_row")

                def v_wh(dve, g, s, turn):
                    after(dve, "own", g)
                    rows_left(dve, 0, s, turn)
                    hold(dve)
                    for b, t0, n in parts:
                        ins = dve.tensor_copy(rN[s][:, t0:t0 + n, 0:D], tiles_of(FIRST + b, n, 0, D))
                    done(ins, "wh")
                    after(dve, "wh", g)
                    dve.scalar_tensor_tensor(group_of(X, g), rN[s][:, :, 0:D], coef[:, 12:13], group_of(X, g), ALU.mult, ALU.add)

                def v_norm2(dve, g, s, turn):
                    after(dve, "wh_square", g)
                    done(dve.tensor_reduce(st[s][:, 5, :], xc[s][:], AX, ALU.add), "norm2")

                def v_scores(dve, g, s, turn):
                    v_own(dve, g, s, turn)
                    rows_left(dve, 1, s, turn)
                    hold(dve)
                    for b, t0, n in parts:
                        dve.tensor_copy(hN[s][:, t0:t0 + n, D + 1:D + 2], tiles_of(SECOND + b, n, D, D + 1))
                        dve.tensor_copy(tS[s][:, t0:t0 + n, :], tiles_of(SECOND + b, n, D + 1, D + 2))
                    done(dve.memset(hN[s][:, :, D:D + 1], 1.0), "row")

                def a_sums(act, g, s, turn):
                    after(act, "mean", g, 2)
                    hold(act)
                    done(act.activation(accS[s][:], acc[0:D + 1, bass.ds(g * (GT * P), GT * P)], ACT.Copy), "sums")

                def a_square(act, g, s, turn):
                    after(act, "xc", g)
                    if any(r[1] == "hN" for r in rows):
                        rows_left(act, 0, s, turn)
                    after(act, "turned", g, 2)
                    done(act.activation(hN[s][:, :, 0:D], xc[s][:], ACT.Square), "square")

                def a_std(act, g, s, turn):
                    after(act, "var", g)
                    done(act.activation(st[s][:, 3, :], st[s][:, 2, :], ACT.Sqrt, bias=small[:, 0:1], scale=1.0 / D), "std")

                def a_zT(act, g, s, turn):
                    after(act, "z_turned", g)
                    after(act, "upd", g, 2)
                    done(act.activation(zT[s][0:D, :], psT[:, 0:GT * P], ACT.Copy), "zT")

                def a_hT(act, g, s, turn):
                    after(act, "turned", g)
                    after(act, "dst" if take is None else "own", g, 2)
                    done(act.activation(hT[s][0:D, :], psT[:, 0:GT * P], ACT.Copy), "hT")

                def a_src_row(act, g, s, turn):
                    after(act, "src", g)
                    rows_left(act, 0, s, turn)
                    for b, t0, n in parts:
                        ins = act.activation(rowsrc[s][:, t0:t0 + n, :], tiles_of(FIRST + b, n, 0, D), ACT.Copy)
                    done(ins, "src_row")

                def a_wh_square(act, g, s, turn):
                    after(act, "wh", g)
                    after(act, "h", g)
                    done(act.activation(xc[s][:], rN[s][:, :, 0:D], ACT.Square), "wh_square")

                def a_norm(act, g, s, turn):
                    after(act, "norm2", g)
                    done(act.activation(rN[s][:, :, D:D + 1], one(st[s][:, 5, :]), ACT.Sqrt), "row")

                def p_mean(pe, g, s, turn):
                    after(pe, "sums", g)
                    if take == "msg":
                        after(pe, "wh", g, 3)
                    else:
                        after(pe, "scaled", g, 1)
                    w = {"msg": w_fold, "sage1": w_l1, "sage2": w_l2, "soft": w_hm}[take]
                    done(products(pe, accS[s], w.shape[0], w[:], FIRST), "mean")

                def p_z_turned(pe, g, s, turn):
                    after(pe, "z", g)
                    after(pe, "hT", g, 1)
                    hold(pe)
                    for t in range(GT):
                        ins = pe.transpose(psT[:, t * P:(t + 1) * P], zN[s][:, t, :], ident[:])
                    done(ins, "z_turned")

                def p_upd(pe, g, s, turn):
                    after(pe, "zT", g)
                    after(pe, "x", g, 1)
                    done(products(pe, zT[s], D + 1, w_upd2[:], SECOND), "upd")

                def p_turned(pe, g, s, turn):
                    after(pe, "h", g)
                    if take == "msg":
                        after(pe, "zT", g)
                    else:
                        after(pe, "hT", g, 1)
                    hold(pe)
                    for t in range(GT):
                        ins = pe.transpose(psT[:, t * P:(t + 1) * P], hN[s][:, t, 0:D], ident[:])
                    done(ins, "turned")

                def p_own(pe, g, s, turn):
                    after(pe, "hT", g)
                    if take == "msg":
                        after(pe, "pre", g, -2 if not isinstance(g, int) or g + 2 < NG else -(NG - 1 - g))
                        after(pe, "wh", g, 1)
                        done(products(pe, hT[s], D + 1, w_att[:], FIRST), "own")
                        return
                    after(pe, {None: "dst_row", "sage2": "row"}.get(take, "kept"), g, 1)
                    w = {None: w_in[:, 2 * D:3 * D], "prop": w_r1[:], "sage1": w_r2[:], "sage2": w_own[:]}[take]
                    done(products(pe, hT[s], D + 1, w, SECOND), "own")

                def p_src(pe, g, s, turn):
                    after(pe, "src_row", g, 1)
                    done(products(pe, hT[s], D + 1, w_in[:, 0:D], FIRST), "src")

                def p_dst(pe, g, s, turn):
                    after(pe, "kept", g)
                    done(products(pe, hT[s], D + 1, w_in[:, D:2 * D], SECOND), "dst")

                rowsrc = pair("rowsrc", [P, GT, D]) if take is None else None
                src_of["rowsrc"] = rowsrc
                made = locals()

                def groups(eng, plan):
                    def iteration(i, k, hi):
                        for lag, f in plan:
                            s = k - lag
                            if s < hi and not (isinstance(i, int) and i * 2 + s < 0):
                                f(eng, i * 2 + s, s % 2, i + (s // 2 + 1))

                    for k in range(4):
                        iteration(k // 2, k % 2, 2)
                    with eng.Fori(2, NG // 2) as i:
                        for k in range(2):
                            iteration(i, k, 2)
                    for k in range(2, 2 + max(lag for lag, _ in plan)):
                        iteration(NG // 2 - 1, k, 2)

                block = scratch.enter_context(nc.Block())
                sync_plan = [(rows[k][4], store(k)) for k in range(len(rows))]
                if take == "prop":
                    sync_plan.insert(0, (0, load_props))

                @block.sync
                def _(sp):
                    if sync_plan:
                        groups(sp, sync_plan)
                    for k in range(len(rows)):
                        for s in range(2):
                            sp.wait_ge(out_sem[k][s], outs[k] + 16 * (NG // 2))

                @block.vector
                def _(dve):
                    for t in (hT if take != "soft" else []) + (zT or []):
                        dve.memset(t[D:D + 1, :], 1.0).then_inc(s_ones, 1)
                        total_ones[0] += 1
                    groups(dve, [(lag, made["v_" + f]) for lag, f in plan["v"]])

                ones[0] += total_ones[0]

                @block.scalar
                def _(act):
                    if plan["a"]:
                        groups(act, [(lag, made["a_" + f]) for lag, f in plan["a"]])

                @block.tensor
                def _(pe):
                    if ones[0]:
                        pe.wait_ge(s_ones, ones[0])
                    groups(pe, [(lag, made["p_" + f]) for lag, f in plan["p"]])

                if take in ("prop", "sage1", "sage2"):
                    @block.gpsimd
                    def _(pool):
                        for g in range(NG):
                            nodes = slice(g * (GT * P), (g + 1) * (GT * P))
                            if take != "prop":
                                after(pool, "sums", g)
                            done(pool.memset(acc[0:TOP, nodes], 0.0), "zeroed")
                            if take == "sage2":
                                done(pool.memset(acc[TOP:TOP + 1, nodes], NEG), "no_max")
            for k in range(len(rows)):
                outs[k] += 16 * (NG // 2)
            for n in used:
                steps[n].before += NG

        ones = [0]

        s_acc0 = sem("acc_zeroed")
        gathered = [sem(f"gathered{k}") for k in range(U)]
        s_const, n_const = sem("constant_columns"), [0]
        s_next = sem("next_bases")
        n_next = [0]

        def zero_sums():
            with nc.Block() as block:
                @block.vector
                def _(dve):
                    dve.memset(acc[:, 0:setup_end // 2], 0.0).then_inc(s_acc0, 1)

                @block.gpsimd
                def _(pool):
                    pool.memset(acc[:, setup_end // 2:setup_end], 0.0).then_inc(s_acc0, 1)

                @block.scalar
                def _(act):
                    act.wait_ge(s_filler, 1)
                    for k in range(NPROP):
                        act.dma_start(props[k].rearrange("(p q t) d -> p q (t d)", p=P, q=4),
                                      zero[:].rearrange("p (o n) -> p o n", o=1).broadcast_to([P, 4, NT // 4 * D])).then_inc(s_fill, 16)

        def move_bases(dve, to_start):
            if to_start:
                dve.tensor_copy(base_bc[:], base0[:]).then_inc(s_next, 1)
            else:
                dve.tensor_scalar(base_bc[:], base_bc[:], float(P), float(N), ALU.add, ALU.min).then_inc(s_next, 1)
            dve.drain()
            dve.tensor_copy(base_i[:], base_bc[0:1, :]).then_inc(s_next, 1)
            dve.drain()

        def edge_pass(name, stages, src_table, cols, bufs, programs, rows_user, oh_user="sums", win_user="pre",
                      last_stage="acc", win_table=None, wcols=0, edges=False, pool=None, views={}):
            with ExitStack() as scope:
                S = {n: scope.enter_context(nc.semaphore(f"{name}_{n}")) for n in stages.split()}
                loaded = [scope.enter_context(nc.semaphore(f"{name}_loaded{k}")) for k in range(2)]

                def buf(n, shape, dt=F32, k=2):
                    return [scope.enter_context(nc.sbuf_tensor(f"{name}_{n}{i}", shape, dt)) for i in range(k)]

                B = {"G": buf("G", [P, TPC, cols], k=U), "idx": buf("idx", [P, TPC], I32, k=U),
                     "OH": buf("OH", [P, TPC, P], k=U), "drel": buf("drel", [P, TPC])}
                if win_table is not None:
                    B["win"], B["OHT"] = buf("win", [P, wcols]), buf("OHT", [P, TPC, P])
                if edges:
                    B["edge"] = buf("edge", [P, TPC, D])
                for n, shape, dt, k in bufs:
                    B[n] = buf(n, shape, dt, k)
                B.update(views)
                load_inc = 16 * ((win_table is not None) + edges)
                with nc.Block() as block:
                    @block.vector
                    def _(dve):
                        if "msg" in B:
                            for m in B["msg"]:
                                dve.memset(m[:, :, D:D + 1], 1.0).then_inc(s_const, 1)
                            n_const[0] += len(B["msg"])
                            dve.wait_ge(s_const, n_const[0])
                        move_bases(dve, True)
                rounds = nc.values_load(rounds_i[0:1, 0:1], min_val=1, max_val=NT)
                with nc.Fori(0, rounds) as r:

                    def at(c, back=0):
                        return c + (1 + U - back)

                    def chunks(eng, *stages):
                        def iteration(i, k, lo, hi):
                            for lag, body in stages:
                                s = k - lag
                                if lo <= s < hi:
                                    body((i * U) + s, s % U, i + (s // U + 1), isinstance(i, int) and i * U + s == C - 1)

                        for k in range(U):
                            iteration(0, k, 0, C)
                        with eng.Fori(1, C // U - 1) as i:
                            for k in range(U):
                                iteration(i, k, -U, C)
                        for k in range(U + max(lag for lag, _ in stages)):
                            iteration(C // U - 1, k, -U, U)

                    def wait_gather(eng, h, turn):
                        eng.wait_ge(gathered[h], turn * (16 * TPC))

                    def wait_loads(eng, h, turn):
                        eng.wait_ge(loaded[h % 2], turn * (U // 2 * load_inc) + (h // 2 + 1 - U // 2) * load_inc)

                    K = dict(S=S, B=B, at=at, rows_user=rows_user, oh_user=oh_user, wait_gather=wait_gather, wait_loads=wait_loads, chunks=chunks)

                    def run(eng, key):
                        chunks(eng, *[(lag, lambda c, h, turn, last, f=f: f(K, eng, c, h, turn)) for lag, f in programs[key]])

                    def gather(eng, c, h, turn):
                        eng.wait_ge(S[rows_user], at(c, U))
                        eng.wait_ge(S["idx"], at(c))
                        hold(eng)
                        for j in range(TPC):
                            gather_tile(eng, h, j)

                    def gather_tile(eng, h, j):
                        eng.indirect_dma_start(B["G"][h][:, j, :], None, src_table, bass.IndirectOffsetOnAxis(
                            ap=B["idx"][h][:, j:j + 1], axis=0)).then_inc(gathered[h], 16)

                    with nc.Block() as block:
                        if load_inc:
                            @block.sync
                            def _(sp):
                                def body(c, h, turn, last):
                                    b = h % 2
                                    if win_table is not None:
                                        first = sp.value_load(base_i[0:1, bass.ds(c, 1)], min_val=0, max_val=N)
                                        sp.wait_ge(S[win_user], at(c, 2))
                                        hold(sp)
                                        with nc.allow_non_contiguous_dma("a window's column"):
                                            sp.dma_start(B["win"][b][:], win_table[bass.ds(first, P), 0:wcols]).then_inc(loaded[b], 16)
                                    if edges:
                                        sp.wait_ge(S["edge_turned"], at(c, 2))
                                        hold(sp)
                                        lo = E - CE if last else c * CE
                                        rows = a["edge_attr_64"][bass.ds(lo, CE), :].rearrange("(p j) d -> p j d", j=TPC)
                                        sp.dma_start(B["edge"][b][:], rows).then_inc(loaded[b], 16)
                                chunks(sp, (0, body))

                        @block.gpsimd
                        def _(eng):
                            if pool is None:
                                chunks(eng, (0, lambda c, h, turn, last: gather(eng, c, h, turn)))
                            else:
                                pool(K, eng, gather_tile)

                        @block.vector
                        def _(dve):
                            for s in S.values():
                                dve.sem_inc(s, U)
                            run(dve, "dve")
                            dve.wait_ge(S[last_stage], at(C - 1))
                            move_bases(dve, False)

                        @block.scalar
                        def _(act):
                            run(act, "act")

                        @block.tensor
                        def _(pe):
                            run(pe, "pe")
                    with nc.Block() as block:
                        @block.gpsimd
                        def _(eng):
                            for s in gathered:
                                eng.wait_ge(s, C // U * (16 * TPC))
                            eng.inc_swdge_sem(gathered, [C // U * (16 * TPC)] * U, mode="sub")
                            if pool is not None:
                                for s in s_prop:
                                    eng.wait_ge(s, CREDIT + SCATTERED)
                                eng.inc_swdge_sem(s_prop, [CREDIT + SCATTERED] * NPROP, mode="sub")

                        @block.sync
                        def _(sp):
                            for s in [*S.values(), *loaded, s_held]:
                                sp.sem_clear(s)


        def cols_of(t, c):
            return t[:, bass.ds(c, 1), :].rearrange("p o j -> p (o j)")

        def wide(v, m):
            return v.rearrange("p (j o) -> p j o", o=1).broadcast_to([P, TPC, m])

        iota_all = iota_f[:].rearrange("p (o n) -> p o n", o=1).broadcast_to([P, TPC, P])
        banks = lambda b: ps[:, b:b + 2, :].rearrange("p b q -> p (b q)").rearrange("p (j n) -> p j n", n=P)

        def one_hot(K, dve, c, h, turn):
            S, B, at, b = K["S"], K["B"], K["at"], h % 2
            dve.tensor_scalar(B["drel"][b][:], cols_of(dstf, c), base_bc[:, bass.ds(c, 1)], None, ALU.subtract).then_inc(S["drel"], 1)
            dve.wait_ge(S[K["oh_user"]], at(c, U))
            dve.wait_ge(S["drel"], at(c))
            dve.tensor_tensor(B["OH"][h][:], iota_all, wide(B["drel"][b][:], P), ALU.is_equal).then_inc(S["oh"], 1)

        def copy_indices(K, act, c, h, turn):
            S, B, at = K["S"], K["B"], K["at"]
            act.wait_ge(S[K["rows_user"]], at(c, U))
            hold(act)
            act.activation(B["idx"][h][:], cols_of(srci, c), ACT.Copy).then_inc(S["idx"], 1)

        def turn_one_hot(K, pe, c, h, turn):
            S, B, at, b = K["S"], K["B"], K["at"], h % 2
            pe.wait_ge(S["oh"], at(c))
            pe.wait_ge(S["oht"], at(c, 1))
            for j in range(TPC):
                ins = pe.transpose(banks(0)[:, j, :], B["OH"][h][:, j, :], ident[:])
            ins.then_inc(S["oh_turned"], 1)

        def take_one_hot(K, act, c, h, turn, user):
            S, B, at, b = K["S"], K["B"], K["at"], h % 2
            act.wait_ge(S["oh_turned"], at(c))
            act.wait_ge(S[user], at(c, 2))
            act.activation(B["OHT"][b][:], banks(0), ACT.Copy).then_inc(S["oht"], 1)

        def sum_by_node(K, pe, rows, m, c, h):
            S, B, at = K["S"], K["B"], K["at"]
            pe.wait_ge(S["acc"], at(c, 2))
            for j in range(TPC):
                ins = pe.matmul(ps[0:m, 6 + h % 2, 0:P], rows(j), B["OH"][h][:, j, :], start=(j == 0), stop=(j == TPC - 1))
            ins.then_inc(S["sums"], 1)

        def add_sums(K, dve, m, c, h):
            S, at = K["S"], K["at"]
            first = dve.value_load(base_i[0:1, bass.ds(c, 1)], min_val=0, max_val=N)
            dve.wait_ge(S["sums"], at(c))
            dve.wait_ge(S["acc"], at(c, 1))
            w = acc[0:m, bass.ds(first, P)]
            dve.tensor_tensor(w, w, ps[0:m, 6 + h % 2, 0:P], ALU.add).then_inc(S["acc"], 1)

        def msg_dve(K, dve, c, h, turn):
            S, B, at, b = K["S"], K["B"], K["at"], h % 2
            dve.wait_ge(S["pre"], at(c))
            dve.wait_ge(S["sums"], at(c, 2))
            K["wait_gather"](dve, h, turn)
            dve.tensor_tensor(B["msg"][b][:, :, 0:D], ps[:, 4 + b, :].rearrange("p (j d) -> p j d", d=D), B["G"][h][:], ALU.add).then_inc(S["summed"], 1)

        def msg_dve_add(K, dve, c, h, turn):
            add_sums(K, dve, D + 1, c, h)

        def msg_act_prep(K, act, c, h, turn):
            take_one_hot(K, act, c, h, turn, "pre")
            S, B, at, b = K["S"], K["B"], K["at"], h % 2
            act.wait_ge(S["edge_turned"], at(c))
            act.activation(B["edgeT"][b][:], banks(2)[0:D], ACT.Copy).then_inc(S["edgeT"], 1)

        def msg_act(K, act, c, h, turn):
            S, B, at, b = K["S"], K["B"], K["at"], h % 2
            act.wait_ge(S["summed"], at(c))
            act.activation(B["msg"][b][:, :, 0:D], B["msg"][b][:, :, 0:D], ACT.Relu).then_inc(S["msg"], 1)

        def msg_pe_prep(K, pe, c, h, turn):
            S, B, at, b = K["S"], K["B"], K["at"], h % 2
            turn_one_hot(K, pe, c, h, turn)
            K["wait_loads"](pe, h, turn)
            pe.wait_ge(S["edgeT"], at(c, 1))
            hold(pe)
            for j in range(TPC):
                ins = pe.transpose(banks(2)[0:D, j, :], B["edge"][b][:, j, :], ident[:])
            ins.then_inc(S["edge_turned"], 1)

        def msg_pe(K, pe, c, h, turn):
            S, B, at, b = K["S"], K["B"], K["at"], h % 2
            pe.wait_ge(S["edgeT"], at(c))
            pe.wait_ge(S["oht"], at(c))
            pe.wait_ge(S["summed"], at(c, 2))
            for j in range(TPC):
                o = ps[:, 4 + b, j * D:(j + 1) * D]
                pe.matmul(o, B["edgeT"][b][:, j, :], w_edge[:], start=True, stop=False)
                ins = pe.matmul(o, B["OHT"][b][:, j, :], B["win"][b][:], start=False, stop=True)
            ins.then_inc(S["pre"], 1)

        def msg_pe_sum(K, pe, c, h, turn):
            S, B, at, b = K["S"], K["B"], K["at"], h % 2
            pe.wait_ge(S["msg"], at(c))
            sum_by_node(K, pe, lambda j: B["msg"][b][:, j, :], D + 1, c, h)

        def sage_act(K, act, c, h, turn):
            copy_indices(K, act, c, h, turn)

        def sage_pe(K, pe, c, h, turn):
            K["wait_gather"](pe, h, turn)
            pe.wait_ge(K["S"]["oh"], K["at"](c))
            sum_by_node(K, pe, lambda j: K["B"]["G"][h][:, j, :], D, c, h)

        def sage_dve(K, dve, c, h, turn):
            add_sums(K, dve, D, c, h)

        CREDIT = 16 * TPC // NPROP * U
        SCATTERED = C * (16 * TPC // NPROP)
        s_prop = [sem(f"prop{k}") for k in range(NPROP)]

        def scatters_before(K, c, more=0):
            return c * (16 * TPC // NPROP) + (CREDIT + more)

        def wait_scatters(K, eng, c):
            for s in s_prop:
                eng.wait_ge(s, scatters_before(K, c, -16 * TPC // NPROP * (U - 1)))

        def att_pool(K, eng, gather_tile):
            S, B, at = K["S"], K["B"], K["at"]

            def tiles(c, h, gathers, scatters):
                if gathers:
                    c2, h2 = c + 2, (h + 2) % U
                    eng.wait_ge(S[K["rows_user"]], at(c2, U))
                    eng.wait_ge(S["idx"], at(c2))
                if scatters:
                    eng.wait_ge(S["sidx"], at(c))
                    eng.wait_ge(S["out"], at(c))
                hold(eng)
                for j in range(TPC):
                    if gathers:
                        gather_tile(eng, h2, j)
                    if scatters:
                        k = j % NPROP
                        eng.wait_ge(s_prop[k], scatters_before(K, c, 16 * (j // NPROP)))
                        hold(eng)
                        eng.indirect_dma_start(props[k], bass.IndirectOffsetOnAxis(ap=B["sidx"][h][:, j:j + 1], axis=0),
                                               B["out"][h][:, j, :], None, compute_op=ALU.add).then_inc(s_prop[k], 16)

            eng.inc_swdge_sem(s_prop, [CREDIT] * NPROP, mode="add")
            eng.wait_ge(s_fill, 16 * NPROP)
            for h in (-2, -1):
                tiles(h, h, True, False)
            with eng.Fori(0, C // U - 1) as i:
                for h in range(U):
                    tiles(i * U + h, h, True, True)
            for h in range(U):
                tiles(C - U + h, h, h < U - 2, True)
            for s in s_prop:
                eng.wait_ge(s, scatters_before(K, C))

        def att_dve_prep(K, dve, c, h, turn):
            S, B, at, b = K["S"], K["B"], K["at"], h % 2
            dve.wait_ge(S["src_turned"], at(c))
            dve.wait_ge(S["merged"], at(c, 2))
            dve.tensor_tensor(B["SM"][b][:], banks(2), wide(B["srcs"][b][:], P), ALU.is_equal).then_inc(S["sm"], 1)
            dve.wait_ge(S["sm"], at(c))
            dve.tensor_tensor(B["before"][0][:], B["SM"][b][:], lower[:].rearrange("p (o n) -> p o n", o=1).broadcast_to([P, TPC, P]), ALU.mult).then_inc(S["before"], 1)
            dve.tensor_scalar(B["t"][b][:, 0], B["srcs"][b][:], -1.0, trash[:], ALU.mult, ALU.add).then_inc(S["away"], 1)
            dve.wait_ge(S["before"], at(c))
            dve.tensor_reduce(B["t"][b][:, 1], B["before"][0][:], AX, ALU.add).then_inc(S["count"], 1)
            dve.wait_ge(S["count"], at(c))
            dve.wait_ge(S["away"], at(c))
            dve.scalar_tensor_tensor(B["t"][b][:, 2], B["t"][b][:, 1], 0.5, B["t"][b][:, 0], ALU.is_gt, ALU.mult).then_inc(S["shift"], 1)
            dve.wait_ge(S["shift"], at(c))
            wait_scatters(K, dve, c)
            dve.tensor_tensor(B["sidx"][h][:], B["t"][b][:, 2], B["srcs"][b][:], ALU.add).then_inc(S["sidx"], 1)

        def att_dve(K, dve, c, h, turn):
            S, B, at, b = K["S"], K["B"], K["at"], h % 2
            t = B["m"][b]
            G = B["G"][h]
            wc = lambda q, lo, hi: ps[:, 4 + q, 0:4 * (D + 1)].rearrange("p (j d) -> p j d", d=D + 1)[:, :, lo:hi]
            K["wait_gather"](dve, h, turn)
            dve.wait_ge(S["wc"], at(c))
            for q in range(2):
                j = slice(4 * q, 4 * q + 4)
                dve.tensor_tensor(B["prod"][0][:, j, :], G[:, j, 0:D], wc(q, 0, D), ALU.mult)
                ins = dve.tensor_tensor(t[:, 0, j].rearrange("p (j o) -> p j o", o=1), G[:, j, D:D + 1], wc(q, D, D + 1), ALU.mult)
            ins.then_inc(S["dot"], 1)
            dve.wait_ge(S["dot"], at(c))
            dve.tensor_reduce(t[:, 1], B["prod"][0][:], AX, ALU.add)
            dve.tensor_scalar(t[:, 2], t[:, 0], 1.0e-8, None, ALU.max).then_inc(S["a1"], 1)
            dve.wait_ge(S["a1"], at(c))
            dve.reciprocal(t[:, 3], t[:, 2]).then_inc(S["a2"], 1)
            dve.wait_ge(S["a2"], at(c))
            dve.tensor_tensor(t[:, 4], t[:, 1], t[:, 3], ALU.mult).then_inc(S["sim"], 1)
            dve.wait_ge(S["sim"], at(c))
            dve.tensor_scalar(t[:, 5], t[:, 4], 0.0, coef[:, 10:11], ALU.max, ALU.mult)
            dve.tensor_scalar(t[:, 6], t[:, 4], 0.0, coef[:, 11:12], ALU.min, ALU.mult).then_inc(S["a3"], 1)
            dve.wait_ge(S["a3"], at(c))
            dve.tensor_tensor(t[:, 7], t[:, 5], t[:, 6], ALU.add).then_inc(S["a4"], 1)
            dve.wait_ge(S["a4"], at(c))
            dve.tensor_tensor(t[:, 8], t[:, 7], cols_of(ewt, c), ALU.mult).then_inc(S["weight"], 1)
            dve.wait_ge(S["weight"], at(c))
            dve.wait_ge(S["merged"], at(c, 2))
            for q in range(2):
                j = slice(4 * q, 4 * q + 4)
                w = t[:, 8, j].rearrange("p (j o) -> p j o", o=1).broadcast_to([P, 4, D])
                ins = dve.tensor_tensor(B["V"][b][:, j, :], wc(q, 0, D), w, ALU.mult)
            ins.then_inc(S["v"], 1)

        def att_act_prep(K, act, c, h, turn):
            S, B, at, b = K["S"], K["B"], K["at"], h % 2
            act.wait_ge(S["sidx"], at(c, 2))
            hold(act)
            act.activation(B["srcs"][b][:], cols_of(srci, c), ACT.Copy).then_inc(S["srcs"], 1)
            take_one_hot(K, act, c, h, turn, "wc")

        def att_act(K, act, c, h, turn):
            S, B, at, b = K["S"], K["B"], K["at"], h % 2
            act.wait_ge(S["merged"], at(c))
            wait_scatters(K, act, c)
            act.activation(B["out"][h][:], ps[:, 6 + b, :].rearrange("p (j d) -> p j d", d=D), ACT.Copy).then_inc(S["out"], 1)

        def att_pe_prep(K, pe, c, h, turn):
            S, B, at, b = K["S"], K["B"], K["at"], h % 2
            turn_one_hot(K, pe, c, h, turn)
            pe.wait_ge(S["srcs"], at(c))
            pe.wait_ge(S["sm"], at(c, 1))
            for j in range(TPC):
                ins = pe.transpose(banks(2)[:, j, :], B["srcs"][b][:, j:j + 1].broadcast_to([P, P]), ident[:])
            ins.then_inc(S["src_turned"], 1)

        def att_pe(K, pe, c, h, turn):
            S, B, at, b = K["S"], K["B"], K["at"], h % 2
            pe.wait_ge(S["oht"], at(c))
            K["wait_loads"](pe, h, turn)
            pe.wait_ge(S["v"], at(c, 1))
            for j in range(TPC):
                ins = pe.matmul(ps[:, 4 + j // 4, (j % 4) * (D + 1):(j % 4 + 1) * (D + 1)], B["OHT"][b][:, j, :], B["win"][b][:], start=True, stop=True)
            ins.then_inc(S["wc"], 1)

        def att_pe_merge(K, pe, c, h, turn):
            S, B, at, b = K["S"], K["B"], K["at"], h % 2
            pe.wait_ge(S["v"], at(c))
            pe.wait_ge(S["sm"], at(c))
            pe.wait_ge(S["out"], at(c, 2))
            for j in range(TPC):
                ins = pe.matmul(ps[:, 6 + b, j * D:(j + 1) * D], B["SM"][b][:, j, :], B["V"][b][:, j, :], start=True, stop=True)
            ins.then_inc(S["merged"], 1)


        def soft_act_prep(K, act, c, h, turn):
            S, B, at, b = K["S"], K["B"], K["at"], h % 2
            act.wait_ge(S["oh_turned"], at(c))
            act.wait_ge(S["top"], at(c, 2))
            act.activation(B["pen"][b][:], banks(0), ACT.Identity, bias=small[:, 8:9], scale=BIG)
            act.wait_ge(S["spread"], at(c, 2))
            act.activation(B["OHT"][b][:], banks(0), ACT.Copy).then_inc(S["oht"], 1)

        def soft_act_ratio(K, act, c, h, turn):
            S, B, at, b = K["S"], K["B"], K["at"], h % 2
            act.wait_ge(S["em"], at(c))
            act.activation(B["Q"][b][:, 0:TOP], B["q"][b][:, 7:8].broadcast_to([P, TOP]), ACT.Exp).then_inc(S["ratio"], 1)

        def soft_act_ex(K, act, c, h, turn):
            S, B, at, b = K["S"], K["B"], K["at"], h % 2
            act.wait_ge(S["e4"], at(c))
            act.activation(B["e"][b][:, 4], B["e"][b][:, 3], ACT.Exp).then_inc(S["ex"], 1)

        def soft_pe_spread(K, pe, c, h, turn):
            S, B, at, b = K["S"], K["B"], K["at"], h % 2
            pe.wait_ge(S["em"], at(c))
            pe.wait_ge(S["oht"], at(c))
            pe.wait_ge(S["e3"], at(c, 1))
            for j in range(TPC):
                ins = pe.matmul(ps[:, 4, 2 * j:2 * j + 2], B["OHT"][b][:, j, :], B["em"][b][:], start=True, stop=True)
            ins.then_inc(S["spread"], 1)

        def soft_pe_scores(K, pe, c, h, turn):
            S, B, at, b = K["S"], K["B"], K["at"], h % 2
            K["wait_gather"](pe, h, turn)
            pe.wait_ge(S["top"], at(c, 1))
            for j in range(TPC):
                pe.transpose(banks(2)[:, j, :], B["G"][h][:, j, D + 1:D + 2].broadcast_to([P, P]), ident[:])
            pe.wait_ge(S["mrow"], at(c))
            pe.wait_ge(S["top_row"], at(c, 1))
            pe.matmul(ps[:, 5, 2 * P:2 * P + 1], B["mrow"][b][:], small[0:1, 1:2], start=True, stop=True).then_inc(S["old"], 1)

        def soft_pe_rows(K, pe, c, h, turn):
            S, B, at, b = K["S"], K["B"], K["at"], h % 2
            pe.wait_ge(S["ratio"], at(c))
            pe.wait_ge(S["scaled"], at(c, 2))
            pe.matmul(ps[0:TOP + 1, 5, b * P:(b + 1) * P], B["Q"][b][:], ident[:], start=True, stop=True).then_inc(S["rows"], 1)

        def soft_pe_sum(K, pe, c, h, turn):
            pe.wait_ge(K["S"]["msg"], K["at"](c))
            sum_by_node(K, pe, lambda j: K["B"]["msg"][h % 2][:, j, :], D + 1, c, h)

        def soft_dve_old(K, dve, c, h, turn):
            S, B, at, b = K["S"], K["B"], K["at"], h % 2
            first = dve.value_load(base_i[0:1, bass.ds(c, 1)], min_val=0, max_val=N)
            dve.wait_ge(S["top_row"], at(c, 1))
            dve.wait_ge(S["old"], at(c, 2))
            hold(dve)
            dve.tensor_copy(B["mrow"][b][:], acc[TOP:TOP + 1, bass.ds(first, P)]).then_inc(S["mrow"], 1)

        def soft_dve_top(K, dve, c, h, turn):
            S, B, at, b = K["S"], K["B"], K["at"], h % 2
            q, em, t_dst = B["q"][b], B["em"][b], B["win"][b]
            dve.wait_ge(S["old"], at(c))
            dve.wait_ge(S["oht"], at(c))
            hold(dve)
            dve.tensor_tensor_reduce(B["junk"][0][:], two_banks(2), B["pen"][b].rearrange("p j n -> p (j n)"), 1.0, NEG, ALU.add, ALU.max,
                                     q[:, 2:3]).then_inc(S["top"], 1)
            dve.tensor_copy(q[:, 0:1], ps[:, 5, 2 * P:2 * P + 1])
            dve.wait_ge(S["top"], at(c))
            dve.tensor_tensor(q[:, 1:2], ps[:, 5, 2 * P:2 * P + 1], q[:, 2:3], ALU.max).then_inc(S["new"], 1)
            K["wait_loads"](dve, h, turn)
            dve.wait_ge(S["new"], at(c))
            dve.wait_ge(S["rows"], at(c, 2))
            dve.tensor_copy(B["Q"][b][:, TOP:TOP + 1], q[:, 1:2])
            dve.tensor_scalar(q[:, 3:5], q[:, 0:2], t_dst[:, 0:1], None, ALU.add).then_inc(S["u"], 1)
            dve.wait_ge(S["u"], at(c))
            dve.scalar_tensor_tensor(q[:, 5:7], q[:, 3:5], 0.01, q[:, 3:5], ALU.mult, ALU.max).then_inc(S["l"], 1)
            dve.wait_ge(S["l"], at(c))
            dve.wait_ge(S["spread"], at(c, 2))
            dve.tensor_tensor(q[:, 7:8], q[:, 5:6], q[:, 6:7], ALU.subtract)
            dve.tensor_copy(em[:, 0:1], t_dst[:, 0:1])
            dve.tensor_copy(em[:, 1:2], q[:, 6:7]).then_inc(S["em"], 1)

        def soft_dve_score(K, dve, c, h, turn):
            S, B, at, b = K["S"], K["B"], K["at"], h % 2
            e, G = B["e"][b], B["G"][h]
            sp2 = ps[:, 4, 0:2 * TPC].rearrange("p (j k) -> p k j", k=2)
            K["wait_gather"](dve, h, turn)
            dve.wait_ge(S["spread"], at(c))
            dve.tensor_tensor(e[:, 0], G[:, :, D + 1], sp2[:, 0], ALU.add).then_inc(S["e1"], 1)
            dve.wait_ge(S["e1"], at(c))
            dve.scalar_tensor_tensor(e[:, 1], e[:, 0], 0.01, e[:, 0], ALU.mult, ALU.max).then_inc(S["e2"], 1)
            dve.wait_ge(S["e2"], at(c))
            dve.tensor_tensor(e[:, 2], e[:, 1], sp2[:, 1], ALU.subtract).then_inc(S["e3"], 1)
            dve.wait_ge(S["e3"], at(c))
            dve.tensor_scalar(e[:, 3], e[:, 2], 0.0, None, ALU.min).then_inc(S["e4"], 1)

        def soft_dve_msg(K, dve, c, h, turn):
            S, B, at, b = K["S"], K["B"], K["at"], h % 2
            dve.wait_ge(S["ex"], at(c))
            dve.wait_ge(S["sums"], at(c, 2))
            dve.tensor_tensor(B["msg"][b][:], B["G"][h][:, :, 0:D + 1], wide(B["e"][b][:, 4], D + 1), ALU.mult).then_inc(S["msg"], 1)

        def soft_dve_add(K, dve, c, h, turn):
            S, B, at, b = K["S"], K["B"], K["at"], h % 2
            first = dve.value_load(base_i[0:1, bass.ds(c, 1)], min_val=0, max_val=N)
            w = acc[0:D + 1, bass.ds(first, P)]
            dve.wait_ge(S["rows"], at(c))
            dve.wait_ge(S["acc"], at(c, 1))
            dve.tensor_tensor(w, w, ps[0:D + 1, 5, b * P:(b + 1) * P], ALU.mult).then_inc(S["scaled"], 1)
            dve.wait_ge(S["sums"], at(c))
            dve.wait_ge(S["scaled"], at(c))
            dve.tensor_tensor(w, w, ps[0:D + 1, 6 + b, 0:P], ALU.add).then_inc(S["acc"], 1)

        def soft_dve_row(K, dve, c, h, turn):
            S, B, at, b = K["S"], K["B"], K["at"], h % 2
            first = dve.value_load(base_i[0:1, bass.ds(c, 1)], min_val=0, max_val=N)
            dve.wait_ge(S["rows"], at(c))
            hold(dve)
            dve.tensor_copy(acc[TOP:TOP + 1, bass.ds(first, P)], ps[TOP:TOP + 1, 5, b * P:(b + 1) * P]).then_inc(S["top_row"], 1)

        two_banks = lambda b: ps[:, b:b + 2, :].rearrange("p b q -> p (b q)")
        phase("enter", None, {"v": [(0, "xc"), (0, "var"), (1, "own"), (0, "h"), (1, "dst_row")],
                              "a": [(0, "square"), (0, "std"), (1, "src_row"), (0, "hT")],
                              "p": [(1, "own"), (1, "src"), (0, "turned"), (1, "dst")]},
              [(msg_src, "rowsrc", D, "src_row", 1), (msg_dst, "tN", D, "dst_row", 1)])
        work = acc[:, 4 * C * TPC:]
        lo_hi = work[:, 0:2 * C].rearrange("p (k c) -> p k c", k=2)
        hi_bc = work[:, 2 * C:3 * C]
        lim = work[:, 3 * C:3 * C + NT]
        srcf = acc[:, 3 * C * TPC:4 * C * TPC].rearrange("p (c j) -> p c j", j=TPC)
        sp_t = work[:, 3 * C + NT:3 * C + NT + C * TPC].rearrange("p (c j) -> p c j", j=TPC)
        c_v, c_a, c_p = sem("setup_dve"), sem("setup_act"), sem("setup_pe")
        setup_end = 5 * C * TPC + 3 * C + NT
        with nc.Block() as block:
            @block.gpsimd
            def _(pool):
                pool.memset(acc[:, setup_end:NPAD], 0.0).then_inc(s_acc0, 1)

            @block.vector
            def _(dve):
                dve.wait_ge(ld_index, 16 * len(index_loads))
                dve.tensor_copy(dstf[:], dsti).then_inc(c_v, 1)
                dve.tensor_copy(srcf[:], srci[:]).then_inc(c_v, 1)
                dve.wait_ge(c_v, 2)
                dve.tensor_reduce(lo_hi[:, 0, :], dstf[:], AX, ALU.min).then_inc(c_v, 1)
                dve.tensor_reduce(lo_hi[:, 1, :], dstf[:], AX, ALU.max).then_inc(c_v, 1)
                dve.tensor_scalar(ew2, ew2, coef[:, 0:1], coef[:, 1:2], ALU.mult, ALU.add).then_inc(c_v, 1)
                dve.wait_ge(c_v, 5)
                dve.scalar_tensor_tensor(sp_t, ew2, -1.0, ew2, ALU.mult, ALU.min).then_inc(c_v, 1)
                dve.tensor_copy(coef[:, 6:7], coef[:, 5:6]).then_inc(c_v, 1)
                dve.wait_ge(c_v, 7)
                dve.scalar_tensor_tensor(coef[:, 7:8], coef[:, 6:7], -1.0, coef[:, 6:7], ALU.mult, ALU.min).then_inc(c_v, 1)
                dve.tensor_reduce(coef[:, 8:9], coef[:, 2:5], AX, ALU.max).then_inc(c_v, 1)
                dve.wait_ge(c_v, 9)
                dve.tensor_scalar(coef[:, 2:5], coef[:, 2:5], coef[:, 8:9], None, ALU.subtract).then_inc(c_v, 1)
                dve.wait_ge(c_a, 4)
                dve.scalar_tensor_tensor(ew2, ew2, 0.0, sp_t, ALU.max, ALU.add).then_inc(c_v, 1)
                dve.scalar_tensor_tensor(coef[:, 6:7], coef[:, 6:7], 0.0, coef[:, 7:8], ALU.max, ALU.add).then_inc(c_v, 1)
                dve.tensor_reduce(coef[:, 8:9], coef[:, 10:13], AX, ALU.add).then_inc(c_v, 1)
                dve.wait_ge(c_v, 13)
                dve.reciprocal(coef[:, 9:10], coef[:, 8:9]).then_inc(c_v, 1)
                dve.tensor_tensor(ewt[:], ewt[:], ew2, ALU.mult).then_inc(c_v, 1)
                dve.tensor_tensor(sp_t, srcf[:], dstf[:], ALU.not_equal).then_inc(c_v, 1)
                dve.wait_ge(c_v, 16)
                dve.tensor_tensor(ewt[:], ewt[:], sp_t, ALU.mult).then_inc(c_v, 1)
                dve.tensor_scalar(coef[:, 10:13], coef[:, 10:13], coef[:, 9:10], coef[:, 6:7], ALU.mult, ALU.mult).then_inc(c_v, 1)
                dve.wait_ge(c_v, 18)
                dve.memset(ewt[0:DUP, C - 1, :], 0.0).then_inc(c_v, 1)
                dve.memset(dstf[0:DUP, C - 1, :], -4.0 * P).then_inc(c_v, 1)
                dve.wait_ge(c_p, 1)
                for k in range(4):
                    dve.tensor_reduce(small[0:HALF, 2 + k:3 + k], ps[0:HALF, k, 0:P], AX,
                                      (ALU.min, ALU.max)[k // 2]).then_inc(c_v, 1)
                dve.tensor_copy(w_msg2T[:], ps[0:D, 4, 0:D + 1]).then_inc(c_v, 1)
                dve.tensor_copy(w_own[0:D, 0:D], ps[0:D, 5, 0:D]).then_inc(c_v, 1)
                dve.tensor_copy(w_hm[0:D, 0:D], ps[0:D, 6, 0:D]).then_inc(c_v, 1)
                dve.wait_ge(c_p, 2)
                for k in range(4):
                    dst = (base_bc[:], hi_bc)[k // 2]
                    dve.tensor_copy(dst[:, (k % 2) * HALF:(k % 2 + 1) * HALF], ps[:, k, 0:HALF]).then_inc(c_v, 1)
                dve.tensor_copy(w_fold[:, 0:D], ps[0:D + 1, 7, 0:D]).then_inc(c_v, 1)
                dve.wait_ge(c_v, 32)
                dve.tensor_tensor(hi_bc, hi_bc, base_bc[:], ALU.subtract).then_inc(c_v, 1)
                dve.tensor_copy(base0[:], base_bc[:])
                dve.tensor_copy(base_i[:], base_bc[0:1, :]).then_inc(c_v, 1)
                dve.wait_ge(c_v, 34)
                dve.tensor_reduce(small[:, 6:7], hi_bc, AX, ALU.max).then_inc(c_v, 1)
                dve.tensor_scalar(lim, iota_f[:, 0:NT], float(P), None, ALU.mult).then_inc(c_v, 1)
                dve.wait_ge(c_v, 36)
                dve.tensor_scalar(lim, lim, small[:, 6:7], None, ALU.is_le).then_inc(c_v, 1)
                dve.wait_ge(c_v, 37)
                dve.tensor_reduce(small[:, 7:8], lim, AX, ALU.add).then_inc(c_v, 1)
                dve.wait_ge(c_v, 38)
                dve.tensor_copy(rounds_i[:], small[0:1, 7:8]).then_inc(c_v, 1)
                dve.wait_ge(c_v, 39)

            @block.scalar
            def _(act):
                act.wait_ge(c_v, 10)
                act.activation(coef[:, 10:13], coef[:, 2:5], ACT.Exp).then_inc(c_a, 1)
                act.activation(sp_t, sp_t, ACT.Exp).then_inc(c_a, 1)
                act.activation(coef[:, 7:8], coef[:, 7:8], ACT.Exp).then_inc(c_a, 1)
                act.wait_ge(c_a, 3)
                act.activation(sp_t, sp_t, ACT.Ln, bias=small[:, 1:2])
                act.activation(coef[:, 7:8], coef[:, 7:8], ACT.Ln, bias=small[:, 1:2]).then_inc(c_a, 1)

            @block.tensor
            def _(pe):
                pe.wait_ge(c_v, 4)
                for k in range(4):
                    pe.transpose(ps[0:HALF, k, 0:P], lo_hi[:, k // 2, (k % 2) * HALF:(k % 2 + 1) * HALF], ident[:])
                pe.transpose(ps[0:D, 4, 0:D + 1], w_msg2[:], ident[0:D + 1, 0:D + 1])
                pe.transpose(ps[0:D, 5, 0:D], w_lin[:, 0:D], ident[0:D, 0:D])
                pe.transpose(ps[0:D, 6, 0:D], w_lin[:, D:2 * D], ident[0:D, 0:D]).then_inc(c_p, 1)
                pe.wait_ge(c_v, 27)
                for k in range(4):
                    pe.matmul(ps[:, k, 0:HALF], bc(small[0:HALF, 2 + k:3 + k], [HALF, P]), ident[0:HALF, 0:HALF],
                              start=True, stop=True)
                pe.matmul(ps[0:D + 1, 7, 0:D], w_msg2T[:], w_upd1[:], start=True, stop=True).then_inc(c_p, 1)

        zero_sums()
        edge_pass("msg", "drel oh idx oh_turned oht edge_turned edgeT pre summed msg sums acc", msg_src, D,
                  [("edgeT", [D, TPC, P], F32, 2), ("msg", [P, TPC, D + 1], F32, 2)],
                  {"dve": [(0, one_hot), (2, msg_dve), (3, msg_dve_add)], "act": [(0, copy_indices), (1, msg_act_prep), (2, msg_act)],
                   "pe": [(1, msg_pe_prep), (2, msg_pe), (3, msg_pe_sum)]},
                  rows_user="summed", win_table=msg_dst, wcols=D, edges=True)
        phase("after_msg", "msg", {"v": [(2, "xc"), (1, "z"), (2, "var"), (2, "h"), (3, "wh"), (1, "x_msg"), (3, "norm2")],
                                   "a": [(2, "square"), (2, "std"), (0, "sums"), (2, "hT"), (1, "zT"), (3, "wh_square"), (3, "norm")],
                                   "p": [(1, "mean"), (2, "turned"), (1, "z_turned"), (3, "own"), (1, "upd")]},
              [(att, "rN", D + 1, "row", 3)])
        edge_pass("att", "drel oh idx oh_turned oht srcs src_turned sm before away count shift sidx wc dot a1 a2 sim a3 a4 weight v merged out",
                  att, D + 1,
                  [("V", [P, TPC, D], F32, 2), ("out", [P, TPC, D], F32, U), ("sidx", [P, TPC], I32, U), ("srcs", [P, TPC], F32, 2),
                   ("t", [P, 3, TPC], F32, 2), ("m", [P, 9, TPC], F32, 2)],
                  {"dve": [(0, one_hot), (2, att_dve), (1, att_dve_prep)], "act": [(0, copy_indices), (1, att_act_prep), (3, att_act)],
                   "pe": [(1, att_pe_prep), (2, att_pe), (3, att_pe_merge)]},
                  rows_user="dot", oh_user="oh_turned", win_user="wc", last_stage="v", win_table=att, wcols=D + 1, pool=att_pool,
                  views={"SM": [acc[:, k * CE:(k + 1) * CE].rearrange("p (j n) -> p j n", n=P) for k in range(2)],
                         "before": [acc[:, 2 * CE:3 * CE].rearrange("p (j n) -> p j n", n=P)],
                         "prod": [acc[:, 3 * CE:3 * CE + TPC * D].rearrange("p (j d) -> p j d", d=D)]})
        phase("after_att", "prop", {"v": [(0, "x_prop"), (1, "xc"), (1, "var"), (2, "own"), (1, "h")],
                                    "a": [(1, "square"), (1, "std"), (1, "hT")],
                                    "p": [(2, "own"), (1, "turned")]},
              [(sage1, "hN", D, "h", 1)])
        sage = {"dve": [(0, one_hot), (1, sage_dve)], "act": [(0, sage_act)], "pe": [(0, sage_pe)]}
        edge_pass("sage1", "drel oh idx sums acc", sage1, D, [], sage, rows_user="sums")
        phase("after_sage1", "sage1", {"v": [(1, "mean"), (2, "own")], "a": [(0, "sums"), (1, "hT")],
                                       "p": [(1, "mean"), (2, "own"), (1, "turned")]},
              [(sage2, "hN", D, "h", 1)])
        edge_pass("sage2", "drel oh idx sums acc", sage2, D, [], sage, rows_user="sums")
        phase("after_sage2", "sage2", {"v": [(1, "mean"), (2, "xc"), (2, "var"), (3, "scores"), (2, "h")],
                                       "a": [(0, "sums"), (2, "square"), (2, "std"), (2, "hT")],
                                       "p": [(1, "mean"), (3, "own"), (2, "turned")]},
              [(soft, "hN", D + 2, "row", 3), (soft_dst, "tS", 1, "row", 3)])
        edge_pass("soft", "drel oh idx oh_turned oht mrow old top new u l em ratio spread rows e1 e2 e3 e4 ex msg scaled top_row sums acc",
                  soft, D + 2,
                  [("msg", [P, TPC, D + 1], F32, 2), ("q", [P, 8], F32, 2), ("e", [P, 5, TPC], F32, 2), ("em", [P, 2], F32, 2),
                   ("mrow", [1, P], F32, 2), ("Q", [P, TOP + 1], F32, 2), ("pen", [P, TPC, P], F32, 2), ("junk", [P, CE], F32, 1)],
                  {"dve": [(1, soft_dve_old), (0, one_hot), (2, soft_dve_score), (1, soft_dve_top), (2, soft_dve_msg),
                           (3, soft_dve_add), (1, soft_dve_row)],
                   "act": [(0, copy_indices), (2, soft_act_ex), (0, soft_act_prep), (1, soft_act_ratio)],
                   "pe": [(2, soft_pe_spread), (1, soft_pe_scores), (0, turn_one_hot), (3, soft_pe_sum), (1, soft_pe_rows)]},
                  rows_user="msg", win_user="em", win_table=soft_dst, wcols=1)
        phase("leave", "soft", {"v": [(1, "soft")], "a": [(0, "sums")], "p": [(1, "mean")]}, [])

        s_out = sem("out")
        with nc.Block() as block:
            @block.sync
            def _(sp):
                sp.dma_start(out[0:FULL * P].rearrange("(t p) d -> p t d", p=P), X[:, 0:FULL, :]).then_inc(s_out, 16)
                sp.dma_start(out[FULL * P:N], X[0:TAIL, FULL, :]).then_inc(s_out, 16)
                sp.wait_ge(s_out, 32)


def kernel(**inputs):
    import numpy as _np
    import concourse.bacc as _bacc
    from concourse import mybir as _mybir
    from concourse.bass_utils import run_bass_kernel_spmd as _run

    nc = _bacc.Bacc("TRN2", target_bir_lowering=False, num_devices=1)
    arrays, aps = {}, {}
    for name, v in inputs.items():
        v = _np.ascontiguousarray(v)
        arrays[name] = v
        aps[name] = nc.dram_tensor(name, v.shape, _mybir.dt.from_np(v.dtype), kind="ExternalInput").ap()
    out = nc.dram_tensor("result", inputs["x"].shape, F32, kind="ExternalOutput").ap()
    gnn_kernel(nc, aps, out)
    r = _run(nc, [arrays], core_ids=[0])
    return r.results[0]["result"]
```
